# Optimizing a Trainium2 kernel written in Bass

```python
import numpy as np
import jax
import jax.numpy as jnp

def _softmax(x, axis=-1):
    return jax.nn.softmax(x, axis=axis)

def _gelu(x):
    return jax.nn.gelu(x, approximate=True)

def _silu(x):
    return jax.nn.silu(x)

def _sigmoid(x):
    return jax.nn.sigmoid(x)

def _layernorm(x, axis=-1, eps=1e-05):
    m = jnp.mean(x, axis=axis, keepdims=True)
    v = jnp.var(x, axis=axis, keepdims=True)
    return (x - m) / jnp.sqrt(v + eps)

def _scatter_add(tgt, idx, src, axis=0):
    return tgt.at[idx].add(src)

def _segment_sum(src, seg, n):
    return jax.ops.segment_sum(src, seg, n)
kernel_name = 'mk_seq_preln_d2_jaxref_r8_1d0784'

def setup_inputs(seed: int=0):
    np.random.seed(seed)
    _w = jnp.asarray

    def _L0_attn_setup():
        import jax, jax.numpy as jnp
        import numpy as np
        import math
        B, T, D, H = (4, 128, 128, 16)
        DK = D // H
        EPS = 1e-12
        key = jax.random.key(seed)
        ks = jax.random.split(key, 6)
        xav = math.sqrt(6.0 / (D + D))
        x = jax.random.normal(ks[0], (B, T, D), dtype=jnp.float32)
        Wq = jax.random.uniform(ks[1], (D, D), jnp.float32, -xav, xav)
        Wk = jax.random.uniform(ks[2], (D, D), jnp.float32, -xav, xav)
        Wv = jax.random.uniform(ks[3], (D, D), jnp.float32, -xav, xav)
        Wo = jax.random.uniform(ks[4], (D, D), jnp.float32, -xav, xav)
        logit_g = math.log(0.9 / 0.1)
        logit_l = math.log(0.1 / 0.9)
        W_gamma = jnp.zeros((H,), jnp.float32)
        b_gamma = jnp.full((H,), logit_g, jnp.float32)
        W_lambda = jnp.zeros((H,), jnp.float32)
        b_lambda = jnp.full((H,), logit_l, jnp.float32)
        return {'x': x, 'Wq': Wq, 'Wk': Wk, 'Wv': Wv, 'Wo': Wo, 'W_gamma': W_gamma, 'b_gamma': b_gamma, 'W_lambda': W_lambda, 'b_lambda': b_lambda}
    _L0_attn_in = _L0_attn_setup()

    def _L0_ffn_setup():
        import jax, jax.numpy as jnp
        import numpy as np
        B, S, D = (1, 256, 128)
        E, F = (16, 128)
        NG, TKG, K = (4, 2, 4)
        NSH = 2
        SCALE = 2.5
        STD = 0.02
        EPG = E // NG

        def _route(x_flat, router_w, bias):
            logits = x_flat.astype(jnp.float32) @ router_w.T
            scores = jax.nn.sigmoid(logits)
            s = scores + bias[None, :]
            sg = s.reshape(-1, NG, EPG)
            group_score = jax.lax.top_k(sg, 2)[0].sum(-1)
            gidx = jax.lax.top_k(group_score, TKG)[1]
            gmask = jnp.sum(jax.nn.one_hot(gidx, NG, dtype=jnp.float32), axis=1) > 0
            emask = jnp.repeat(gmask, EPG, axis=1)
            masked = jnp.where(emask, s, -1.0)
            topk_idx = jax.lax.top_k(masked, K)[1]
            tw = jnp.take_along_axis(scores, topk_idx, axis=1)
            tw = tw / (tw.sum(-1, keepdims=True) + 1e-20)
            tw = tw * SCALE
            return (topk_idx, tw)
        key = jax.random.key(seed)
        ks = jax.random.split(key, 8)
        return {'hidden_states': jax.random.normal(ks[0], (B, S, D), jnp.float32), 'router_w': jax.random.normal(ks[1], (E, D), jnp.float32) * STD, 'bias': jnp.zeros((E,), jnp.float32), 'gate_w': jax.random.normal(ks[2], (E, D, F), jnp.float32) * STD, 'up_w': jax.random.normal(ks[3], (E, D, F), jnp.float32) * STD, 'down_w': jax.random.normal(ks[4], (E, F, D), jnp.float32) * STD, 'sh_gate_w': jax.random.normal(ks[5], (D, NSH * F), jnp.float32) * STD, 'sh_up_w': jax.random.normal(ks[6], (D, NSH * F), jnp.float32) * STD, 'sh_down_w': jax.random.normal(ks[7], (NSH * F, D), jnp.float32) * STD}
    _L0_ffn_in = _L0_ffn_setup()

    def _L1_attn_setup():
        import jax, jax.numpy as jnp
        import numpy as np
        BATCH, SEQ, D_IN, D_H = (16, 256, 128, 128)
        LN_EPS = 1e-05
        key = jax.random.key(seed)
        ks = jax.random.split(key, 4)
        x = jax.random.normal(ks[0], (BATCH, SEQ, D_IN), dtype=jnp.float32)
        a = jax.random.normal(ks[1], (D_H, D_H), dtype=jnp.float32)
        q, _ = jnp.linalg.qr(a)
        A = q.astype(jnp.float32)
        limB = float(np.sqrt(6.0 / (D_H + D_IN)))
        B = jax.random.uniform(ks[2], (D_H, D_IN), minval=-limB, maxval=limB, dtype=jnp.float32)
        limC = float(np.sqrt(6.0 / (D_H + D_H)))
        C = jax.random.uniform(ks[3], (D_H, D_H), minval=-limC, maxval=limC, dtype=jnp.float32)
        gamma = jnp.ones((D_H,), dtype=jnp.float32)
        beta = jnp.zeros((D_H,), dtype=jnp.float32)
        return {'x': x, 'A': A, 'B': B, 'C': C, 'gamma': gamma, 'beta': beta}
    _L1_attn_in = _L1_attn_setup()

    def _L1_ffn_setup():
        import jax, jax.numpy as jnp
        import numpy as np
        import math
        D = 128
        H = 16
        E = 8
        TOPK = 2
        LAT = D // 2
        KPH = LAT // H
        HD = D // H

        def _forward(hs, q_w, q_b, k_w, k_b, v_w, v_b, o_w, o_b, router_w, router_b, w1, b1, w2, b2):
            B, S, _ = hs.shape
            Q = (hs @ q_w + q_b).reshape(B, S, H, HD).transpose(0, 2, 1, 3)
            K = (hs @ k_w + k_b).reshape(B, S, H, KPH).transpose(0, 2, 1, 3)
            V = (hs @ v_w + v_b).reshape(B, S, H, KPH).transpose(0, 2, 1, 3)
            scores = jnp.einsum('bhsk,bhtk->bhst', Q[..., :KPH], K) / math.sqrt(KPH)
            attn = jax.nn.softmax(scores, axis=-1)
            ao = jnp.einsum('bhst,bhtv->bhsv', attn, V)
            ao = ao.transpose(0, 2, 1, 3).reshape(B, S, H * KPH)
            ao = jnp.concatenate([ao, jnp.zeros((B, S, D - LAT), ao.dtype)], axis=-1)
            mla_out = ao @ o_w + o_b
            probs = jax.nn.softmax(mla_out @ router_w + router_b, axis=-1)
            topw, topi = jax.lax.top_k(probs, TOPK)
            topw = topw / (topw.sum(-1, keepdims=True) + 1e-08)
            combine = jnp.sum(jax.nn.one_hot(topi, E, dtype=probs.dtype) * topw[..., None], axis=-2)
            h1 = jnp.einsum('bsd,edf->ebsf', mla_out, w1) + b1[:, None, None, :]
            h1 = jax.nn.gelu(h1, approximate=False)
            h2 = jnp.einsum('ebsf,efd->ebsd', h1, w2) + b2[:, None, None, :]
            moe_out = jnp.einsum('bse,ebsd->bsd', combine, h2)
            return hs + 0.3 * moe_out
        key = jax.random.key(seed)
        ks = jax.random.split(key, 16)
        s = 0.02
        inp = {'hidden_states': jax.random.normal(ks[0], (2, 256, D), jnp.float32), 'q_w': jax.random.normal(ks[1], (D, D), jnp.float32) * s, 'q_b': jnp.zeros((D,), jnp.float32), 'k_w': jax.random.normal(ks[2], (D, LAT), jnp.float32) * s, 'k_b': jnp.zeros((LAT,), jnp.float32), 'v_w': jax.random.normal(ks[3], (D, LAT), jnp.float32) * s, 'v_b': jnp.zeros((LAT,), jnp.float32), 'o_w': jax.random.normal(ks[4], (D, D), jnp.float32) * s, 'o_b': jnp.zeros((D,), jnp.float32), 'router_w': jax.random.normal(ks[5], (D, E), jnp.float32) * s, 'router_b': jnp.zeros((E,), jnp.float32), 'w1': jax.random.normal(ks[6], (E, D, 2 * D), jnp.float32) * s, 'b1': jnp.zeros((E, 2 * D), jnp.float32), 'w2': jax.random.normal(ks[7], (E, 2 * D, D), jnp.float32) * s, 'b2': jnp.zeros((E, D), jnp.float32)}
        return inp
    _L1_ffn_in = _L1_ffn_setup()
    _d = {'L0_attn_x': _L0_attn_in['x'], 'L0_attn_Wq': _L0_attn_in['Wq'], 'L0_attn_Wk': _L0_attn_in['Wk'], 'L0_attn_Wv': _L0_attn_in['Wv'], 'L0_attn_Wo': _L0_attn_in['Wo'], 'L0_attn_W_gamma': _L0_attn_in['W_gamma'], 'L0_attn_b_gamma': _L0_attn_in['b_gamma'], 'L0_attn_W_lambda': _L0_attn_in['W_lambda'], 'L0_attn_b_lambda': _L0_attn_in['b_lambda'], 'L0_ffn_router_w': _L0_ffn_in['router_w'], 'L0_ffn_bias': _L0_ffn_in['bias'], 'L0_ffn_gate_w': _L0_ffn_in['gate_w'], 'L0_ffn_up_w': _L0_ffn_in['up_w'], 'L0_ffn_down_w': _L0_ffn_in['down_w'], 'L0_ffn_sh_gate_w': _L0_ffn_in['sh_gate_w'], 'L0_ffn_sh_up_w': _L0_ffn_in['sh_up_w'], 'L0_ffn_sh_down_w': _L0_ffn_in['sh_down_w'], 'L1_attn_A': _L1_attn_in['A'], 'L1_attn_B': _L1_attn_in['B'], 'L1_attn_C': _L1_attn_in['C'], 'L1_attn_gamma': _L1_attn_in['gamma'], 'L1_attn_beta': _L1_attn_in['beta'], 'L1_ffn_q_w': _L1_ffn_in['q_w'], 'L1_ffn_q_b': _L1_ffn_in['q_b'], 'L1_ffn_k_w': _L1_ffn_in['k_w'], 'L1_ffn_k_b': _L1_ffn_in['k_b'], 'L1_ffn_v_w': _L1_ffn_in['v_w'], 'L1_ffn_v_b': _L1_ffn_in['v_b'], 'L1_ffn_o_w': _L1_ffn_in['o_w'], 'L1_ffn_o_b': _L1_ffn_in['o_b'], 'L1_ffn_router_w': _L1_ffn_in['router_w'], 'L1_ffn_router_b': _L1_ffn_in['router_b'], 'L1_ffn_w1': _L1_ffn_in['w1'], 'L1_ffn_b1': _L1_ffn_in['b1'], 'L1_ffn_w2': _L1_ffn_in['w2'], 'L1_ffn_b2': _L1_ffn_in['b2']}
    _x0 = _d['L0_attn_x']
    _d['L0_attn_x'] = jax.random.normal(jax.random.fold_in(jax.random.key(seed), 1), (2, 1024, 128), dtype=_x0.dtype)
    del _x0
    return _d

def reference(L0_attn_x, L0_attn_Wq, L0_attn_Wk, L0_attn_Wv, L0_attn_Wo, L0_attn_W_gamma, L0_attn_b_gamma, L0_attn_W_lambda, L0_attn_b_lambda, L0_ffn_router_w, L0_ffn_bias, L0_ffn_gate_w, L0_ffn_up_w, L0_ffn_down_w, L0_ffn_sh_gate_w, L0_ffn_sh_up_w, L0_ffn_sh_down_w, L1_attn_A, L1_attn_B, L1_attn_C, L1_attn_gamma, L1_attn_beta, L1_ffn_q_w, L1_ffn_q_b, L1_ffn_k_w, L1_ffn_k_b, L1_ffn_v_w, L1_ffn_v_b, L1_ffn_o_w, L1_ffn_o_b, L1_ffn_router_w, L1_ffn_router_b, L1_ffn_w1, L1_ffn_b1, L1_ffn_w2, L1_ffn_b2):

    def _L0_attn_ref(x, Wq, Wk, Wv, Wo, W_gamma, b_gamma, W_lambda, b_lambda):
        import jax, jax.numpy as jnp
        import numpy as np
        import math
        B, T, D, H = (4, 128, 128, 16)
        DK = D // H
        EPS = 1e-12
        b, t, d = x.shape

        def proj(W):
            return jnp.einsum('btd,ed->bte', x, W).reshape(b, t, H, DK).transpose(1, 0, 2, 3)
        q = proj(Wq)
        k = proj(Wk)
        v = proj(Wv)
        k = k / jnp.maximum(jnp.linalg.norm(k, axis=-1, keepdims=True), EPS)
        k_bar = k.mean(axis=-1)
        gamma = jax.nn.sigmoid(W_gamma * k_bar + b_gamma)
        lam = jax.nn.sigmoid(W_lambda * k_bar + b_lambda)
        rho = (1.0 - lam) * gamma
        S0 = jnp.zeros((b, H, DK, DK), x.dtype)

        def step(S, inp):
            q_t, k_t, v_t, rho_t = inp
            r = rho_t[..., None, None]
            S = r * S + (1.0 - r) * jnp.einsum('bhv,bhk->bhvk', v_t, k_t)
            y_t = jnp.einsum('bhv,bhvk->bhk', q_t, S)
            return (S, y_t)
        _, ys = jax.lax.scan(step, S0, (q, k, v, rho))
        out = ys.transpose(1, 0, 2, 3).reshape(b, t, d)
        return jnp.einsum('btd,ed->bte', out, Wo)

    def _L0_ffn_ref(hidden_states, router_w, bias, gate_w, up_w, down_w, sh_gate_w, sh_up_w, sh_down_w):
        import jax, jax.numpy as jnp
        import numpy as np
        B, S, D = (1, 256, 128)
        E, F = (16, 128)
        NG, TKG, K = (4, 2, 4)
        NSH = 2
        SCALE = 2.5
        STD = 0.02
        EPG = E // NG

        def _route(x_flat, router_w, bias):
            logits = x_flat.astype(jnp.float32) @ router_w.T
            scores = jax.nn.sigmoid(logits)
            s = scores + bias[None, :]
            sg = s.reshape(-1, NG, EPG)
            group_score = jax.lax.top_k(sg, 2)[0].sum(-1)
            gidx = jax.lax.top_k(group_score, TKG)[1]
            gmask = jnp.sum(jax.nn.one_hot(gidx, NG, dtype=jnp.float32), axis=1) > 0
            emask = jnp.repeat(gmask, EPG, axis=1)
            masked = jnp.where(emask, s, -1.0)
            topk_idx = jax.lax.top_k(masked, K)[1]
            tw = jnp.take_along_axis(scores, topk_idx, axis=1)
            tw = tw / (tw.sum(-1, keepdims=True) + 1e-20)
            tw = tw * SCALE
            return (topk_idx, tw)
        x = hidden_states.reshape(-1, D)
        topk_idx, tw = _route(x, router_w, bias)
        combine = (jax.nn.one_hot(topk_idx, E, dtype=tw.dtype) * tw[..., None]).sum(1)
        h = jnp.einsum('td,edf->etf', x, gate_w)
        u = jnp.einsum('td,edf->etf', x, up_w)
        y = jnp.einsum('etf,efd->etd', jax.nn.silu(h) * u, down_w)
        routed = jnp.einsum('etd,te->td', y, combine)
        sh = jax.nn.silu(x @ sh_gate_w) * (x @ sh_up_w) @ sh_down_w
        return (routed + sh).reshape(hidden_states.shape)

    def _L1_attn_ref(x, A, B, C, gamma, beta):
        import jax, jax.numpy as jnp
        import numpy as np
        BATCH, SEQ, D_IN, D_H = (16, 256, 128, 128)
        LN_EPS = 1e-05
        Bu = jnp.einsum('bti,hi->bth', x, B)

        def step(h, bu_t):
            h_new = jax.nn.gelu(h @ A.T + bu_t, approximate=False)
            y_t = h_new @ C.T
            return (h_new, y_t)
        h0 = jnp.zeros((x.shape[0], A.shape[0]), dtype=x.dtype)
        _, ys = jax.lax.scan(step, h0, jnp.swapaxes(Bu, 0, 1))
        out = jnp.swapaxes(ys, 0, 1)
        mean = jnp.mean(out, axis=-1, keepdims=True)
        var = jnp.var(out, axis=-1, keepdims=True)
        return (out - mean) * jax.lax.rsqrt(var + LN_EPS) * gamma + beta

    def _L1_ffn_ref(hidden_states, q_w, q_b, k_w, k_b, v_w, v_b, o_w, o_b, router_w, router_b, w1, b1, w2, b2):
        import jax, jax.numpy as jnp
        import numpy as np
        import math
        D = 128
        H = 16
        E = 8
        TOPK = 2
        LAT = D // 2
        KPH = LAT // H
        HD = D // H

        def _forward(hs, q_w, q_b, k_w, k_b, v_w, v_b, o_w, o_b, router_w, router_b, w1, b1, w2, b2):
            B, S, _ = hs.shape
            Q = (hs @ q_w + q_b).reshape(B, S, H, HD).transpose(0, 2, 1, 3)
            K = (hs @ k_w + k_b).reshape(B, S, H, KPH).transpose(0, 2, 1, 3)
            V = (hs @ v_w + v_b).reshape(B, S, H, KPH).transpose(0, 2, 1, 3)
            scores = jnp.einsum('bhsk,bhtk->bhst', Q[..., :KPH], K) / math.sqrt(KPH)
            attn = jax.nn.softmax(scores, axis=-1)
            ao = jnp.einsum('bhst,bhtv->bhsv', attn, V)
            ao = ao.transpose(0, 2, 1, 3).reshape(B, S, H * KPH)
            ao = jnp.concatenate([ao, jnp.zeros((B, S, D - LAT), ao.dtype)], axis=-1)
            mla_out = ao @ o_w + o_b
            probs = jax.nn.softmax(mla_out @ router_w + router_b, axis=-1)
            topw, topi = jax.lax.top_k(probs, TOPK)
            topw = topw / (topw.sum(-1, keepdims=True) + 1e-08)
            combine = jnp.sum(jax.nn.one_hot(topi, E, dtype=probs.dtype) * topw[..., None], axis=-2)
            h1 = jnp.einsum('bsd,edf->ebsf', mla_out, w1) + b1[:, None, None, :]
            h1 = jax.nn.gelu(h1, approximate=False)
            h2 = jnp.einsum('ebsf,efd->ebsd', h1, w2) + b2[:, None, None, :]
            moe_out = jnp.einsum('bse,ebsd->bsd', combine, h2)
            return hs + 0.3 * moe_out
        return _forward(hidden_states, q_w, q_b, k_w, k_b, v_w, v_b, o_w, o_b, router_w, router_b, w1, b1, w2, b2)
    x = L0_attn_x
    x = x + _L0_attn_ref(_layernorm(x, axis=-1), L0_attn_Wq, L0_attn_Wk, L0_attn_Wv, L0_attn_Wo, L0_attn_W_gamma, L0_attn_b_gamma, L0_attn_W_lambda, L0_attn_b_lambda)
    x = x + _L0_ffn_ref(_layernorm(x, axis=-1), L0_ffn_router_w, L0_ffn_bias, L0_ffn_gate_w, L0_ffn_up_w, L0_ffn_down_w, L0_ffn_sh_gate_w, L0_ffn_sh_up_w, L0_ffn_sh_down_w)
    x = x + _L1_attn_ref(_layernorm(x, axis=-1), L1_attn_A, L1_attn_B, L1_attn_C, L1_attn_gamma, L1_attn_beta)
    x = x + _L1_ffn_ref(_layernorm(x, axis=-1), L1_ffn_q_w, L1_ffn_q_b, L1_ffn_k_w, L1_ffn_k_b, L1_ffn_v_w, L1_ffn_v_b, L1_ffn_o_w, L1_ffn_o_b, L1_ffn_router_w, L1_ffn_router_b, L1_ffn_w1, L1_ffn_b1, L1_ffn_w2, L1_ffn_b2)
    return x

_drawn_inputs = setup_inputs


def setup_inputs(seed=0):
    import zlib

    import numpy as np

    out = dict(_drawn_inputs(seed))
    spreads = {'L0_attn_W_gamma': (0.0, 0.8),
     'L0_attn_b_gamma': (2.1972246170043945, 0.2),
     'L0_attn_W_lambda': (0.0, 0.8),
     'L0_attn_b_lambda': (-2.1972246170043945, 0.2),
     'L0_ffn_bias': (0.0, 0.8),
     'L1_attn_gamma': (1.0, 0.2),
     'L1_attn_beta': (0.0, 0.401),
     'L1_ffn_q_b': (0.0, 0.8),
     'L1_ffn_k_b': (0.0, 2.0),
     'L1_ffn_v_b': (0.0, 0.8),
     'L1_ffn_o_b': (0.0, 0.8),
     'L1_ffn_router_b': (0.0, 0.8),
     'L1_ffn_b1': (0.0, 0.8),
     'L1_ffn_b2': (0.0, 0.8)}
    factors = {'L0_ffn_router_w': 8.0,
     'L0_ffn_gate_w': 7.726,
     'L0_ffn_up_w': 7.68,
     'L0_ffn_down_w': 7.717,
     'L0_ffn_sh_gate_w': 6.864,
     'L0_ffn_sh_up_w': 6.762,
     'L0_ffn_sh_down_w': 6.825,
     'L1_ffn_q_w': 8.0,
     'L1_ffn_k_w': 8.0,
     'L1_ffn_v_w': 8.0,
     'L1_ffn_o_w': 8.0,
     'L1_ffn_router_w': 8.0,
     'L1_ffn_w1': 8.0,
     'L1_ffn_w2': 8.0}
    for name, (base, spread) in spreads.items():
        noise = np.random.default_rng([zlib.crc32(name.encode()), seed]).standard_normal(out[name].shape)
        drawn = base * np.exp(spread * noise) if base else spread * noise
        out[name] = jnp.asarray(drawn.astype(out[name].dtype))
    for name, factor in factors.items():
        out[name] = (out[name] * factor).astype(out[name].dtype)
    return out
```

```python
from contextlib import ExitStack

import concourse.bass as bass
from concourse import mybir

F32 = mybir.dt.float32
I32 = mybir.dt.int32
F16 = mybir.dt.float16
BF16 = mybir.dt.bfloat16
ALU = mybir.AluOpType
ACT = mybir.ActivationFunctionType
AX = mybir.AxisListType.X

B, T, D = 2, 1024, 128
P = 128
NT = B * T // P
TB = T // P
CH = 512
NC = B * T // CH
H1, DK = 16, 8
E0, NG, TKG, K0, NSH = 16, 4, 2, 4, 2
W0 = E0 + NSH
H3, KPH = 16, 4
LAT = H3 * KPH
E1, TOPK = 8, 2
HG = 4
NHG = H3 // HG
LN_EPS = 1e-5
ZSCALE = 64.0
RSQRT_SEED = float(0x5F3759DF)


class Chain:

    def __init__(self, eng, sem, base=0):
        self.eng, self.sem, self.base, self.n = eng, sem, base, 0

    def __call__(self, ins):
        self.n += 1
        ins.then_inc(self.sem, 1)
        self.eng.wait_ge(self.sem, self.base + self.n)
        return ins


def rsqrt(nc, link, y, x, t):
    link(nc.vector.tensor_scalar(y.bitcast(I32), x.bitcast(I32), 1, None, ALU.logical_shift_right))
    link(nc.vector.tensor_scalar(y.bitcast(I32), y.bitcast(I32), -1.0, RSQRT_SEED, ALU.mult, ALU.add))
    for _ in range(3):
        link(nc.vector.tensor_tensor(t, y, y, ALU.mult))
        link(nc.vector.scalar_tensor_tensor(out=t, in0=x, scalar=-0.5, in1=t, op0=ALU.mult, op1=ALU.mult))
        link(nc.vector.scalar_tensor_tensor(out=y, in0=t, scalar=1.5, in1=y, op0=ALU.add, op1=ALU.mult))


def ln_moments(nc, link, stats, small):
    mean, rstd, dif, cv = (small[:, k, :] for k in range(4))
    nc.vector.tensor_tensor(dif, stats[:, :, 1], stats[:, :, 4], ALU.subtract)
    nc.vector.tensor_tensor(mean, stats[:, :, 1], stats[:, :, 4], ALU.add)
    link(nc.vector.tensor_tensor(cv, stats[:, :, 2], stats[:, :, 5], ALU.add))
    nc.vector.tensor_scalar(mean, mean, 0.5, None, ALU.mult)
    nc.vector.tensor_scalar(cv, cv, 1.0 / D, LN_EPS, ALU.mult, ALU.add)
    link(nc.vector.tensor_tensor(dif, dif, dif, ALU.mult))
    link(nc.vector.scalar_tensor_tensor(out=cv, in0=dif, scalar=0.25, in1=cv, op0=ALU.mult, op1=ALU.add))
    rsqrt(nc, link, rstd, cv, dif)


def layer_norm(nc, link, dst, src, stats, small, done, n=NT):
    for i in range(n):
        ins = nc.vector.bn_stats(stats[:, i, :], src[:, i, :])
    link(ins)
    ln_moments(nc, link, stats, small)
    for i in range(n):
        nc.vector.tensor_scalar(dst[:, i, :], src[:, i, :], small[:, 0, i:i + 1], small[:, 1, i:i + 1],
                                ALU.subtract, ALU.mult).then_inc(done, 1)


def build(nc, a, out, stage):
    ctx = ExitStack()
    with ctx:
        def sb(name, shape, dt=F32):
            return ctx.enter_context(nc.sbuf_tensor(name, shape, dt))

        def sem(name):
            return ctx.enter_context(nc.semaphore(name))

        banks = ctx.enter_context(nc.psum_tensor("banks", [P, 8, 512], F32))
        ps = [banks[:, i, :] for i in range(8)]
        m = {
            "x": sb("x", [P, NT, D]), "xn": sb("xn", [P, NT, D]), "xT": sb("xT", [P, B * T]),
            "stats": sb("stats", [P, NT, 6]), "small": sb("small", [P, 4, NT]),
            "ident": sb("ident", [P, P]), "banks": banks,
        }
        g = {"ld_x": [sem(f"ld_x{i}") for i in range(NC)], "ld_id": sem("ld_id")}
        with ExitStack() as own:
            gated_recurrence(nc, own, a, m, g, ps)
        if stage >= 2:
            with ExitStack() as own:
                grouped_experts(nc, own, a, m, g, ps)
        if stage >= 3:
            with ExitStack() as own:
                gelu_recurrence(nc, own, a, m, g, ps)
        if stage >= 4:
            with ExitStack() as own:
                attention_experts(nc, own, a, m, g, ps)
        stored = sem("stored")
        with nc.Block() as block:
            @block.sync
            def _(sp):
                o = out.rearrange("b (i p) d -> p (b i) d", p=P)
                for c in range(NC):
                    sp.dma_start(o[:, 4 * c:4 * c + 4, :], m["x"][:, 4 * c:4 * c + 4, :]).then_inc(stored, 16)
                sp.wait_ge(stored, 16 * NC)


def scoped(nc, own):
    def sb(name, shape, dt=F32):
        return own.enter_context(nc.sbuf_tensor(name, shape, dt))

    def sem(name):
        return own.enter_context(nc.semaphore(name))

    return sb, sem


def gated_recurrence(nc, own, a, m, g, ps):
    sb, sem = scoped(nc, own)
    x, xn, xT, stats, small, ident = (m[k] for k in ("x", "xn", "xT", "stats", "small", "ident"))
    wT = sb("wT", [P, 3, D])
    wk_rep = sb("wk_rep", [P, DK, P])
    wo_rep = sb("wo_rep", [P, DK, D])
    par = sb("par", [P, 4, H1])
    qT = sb("qT", [P, B * T])
    vT = sb("vT", [P, B * T])
    rhoE = sb("rhoE", [P, B * T])
    uT = sb("uT", [P, B * T])
    ksq = sb("ksq", [P, NT, D])
    s1 = sb("s1", [P, NT, H1])
    s2 = sb("s2", [P, NT, H1])
    gat = sb("gat", [P, 4, NT, H1])
    rho_x, g_x = ksq, xn
    w = sb("w", [P, 2, T])
    S = sb("S", [P, 2, T])
    qS = sb("qS", [P, 2, T])
    ld_w, ld_p, ld_o = sem("a_ld_w"), sem("a_ld_p"), sem("a_ld_o")
    dve, xn_done, xT_ps, xT_done = sem("a_dve"), sem("a_xn"), sem("a_xT_ps"), sem("a_xT")
    rep, proj, proj_out, kt_ps, ksq_done, s_done = (sem("a_" + n) for n in
                                                     ("rep", "proj", "proj_out", "kt", "ksq", "s"))
    z_done, th_done, gate_done, exp_ps, rho_out, u_done = (sem("a_" + n) for n in
                                                          ("z", "th", "gate", "exp", "rho", "u"))
    rho_spread, g_spread = sem("a_rho_spread"), sem("a_g_spread")
    k_ps, w_done, S_done, qS_done, o_ps = (sem("a_" + n) for n in ("kps", "w", "S", "qS", "o"))

    def spread(gate):
        return gate.rearrange("p i (h o) -> p (i h) o", o=1).broadcast_to([P, NT * H1, DK])

    with nc.Block() as block:
        @block.sync
        def _(sp):
            xin = a["x"].rearrange("b (i p) d -> p (b i) d", p=P)
            for c in range(NC):
                sp.dma_start(x[:, 4 * c:4 * c + 4, :], xin[:, 4 * c:4 * c + 4, :]).then_inc(g["ld_x"][c], 16)
            for k, name in enumerate(("W_gamma", "b_gamma", "W_lambda", "b_lambda")):
                src = a[name].rearrange("(o h) -> o h", o=1)
                sp.dma_start(par[:, k, :], src.broadcast_to([P, H1])).then_inc(ld_p, 16)

        @block.scalar
        def _(act):
            act.dma_start(ident[:], a["ident"]).then_inc(g["ld_id"], 16)
            for k, name in enumerate(("WkT", "WqT", "WvT")):
                act.dma_start(wT[:, (1, 0, 2)[k], :], a[name]).then_inc(ld_w, 16)
            wo = a["WoT"].rearrange("(h j) e -> h j e", j=DK)
            for v in range(DK):
                act.dma_start(wo_rep[v:P:DK, :, :], wo).then_inc(ld_o, 16)
            for c in range(NC):
                act.wait_ge(xT_ps, 4 * c + 4)
                nc.scalar.copy(xT[:, CH * c:CH * c + CH], ps[c][:]).then_inc(xT_done, 1)
            for c in range(NC):
                act.wait_ge(kt_ps, 4 * c + 4)
                nc.scalar.activation(ksq[:, 4 * c:4 * c + 4, :].rearrange("p i d -> p (i d)"), ps[c][:],
                                     ACT.Square).then_inc(ksq_done, 1)
            for c in range(NC):
                for k, dst in enumerate((qT, vT)):
                    act.wait_ge(proj, 2 * c + k + 1)
                    nc.scalar.copy(dst[:, CH * c:CH * c + CH], ps[4 + (2 * c + k) % 4][:]).then_inc(proj_out, 1)
            act.wait_ge(z_done, 1)
            nc.scalar.activation(gat[:, 0:2].rearrange("p k i h -> p (k i h)"),
                                 gat[:, 0:2].rearrange("p k i h -> p (k i h)"), ACT.Tanh, scale=0.5).then_inc(th_done, 1)
            act.wait_ge(gate_done, 1)
            nc.scalar.copy(rho_x[:].rearrange("p i (h v) -> p (i h) v", v=DK), spread(gat[:, 2])).then_inc(rho_spread, 1)
            for c in range(NC):
                act.wait_ge(exp_ps, 2 * c + 1)
                nc.scalar.copy(rhoE[:, CH * c:CH * c + CH], ps[2 * (c % 2)][:]).then_inc(rho_out, 1)

        @block.gpsimd
        def _(pool):
            pool.wait_ge(ld_w, 48)
            for j in range(DK):
                src = wT[:, 1, j::DK].rearrange("p (h o) -> p h o", o=1).broadcast_to([P, H1, DK])
                nc.gpsimd.tensor_copy(wk_rep[:, j, :].rearrange("p (h v) -> p h v", v=DK), src).then_inc(rep, 1)
            for b in range(B):
                for j in range(DK):
                    n = DK * b + j
                    pool.wait_ge(S_done, n + 1)
                    if n >= 2:
                        pool.wait_ge(o_ps, n - 1)
                    if n == 0:
                        pool.wait_ge(proj_out, 2 * NC)
                    nc.gpsimd.tensor_tensor(qS[:, n % 2, :], S[:, n % 2, :], qT[:, T * b:T * b + T],
                                            ALU.mult).then_inc(qS_done, 1)

        @block.tensor
        def _(pe):
            pe.wait_ge(g["ld_id"], 16)
            for i in range(NT):
                pe.wait_ge(xn_done, i + 1)
                nc.tensor.transpose(ps[i // 4][:, P * (i % 4):P * (i % 4) + P], xn[:, i, :], ident[:]).then_inc(xT_ps, 1)
            pe.wait_ge(ld_w, 48)
            pe.wait_ge(xT_done, NC)
            for i in range(NT):
                nc.tensor.matmul(ps[i // 4][:, P * (i % 4):P * (i % 4) + P], xT[:, P * i:P * i + P], wT[:, 1, :],
                                 start=True, stop=True).then_inc(kt_ps, 1)
            for c in range(NC):
                for k in range(2):
                    n = 2 * c + k
                    if n >= 4:
                        pe.wait_ge(proj_out, n - 3)
                    nc.tensor.matmul(ps[4 + n % 4][:], wT[:, 2 * k, :], xT[:, CH * c:CH * c + CH],
                                     start=True, stop=True).then_inc(proj, 1)
            pe.wait_ge(s_done, NC)
            for c in range(NC):
                if c >= 2:
                    pe.wait_ge(rho_out, c - 1)
                    pe.wait_ge(u_done, c - 1)
                if c == 0:
                    pe.wait_ge(rho_spread, 1)
                    pe.wait_ge(g_spread, 1)
                for k in range(2):
                    for i in range(4):
                        mm = nc.tensor.transpose(ps[2 * (c % 2) + k][:, P * i:P * i + P],
                                                 (rho_x, g_x)[k][:, 4 * c + i, :], ident[:])
                    mm.then_inc(exp_ps, 1)
            pe.wait_ge(rep, DK)
            pe.wait_ge(ld_o, 16 * DK)
            pe.wait_ge(proj_out, 2 * NC)
            pe.wait_ge(u_done, NC)
            pe.wait_ge(rho_out, NC)

            def key_column(n):
                if n >= 2:
                    pe.wait_ge(w_done, n - 1)
                for h in range(2):
                    c = T * (n // DK) + CH * h
                    mm = nc.tensor.matmul(ps[2 * (n % 2) + h][:], wk_rep[:, n % DK, :], xT[:, c:c + CH],
                                          start=True, stop=True)
                mm.then_inc(k_ps, 1)

            key_column(0)
            for n in range(B * DK):
                if n + 1 < B * DK:
                    key_column(n + 1)
                pe.wait_ge(qS_done, n + 1)
                b, j = n // DK, n % DK
                for i in range(TB):
                    mm = nc.tensor.matmul(ps[4 + 2 * b + i // 4][:, P * (i % 4):P * (i % 4) + P],
                                          qS[:, n % 2, P * i:P * i + P], wo_rep[:, j, :],
                                          start=(j == 0 and i % 4 == 0), stop=(j == DK - 1), skip_group_check=True)
                mm.then_inc(o_ps, 1)

        @block.vector
        def _(ve):
            link = Chain(ve, dve)
            for c in range(NC):
                ve.wait_ge(g["ld_x"][c], 16)
            layer_norm(nc, link, xn, x, stats, small, xn_done)
            for c in range(NC):
                ve.wait_ge(ksq_done, c + 1)
                nc.vector.tensor_reduce(s1[:, 4 * c:4 * c + 4, :], ps[c][:].rearrange("p (i h j) -> p i h j", i=4, j=DK),
                                        AX, ALU.add)
                nc.vector.tensor_reduce(s2[:, 4 * c:4 * c + 4, :],
                                        ksq[:, 4 * c:4 * c + 4, :].rearrange("p i (h j) -> p i h j", j=DK),
                                        AX, ALU.add).then_inc(s_done, 1)
            ve.wait_ge(s_done, NC)
            flat = lambda t: t.rearrange("p i h -> p (i h)")
            g0, g1, g2, g3 = (flat(gat[:, k]) for k in range(4))
            link(nc.vector.tensor_scalar(flat(s2[:]), flat(s2[:]), 1e-24, None, ALU.max))
            rsqrt(nc, link, g2, flat(s2[:]), g3)
            link(nc.vector.scalar_tensor_tensor(out=flat(s1[:]), in0=flat(s1[:]), scalar=1.0 / DK, in1=g2,
                                                op0=ALU.mult, op1=ALU.mult))
            ve.wait_ge(ld_p, 64)
            bc = lambda k: par[:, k, :].rearrange("p (o h) -> p o h", o=1).broadcast_to([P, NT, H1])
            for k in range(2):
                link(nc.vector.tensor_tensor(gat[:, k], s1[:], bc(2 * k), ALU.mult))
                ins = nc.vector.tensor_tensor(gat[:, k], gat[:, k], bc(2 * k + 1), ALU.add)
                if k == 0:
                    link(ins)
            ins.then_inc(z_done, 1)
            ve.wait_ge(th_done, 1)
            link(nc.vector.tensor_scalar(g1, g1, -0.25, 0.25, ALU.mult, ALU.add))
            link(nc.vector.scalar_tensor_tensor(out=g0, in0=g0, scalar=1.0, in1=g1, op0=ALU.add, op1=ALU.mult))
            link(nc.vector.tensor_scalar(g3, g0, -1.0, 1.0, ALU.mult, ALU.add))
            link(nc.vector.tensor_tensor(g3, g3, g2, ALU.mult))
            nc.vector.tensor_copy(g2, g0).then_inc(gate_done, 1)
            nc.vector.tensor_copy(g_x[:].rearrange("p i (h v) -> p (i h) v", v=DK), spread(gat[:, 3])).then_inc(g_spread, 1)
            ve.wait_ge(proj_out, 2 * NC)
            for c in range(NC):
                ve.wait_ge(exp_ps, 2 * c + 2)
                cols = slice(CH * c, CH * c + CH)
                nc.vector.tensor_tensor(uT[:, cols], vT[:, cols], ps[2 * (c % 2) + 1][:], ALU.mult).then_inc(u_done, 1)
            ve.wait_ge(u_done, NC)
            ve.wait_ge(rho_out, NC)
            for n in range(B * DK):
                b = n // DK
                ve.wait_ge(k_ps, n + 1)
                for h in range(2):
                    ins = nc.vector.tensor_tensor(w[:, n % 2, CH * h:CH * h + CH],
                                                  uT[:, T * b + CH * h:T * b + CH * h + CH],
                                                  ps[2 * (n % 2) + h][:], ALU.mult)
                ins.then_inc(w_done, 1)
                ve.wait_ge(w_done, n + 1)
                if n >= 2:
                    ve.wait_ge(qS_done, n - 1)
                nc.vector.tensor_tensor_scan(S[:, n % 2, :], rhoE[:, T * b:T * b + T], w[:, n % 2, :], 0.0,
                                             ALU.mult, ALU.add).then_inc(S_done, 1)
            for b in range(B):
                ve.wait_ge(o_ps, DK * (b + 1))
                for h in range(2):
                    i = TB * b + 4 * h
                    xs = x[:, i:i + 4, :].rearrange("p i d -> p (i d)")
                    nc.vector.tensor_tensor(xs, xs, ps[4 + 2 * b + h][:], ALU.add)


def turn_tiles(nc, eng, ps, src, ident, ready, turned, first=0):
    for i in range(first, first + NT):
        eng.wait_ge(ready, i + 1)
        nc.tensor.transpose(ps[i // 4][:, P * (i % 4):P * (i % 4) + P], src[:, i, :], ident[:]).then_inc(turned, 1)


def grouped_experts(nc, own, a, m, g, ps):
    sb, sem = scoped(nc, own)
    x, xn, xT, stats, small, ident = (m[k] for k in ("x", "xn", "xT", "stats", "small", "ident"))
    wt = sb("b_wt", [P, 2, 3, D])
    rw = sb("b_rw", [P, E0])
    bias = sb("b_bias", [P, E0])
    low_e = sb("b_low_e", [P, E0, E0])
    low_g = sb("b_low_g", [P, NG, NG])
    sc = sb("b_sc", [P, NT, E0])
    s = sb("b_s", [P, NT, E0])
    gs = sb("b_gs", [P, 6, NT, NG])
    rank = sb("b_rank", [P, 2, NT, E0 * E0])
    rk = sb("b_rk", [P, NT, E0])
    tot = sb("b_tot", [P, NT])
    comb = sb("b_comb", [P, NT, W0])
    th = sb("b_th", [P, 2, CH])
    act_ = sb("b_act", [P, 4, CH])
    ld_c, ld_w = sem("b_ld_c"), [sem("b_ld_w0"), sem("b_ld_w1")]
    dve, xn_done, xT_ps, xT_done = sem("b_dve"), sem("b_xn"), sem("b_xT_ps"), sem("b_xT")
    logit, esig = sem("b_logit"), sem("b_esig")
    h_ps, u_ps, th_done, hu_done, h_free, y_ps, acc_done = (sem("b_" + n) for n in
                                                          ("h", "u", "th", "hu", "hfree", "y", "acc"))
    gtmp = sem("b_gtmp")

    with nc.Block() as block:
        @block.sync
        def _(sp):
            sp.dma_start(rw[:], a["router0"]).then_inc(ld_c, 16)
            sp.dma_start(bias[:], a["bias0"].rearrange("(o e) -> o e", o=1).broadcast_to([P, E0])).then_inc(ld_c, 16)
            sp.dma_start(low_e[:].rearrange("p i j -> p (i j)"),
                         a["low_e"].rearrange("(o e) -> o e", o=1).broadcast_to([P, E0 * E0])).then_inc(ld_c, 16)
            sp.dma_start(low_g[:].rearrange("p i j -> p (i j)"),
                         a["low_g"].rearrange("(o e) -> o e", o=1).broadcast_to([P, NG * NG])).then_inc(ld_c, 16)
            w = a["moe0"].rearrange("(f k) r c -> k f r c", k=2)
            for k in range(2):
                sp.dma_start(wt[:, k].rearrange("p m c -> p (m c)"), w[k, 0]).then_inc(ld_w[k], 16)
            with nc.sync.Fori(1, W0 // 2) as f:
                for k in range(2):
                    sp.wait_ge(y_ps, f * (2 * NC) + (k - 1) * NC)
                    sp.dma_start(wt[:, k].rearrange("p m c -> p (m c)"),
                                 w[k, bass.ds(f, 1)].rearrange("o r c -> r (o c)")).then_inc(ld_w[k], 16)

        @block.scalar
        def _(act):
            for c in range(NC):
                act.wait_ge(xT_ps, 4 * c + 4)
                nc.scalar.copy(xT[:, CH * c:CH * c + CH], ps[c][:]).then_inc(xT_done, 1)
            act.wait_ge(logit, 1)
            nc.scalar.activation(sc[:].rearrange("p i e -> p (i e)"), ps[4][:, 0:NT * E0], ACT.Exp,
                                 scale=-1.0).then_inc(esig, 1)
            nc.scalar.preload_act_table(ACT.Tanh)
            with nc.scalar.Fori(0, W0) as e:
                for c in range(NC):
                    act.wait_ge(h_ps, e * NC + (c + 1))
                    act.wait_ge(hu_done, e * NC + (c + 1))
                    nc.scalar.activation(th[:, c % 2, :], ps[c % 2][:], ACT.Tanh, scale=0.5).then_inc(th_done, 1)

        @block.tensor
        def _(pe):
            turn_tiles(nc, pe, ps, xn, ident, xn_done, xT_ps)
            pe.wait_ge(ld_c, 64)
            pe.wait_ge(xT_done, NC)
            for i in range(NT):
                mm = nc.tensor.matmul(ps[4][:, E0 * i:E0 * i + E0], xT[:, P * i:P * i + P], rw[:], start=True, stop=True)
            mm.then_inc(logit, 1)
            pe.wait_ge(esig, 1)

            def up(k, e, c):
                pe.wait_ge(hu_done, e * NC + (c + 1))
                nc.tensor.matmul(ps[c % 2][:], wt[:, k, 0, :], xT[:, CH * c:CH * c + CH], start=True,
                                 stop=True).then_inc(h_ps, 1)
                nc.tensor.matmul(ps[2 + c % 2][:], wt[:, k, 1, :], xT[:, CH * c:CH * c + CH], start=True,
                                 stop=True).then_inc(u_ps, 1)

            def down(k, e, c):
                pe.wait_ge(hu_done, e * NC + (c + 3))
                pe.wait_ge(acc_done, e * NC + (c + 1))
                for i in range(4):
                    mm = nc.tensor.matmul(ps[4 + c % 2][:, P * i:P * i + P], act_[:, c, P * i:P * i + P],
                                          wt[:, k, 2, :], start=True, stop=True)
                mm.then_inc(y_ps, 1)
                return mm

            with nc.tensor.Fori(0, W0 // 2) as f:
                for k in range(2):
                    e = f * 2 + k
                    pe.wait_ge(ld_w[k], f * 16 + 16)
                    up(k, e, 0)
                    up(k, e, 1)
                    down(k, e, 0)
                    up(k, e, 2)
                    down(k, e, 1)
                    up(k, e, 3)
                    down(k, e, 2)
                    down(k, e, 3)

        @block.vector
        def _(ve):
            link = Chain(ve, dve)
            nc.vector.memset(tot[:], 0.0).then_inc(hu_done, 2)
            nc.vector.memset(rk[:], 0.0).then_inc(acc_done, 2)
            layer_norm(nc, link, xn, x, stats, small, xn_done)
            ve.wait_ge(esig, 1)
            flat = lambda t: t.rearrange("p i e -> p (i e)")
            link(nc.vector.tensor_scalar(flat(sc[:]), flat(sc[:]), 1.0, None, ALU.add))
            link(nc.vector.reciprocal(flat(sc[:]), flat(sc[:])))
            link(nc.vector.tensor_tensor(s[:], sc[:], bias[:].rearrange("p (o e) -> p o e", o=1).broadcast_to([P, NT, E0]),
                                         ALU.add))
            mem = [flat(s[:]).rearrange("p (i g q) -> p i g q", i=NT, g=NG)[:, :, :, q] for q in range(4)]
            nc.vector.tensor_tensor(gs[:, 0], mem[0], mem[1], ALU.add)
            nc.vector.tensor_tensor(gs[:, 1], mem[2], mem[3], ALU.add)
            nc.vector.tensor_tensor(gs[:, 2], mem[0], mem[1], ALU.max)
            link(nc.vector.tensor_tensor(gs[:, 3], mem[2], mem[3], ALU.max))
            nc.vector.tensor_tensor(gs[:, 0], gs[:, 0], gs[:, 1], ALU.max)
            link(nc.vector.tensor_tensor(gs[:, 4], gs[:, 2], gs[:, 3], ALU.add))
            link(nc.vector.tensor_tensor(gs[:, 0], gs[:, 0], gs[:, 4], ALU.max))
            ranks(nc, link, gs[:, 5], gs[:, 0], rank, low_g, NG)
            keep = gs[:, 4]
            link(nc.vector.tensor_scalar(flat(keep), flat(gs[:, 5]), float(TKG), None, ALU.is_lt))
            keep_e = keep.rearrange("p i (g o) -> p (i g) o", o=1).broadcast_to([P, NT * NG, E0 // NG])
            s_g = flat(s[:]).rearrange("p (ig q) -> p ig q", q=E0 // NG)
            link(nc.vector.tensor_tensor(s_g, s_g, keep_e, ALU.mult))
            link(nc.vector.tensor_scalar(flat(keep), flat(keep), 1.0, None, ALU.subtract))
            link(nc.vector.tensor_tensor(s_g, s_g, keep_e, ALU.add))
            ranks(nc, link, rk[:], s[:], rank, low_e, E0)
            link(nc.vector.tensor_scalar(flat(rk[:]), flat(rk[:]), float(K0), None, ALU.is_lt))
            link(nc.vector.tensor_tensor(sc[:], sc[:], rk[:], ALU.mult))
            link(nc.vector.tensor_reduce(tot[:], sc[:], AX, ALU.add))
            link(nc.vector.tensor_scalar(tot[:], tot[:], 1e-20, None, ALU.add))
            link(nc.vector.reciprocal(tot[:], tot[:]))
            link(nc.vector.tensor_scalar(tot[:], tot[:], 1.25, None, ALU.mult))
            nc.vector.tensor_tensor(comb[:, :, 0:E0], sc[:],
                                    tot[:].rearrange("p (i o) -> p i o", o=1).broadcast_to([P, NT, E0]), ALU.mult)
            link(nc.vector.memset(comb[:, :, E0:W0], 0.5))

            def silu(e, c):
                ve.wait_ge(th_done, e * NC + (c + 1))
                nc.vector.scalar_tensor_tensor(out=act_[:, c, :], in0=th[:, c % 2, :], scalar=1.0, in1=ps[c % 2][:],
                                               op0=ALU.add, op1=ALU.mult).then_inc(gtmp, 1)
                ve.wait_ge(u_ps, e * NC + (c + 1))
                ve.wait_ge(gtmp, e * NC + (c + 1))
                nc.vector.tensor_tensor(act_[:, c, :], act_[:, c, :], ps[2 + c % 2][:], ALU.mult).then_inc(hu_done, 1)

            def accumulate(e, c):
                ve.wait_ge(y_ps, e * NC + (c + 1))
                for i in range(4 * c, 4 * c + 4):
                    ins = nc.vector.scalar_tensor_tensor(out=x[:, i, :], in0=ps[4 + c % 2][:, P * (i % 4):P * (i % 4) + P],
                                                         scalar=comb[:, i, bass.ds(e, 1)], in1=x[:, i, :],
                                                         op0=ALU.mult, op1=ALU.add)
                ins.then_inc(acc_done, 1)

            with nc.vector.Fori(0, W0) as e:
                silu(e, 0)
                silu(e, 1)
                accumulate(e, 0)
                silu(e, 2)
                accumulate(e, 1)
                silu(e, 3)
                accumulate(e, 2)
                accumulate(e, 3)


def ranks(nc, link, out, val, scratch, low, n):
    gt = scratch[:, 0, :, 0:n * n].rearrange("p t (i j) -> p t i j", j=n)
    eq = scratch[:, 1, :, 0:n * n].rearrange("p t (i j) -> p t i j", j=n)
    other = val.rearrange("p t (o j) -> p t o j", o=1).broadcast_to([P, NT, n, n])
    own = val.rearrange("p t (i o) -> p t i o", o=1).broadcast_to([P, NT, n, n])
    lower = low[:].rearrange("p (o i) j -> p o (i j)", o=1).broadcast_to([P, NT, n * n])
    nc.vector.tensor_tensor(gt, other, own, ALU.is_gt)
    link(nc.vector.tensor_tensor(eq, other, own, ALU.is_equal))
    link(nc.vector.tensor_tensor(scratch[:, 1, :, 0:n * n], scratch[:, 1, :, 0:n * n], lower, ALU.mult))
    link(nc.vector.tensor_tensor(gt, gt, eq, ALU.add))
    link(nc.vector.tensor_reduce(out, gt, AX, ALU.add))


def gelu_recurrence(nc, own, a, m, g, ps):
    sb, sem = scoped(nc, own)
    x, xn, xT, stats, small, ident = (m[k] for k in ("x", "xn", "xT", "stats", "small", "ident"))
    HALF = 32
    RING = 2 * HALF
    wABC = sb("c_w", [P, 3, D])
    A12 = sb("c_A12", [P, 2, D], F16)
    A1f = sb("c_A1f", [P, D])
    gb = sb("c_gb", [P, 2, D])
    h1 = sb("c_h1", [P, RING, B], F16)
    h2 = sb("c_h2", [P, RING, B], F16)
    hf = sb("c_hf", [P, RING, B])
    hall = sb("c_hall", [P, B, T])
    ld_w, dve, xn_done, xT_ps, xT_done = (sem("c_" + n) for n in ("ldw", "dve", "xn", "xT_ps", "xT"))
    zero, split, h1_done, hf_done, h2_done, z_ps, kept = (sem("c_" + n) for n in
                                                         ("zero", "split", "h1", "hf", "h2", "z", "kept"))
    y_ps, nrm, out_done = sem("c_y"), sem("c_nrm"), sem("c_out")
    xs = xT[:].rearrange("p (b t) -> p t b", b=B)

    with nc.Block() as block:
        @block.sync
        def _(sp):
            for k, name in enumerate(("AT", "BT", "CT")):
                sp.dma_start(wABC[:, k, :], a[name]).then_inc(ld_w, 16)
            for k, name in enumerate(("gamma", "beta")):
                sp.dma_start(gb[:, k, :], a[name].rearrange("(o e) -> o e", o=1).broadcast_to([P, D])).then_inc(ld_w, 16)

        @block.scalar
        def _(act):
            for c in range(NC):
                act.wait_ge(xT_ps, 4 * c + 4)
                nc.scalar.copy(xT[:, CH * c:CH * c + CH], ps[c][:]).then_inc(xT_done, 1)
            nc.scalar.preload_act_table(ACT.Gelu)
            with nc.scalar.Fori(0, T // RING) as r:
                for s in range(RING):
                    if s % HALF == 0:
                        act.wait_ge(kept, r * 2 + (s // HALF + 1))
                    z = ps[4 + 2 * (s // HALF) + s % 2][:, B * (s % HALF // 2):B * (s % HALF // 2) + B]
                    act.wait_ge(z_ps, r * RING + (s + 1))
                    nc.scalar.activation(h1[:, s, :], z, ACT.Gelu, scale=1.0 / ZSCALE).then_inc(h1_done, 1)
                    nc.scalar.activation(hf[:, s, :], z, ACT.Gelu, scale=1.0 / ZSCALE).then_inc(hf_done, 1)

        @block.gpsimd
        def _(pool):
            nc.gpsimd.memset(hall[:, 0, 0:2], 0.0).then_inc(kept, 2)
            with nc.gpsimd.Fori(0, T // RING) as r:
                for k in range(2):
                    pool.wait_ge(hf_done, r * RING + HALF * (k + 1))
                    nc.gpsimd.tensor_copy(hall[:, :, bass.ds(r * RING + k * HALF, HALF)],
                                          hf[:, HALF * k:HALF * k + HALF, :].rearrange("p t b -> p b t")).then_inc(kept, 1)

        @block.tensor
        def _(pe):
            turn_tiles(nc, pe, ps, xn, ident, xn_done, xT_ps)
            pe.wait_ge(xT_done, NC)
            pe.wait_ge(zero, 2)
            pe.wait_ge(split, 1)

            def inputs(k, par, t0):
                nc.tensor.matmul(ps[4 + 2 * k + par][:, 0:HALF], wABC[:, 1, :], xs[:, bass.ds(t0, HALF // 2, step=2), :],
                                 start=True, stop=True, skip_group_check=True)

            with nc.tensor.Fori(0, T // RING) as r:
                inputs(0, 0, r * RING)
                inputs(0, 1, r * RING + 1)
                for s in range(RING):
                    prev = (s - 1) % RING
                    z = ps[4 + 2 * (s // HALF) + s % 2][:, B * (s % HALF // 2):B * (s % HALF // 2) + B]
                    pe.wait_ge(h1_done, r * RING + (s + 1))
                    nc.tensor.matmul(z, A12[:, 1, :], h1[:, prev, :], start=False, stop=True, skip_group_check=True)
                    nc.tensor.matmul(z, A12[:, 0, :], h1[:, prev, :], start=False, stop=True, skip_group_check=True)
                    pe.wait_ge(h2_done, r * RING + (s + 1))
                    nc.tensor.matmul(z, A12[:, 0, :], h2[:, prev, :], start=False, stop=True,
                                     skip_group_check=True).then_inc(z_ps, 1)
                    if s in (4, 5):
                        inputs(1, s % 2, r * RING + (HALF + s % 2))
            for i in range(NT):
                if i == 0:
                    pe.wait_ge(kept, T // HALF + 2)
                hp = hall[:].rearrange("p b t -> p (b t)")[:, P * i:P * i + P]
                nc.tensor.matmul(ps[i // 4][:, P * (i % 4):P * (i % 4) + P], hp, wABC[:, 2, :],
                                 start=True, stop=True).then_inc(y_ps, 1)

        @block.vector
        def _(ve):
            link = Chain(ve, dve)
            nc.vector.memset(h1[:, RING - 1, :], 0.0).then_inc(h1_done, 1)
            nc.vector.memset(h2[:, RING - 1, :], 0.0).then_inc(h2_done, 1)
            nc.vector.memset(hf[:, RING - 1, :], 0.0).then_inc(zero, 2)
            layer_norm(nc, link, xn, x, stats, small, xn_done)
            ve.wait_ge(ld_w, 80)
            link(nc.vector.tensor_scalar(wABC[:, 0:2], wABC[:, 0:2], ZSCALE, None, ALU.mult))
            link(nc.vector.tensor_copy(A12[:, 0, :], wABC[:, 0, :]))
            link(nc.vector.tensor_copy(A1f[:], A12[:, 0, :]))
            nc.vector.tensor_tensor(A12[:, 1, :], wABC[:, 0, :], A1f[:], ALU.subtract).then_inc(split, 1)
            with nc.vector.Fori(0, T // RING) as r:
                for s in range(RING):
                    ve.wait_ge(hf_done, r * RING + (s + 1))
                    nc.vector.tensor_tensor(h2[:, s, :], hf[:, s, :], h1[:, s, :], ALU.subtract).then_inc(h2_done, 1)
            for i in range(NT):
                ve.wait_ge(y_ps, i + 1 if i % 4 else i + 4)
                ins = nc.vector.bn_stats(stats[:, i, :], ps[i // 4][:, P * (i % 4):P * (i % 4) + P])
            link(ins)
            ln_moments(nc, link, stats, small)
            for i in range(NT):
                ins = nc.vector.tensor_scalar(xn[:, i, :], ps[i // 4][:, P * (i % 4):P * (i % 4) + P],
                                              small[:, 0, i:i + 1], small[:, 1, i:i + 1], ALU.subtract, ALU.mult)
            link(ins)
            whole = lambda k: gb[:, k, :].rearrange("p (o e) -> p o e", o=1).broadcast_to([P, NT, D])
            link(nc.vector.tensor_tensor(xn[:], xn[:], whole(0), ALU.mult))
            link(nc.vector.tensor_tensor(xn[:], xn[:], whole(1), ALU.add))
            link(nc.vector.tensor_tensor(x[:], x[:], xn[:], ALU.add))


def attention_experts(nc, own, a, m, g, ps):
    sb, sem = scoped(nc, own)
    mla = sb("d_mla", [P, B * T])
    with ExitStack() as inner:
        attention(nc, inner, a, m, g, ps, mla)
    gelu_experts(nc, own, a, m, g, ps, mla)


PARTS = 3
TERMS = ((0, 0), (0, 1), (1, 0), (1, 1), (0, 2), (2, 0))
MAX_ROW = len(TERMS) * KPH
GROUPS = B * NHG
K_AT, Q_AT = 1, 3
UNITS = HG * TB


def selections():
    import numpy as np
    sel = np.zeros((2, H3, KPH, NHG, 2, PARTS, HG, 32), np.float32)
    for h in range(H3):
        for t, parts in enumerate(TERMS):
            for side in range(2):
                for k in range(KPH):
                    sel[side, h, k, h // HG, side, parts[side], h % HG, t * KPH + k] = 1
    return sel.reshape(P, NHG * 2 * PARTS * P)


def attention(nc, own, a, m, g, ps, mla):
    sb, sem = scoped(nc, own)
    x, xn, xT, stats, small, ident = (m[k] for k in ("x", "xn", "xT", "stats", "small", "ident"))
    banks = m["banks"]
    wqk = sb("d_wqk", [P, P])
    wv = sb("d_wv", [P, LAT])
    wo = sb("d_wo", [LAT, D])
    col = sb("d_col", [P, 3 + HG])
    vb = sb("d_vb", [P, LAT])
    sel = sb("d_sel", [P, NHG, 2, PARTS, P], BF16)
    idb = sb("d_idb", [P, P], BF16)
    qk = sb("d_qk", [P, B * T])
    part = sb("d_part", [P, PARTS, B * T], BF16)
    vall = sb("d_vall", [P, NT, H3, KPH])
    vs = sb("d_vs", [P, 2, TB, HG, 32])
    kall = sb("d_kall", [P, T], BF16)
    km = sb("d_km", [P, 2, HG, T], BF16)
    qs = sb("d_qs", [P, T], BF16)
    qm = sb("d_qm", [P, T], BF16)
    mx = sb("d_mx", [P, 2, TB, HG])
    mtop = sb("d_mtop", [P, 2, TB, HG])
    mrow = sb("d_mrow", [P, TB, HG, 32], BF16)
    NE = 2 * HG
    ex = sb("d_ex", [P, NE, T])
    ot = sb("d_ot", [P, T])
    rs = sb("d_rs", [P, TB, HG])
    ao = sb("d_ao", [P, NT, LAT])
    aoT = sb("d_aoT", [LAT, B * T])
    ld_c, dve, xn_done, xT_ps, xT_done = (sem("d_" + n) for n in ("ldc", "dve", "xn", "xT_ps", "xT"))
    qk_ps, qk_done, split, v_ps, v_done, hs_in = (sem("d_" + n) for n in ("qk_ps", "qk", "split", "v_ps", "v", "hs"))
    k_ps, k_out, q_ps, q_out, km_done, vs_done = (sem("d_" + n) for n in ("k_ps", "k_out", "q_ps", "q_out", "km", "vs"))
    s_ps, s_max, m_done, qm_ps, qm_out = (sem("d_" + n) for n in ("s_ps", "smax", "m", "qm_ps", "qm_out"))
    e_ps, e_done, pv, ot_done, ot_ps, ao_done = (sem("d_" + n) for n in ("e_ps", "e", "pv", "ot", "ot_ps", "ao"))
    aoT_ps, aoT_done, mla_ps, fin = (sem("d_" + n) for n in ("aoT_ps", "aoT", "mla_ps", "fin"))
    ready, mdve, rs_done = sem("d_ready"), sem("d_mdve"), sem("d_rs")
    aov = ao[:].rearrange("p (b s) (g c) -> p b g s c", b=B, g=NHG)

    with nc.Block() as block:
        @block.sync
        def _(sp):
            sp.dma_start(wqk[:], a["wqk"]).then_inc(ld_c, 16)
            sp.dma_start(wv[:], a["wv1"]).then_inc(ld_c, 16)
            sp.dma_start(wo[:], a["wo1"]).then_inc(ld_c, 16)
            sp.dma_start(col[:, 0:1], a["bqk"].rearrange("(p o) -> p o", o=1)).then_inc(ld_c, 16)
            sp.dma_start(col[:, 1:2], a["ob1"].rearrange("(p o) -> p o", o=1)).then_inc(ld_c, 16)
            sp.dma_start(col[:, 2:3 + HG], a["rows"]).then_inc(ld_c, 16)
            sp.dma_start(vb[:], a["vb1"].rearrange("(o e) -> o e", o=1).broadcast_to([P, LAT])).then_inc(ld_c, 16)
            sp.dma_start(sel[:].rearrange("p g s k c -> p (g s k c)"), a["sel"]).then_inc(ld_c, 16)
            sp.dma_start(idb[:], a["identb"]).then_inc(ld_c, 16)

        LOADS = 16 * 9

        @block.scalar
        def _(act):
            for c in range(NC):
                act.wait_ge(xT_ps, 4 * c + 4)
                nc.scalar.copy(xT[:, CH * c:CH * c + CH], ps[c][:]).then_inc(xT_done, 1)
            act.wait_ge(ld_c, LOADS)
            for c in range(NC):
                act.wait_ge(qk_ps, c + 1)
                nc.scalar.activation(qk[:, CH * c:CH * c + CH], ps[4 + c][:], ACT.Identity, bias=col[:, 0:1]).then_inc(qk_done, 1)
            nc.scalar.preload_act_table(ACT.Exp)

            def k_rows(n):
                for h in range(2):
                    act.wait_ge(k_ps, n * 2 + (h + 1))
                    nc.scalar.activation(kall[:, CH * h:CH * h + CH], ps[h][:], ACT.Identity,
                                         bias=col[:, 2:3]).then_inc(k_out, 1)

            def q_rows(n, dst, made, taken):
                for h in range(2):
                    act.wait_ge(made, n * 2 + (h + 1))
                    nc.scalar.copy(dst[:, CH * h:CH * h + CH], ps[h][:]).then_inc(taken, 1)

            def group(n, more):
                for u in range(UNITS):
                    act.wait_ge(e_ps, n * UNITS + (u + 1))
                    if u % HG == 0:
                        act.wait_ge(pv, n * TB + (u // HG + 1))
                    nc.scalar.activation(ex[:, (u % NE), :], banks[:, 2 + 2 * (u % 2):4 + 2 * (u % 2), :].rearrange("p k c -> p (k c)"),
                                         ACT.Exp, scale=0.5).then_inc(e_done, 1)
                    if more and u == K_AT + 1:
                        k_rows(n + 1)
                    if more and u == Q_AT + 1:
                        q_rows(n + 1, qs, q_ps, q_out)
                act.wait_ge(pv, n * TB + (TB + 2))
                nc.scalar.copy(ot[:], banks[:, 6:8, :].rearrange("p k c -> p (k c)")).then_inc(ot_done, 1)
                if more:
                    q_rows(n + 1, qm, qm_ps, qm_out)

            k_rows(0)
            q_rows(0, qs, q_ps, q_out)
            q_rows(0, qm, qm_ps, qm_out)
            with nc.scalar.Fori(0, GROUPS // 2 - 1) as f:
                for k in range(2):
                    group(f * 2 + k, True)
            group(GROUPS - 2, True)
            group(GROUPS - 1, False)
            for c in range(NC):
                act.wait_ge(aoT_ps, 4 * c + 4)
                nc.scalar.copy(aoT[:, CH * c:CH * c + CH], ps[c][0:LAT, :]).then_inc(aoT_done, 1)
            for c in range(NC):
                act.wait_ge(mla_ps, c + 1)
                nc.scalar.activation(mla[:, CH * c:CH * c + CH], ps[4 + c][:], ACT.Identity, bias=col[:, 1:2]).then_inc(fin, 1)

        @block.gpsimd
        def _(pool):
            nc.gpsimd.memset(vs[:], 1.0).then_inc(vs_done, 1)
            nc.gpsimd.memset(mrow[:].rearrange("p s h c -> p (s h c)"), 0.0).then_inc(ready, 1)
            pool.wait_ge(xn_done, NT)
            nc.gpsimd.tensor_tensor(x[:], x[:], xn[:], ALU.add).then_inc(hs_in, 1)
            pool.wait_ge(v_done, NT // 4)
            pool.wait_ge(vs_done, 1)
            vv = vall[:].rearrange("p (b s) (g h) k -> p b g s (h k)", b=B, g=NHG)
            with nc.gpsimd.Fori(0, B) as b:
                with nc.gpsimd.Fori(0, NHG // 2) as hp:
                    for k in range(2):
                        n = b * NHG + hp * 2 + k
                        pool.wait_ge(ot_done, n + 1)
                        for h in range(HG):
                            src = vv[:, bass.ds(b, 1), bass.ds(hp * 2 + k, 1), :, KPH * h:KPH * h + KPH]
                            ins = nc.gpsimd.tensor_copy(vs[:, k, :, h, 0:KPH], src.rearrange("p a c s k -> p (a c s) k"))
                        ins.then_inc(vs_done, 1)

        @block.tensor
        def _(pe):
            turn_tiles(nc, pe, ps, xn, ident, xn_done, xT_ps)
            pe.wait_ge(ld_c, LOADS)
            for c in range(NC):
                pe.wait_ge(xT_done, c + 1)
                nc.tensor.matmul(ps[4 + c][:], wqk[:], xT[:, CH * c:CH * c + CH], start=True, stop=True).then_inc(qk_ps, 1)
            for i in range(NT):
                nc.tensor.matmul(ps[i // 8][:, LAT * (i % 8):LAT * (i % 8) + LAT], xT[:, P * i:P * i + P], wv[:],
                                 start=True, stop=True).then_inc(v_ps, 1)
            pe.wait_ge(v_done, NT // 4)
            pe.wait_ge(split, 1)
            pe.wait_ge(ready, 1)

            def select(bank, hg, side, b, h, stop):
                for k in range(PARTS):
                    mm = nc.tensor.matmul(bank[:], sel[:, bass.ds(hg, 1), side, k, :].rearrange("p o c -> p (o c)"),
                                          part[:, k, bass.ds(b * T + CH * h, CH)],
                                          start=(k == 0), stop=(k == PARTS - 1 and stop), skip_group_check=True)
                return mm


            def k_select(n):
                if not isinstance(n, int) or n:
                    pe.wait_ge(ao_done, n)
                for h in range(2):
                    select(ps[h], n % NHG, 1, n // NHG, h, True).then_inc(k_ps, 1)

            def q_select(n):
                pe.wait_ge(k_out, n * 2 + 2)
                for h in range(2):
                    select(ps[h], n % NHG, 0, n // NHG, h, True).then_inc(q_ps, 1)

            def scores(n, k, u):
                st, hh = u // HG, u % HG
                if u == 0:
                    pe.wait_ge(q_out, n * 2 + 2)
                if st == 0:
                    pe.wait_ge(km_done, n * HG + (hh + 1))
                for h in range(2):
                    if 2 * u + h >= 2:
                        pe.wait_ge(s_max, n * (2 * UNITS) + (2 * u + h - 1))
                    nc.tensor.matmul(ps[h][:], qs[:, P * st:P * st + P], km[:, k, hh, CH * h:CH * h + CH],
                                     start=True, stop=True).then_inc(s_ps, 1)

            def q_and_max(n):
                pe.wait_ge(m_done, n + 1)
                for h in range(2):
                    select(ps[h], n % NHG, 0, n // NHG, h, False)
                    for i in range(4):
                        st = 4 * h + i
                        mm = nc.tensor.matmul(ps[h][:, P * i:P * i + P], mrow[:, st].rearrange("p h c -> p (h c)"), idb[:],
                                              start=False, stop=True, skip_group_check=True)
                    mm.then_inc(qm_ps, 1)
                pe.wait_ge(qm_out, n * 2 + 2)

            def exps(n, k, u):
                tt, hh = u // HG, u % HG
                if u >= 2:
                    pe.wait_ge(e_done, n * UNITS + (u - 1))
                for h in range(2):
                    mm = nc.tensor.matmul(ps[2 + 2 * (u % 2) + h][:], km[:, k, hh, P * tt:P * tt + P],
                                          qm[:, CH * h:CH * h + CH], start=True, stop=True)
                mm.then_inc(e_ps, 1)

            def values(n, k, tt):
                pe.wait_ge(e_done, n * UNITS + HG * (tt + 1))
                for h in range(2):
                    for hh in range(HG):
                        mm = nc.tensor.matmul(ps[6 + h][32 * hh:32 * hh + 32, :], vs[:, k, tt, hh, :],
                                              ex[:, (HG * tt + hh) % NE, CH * h:CH * h + CH],
                                              start=(tt == 0), stop=(tt == TB - 1),
                                              tile_position=(0, 32 * hh), skip_group_check=True)
                mm.then_inc(pv, 1)

            LAG = 2

            def group(n, k, more):
                pe.wait_ge(vs_done, n + 2)
                if more:
                    done = 0
                for u in range(UNITS + LAG):
                    if u < UNITS:
                        exps(n, k, u)
                    if u % HG == LAG - 1 and u > HG:
                        if u // HG == 1:
                            pe.wait_ge(ot_done, n + 2)
                        values(n, k, u // HG - 1)
                    if more:
                        if u == K_AT:
                            k_select(n + 1)
                        if u == Q_AT:
                            q_select(n + 1)
                        if Q_AT < u:
                            upto = min(UNITS, (u - Q_AT) * UNITS // (UNITS + LAG - 1 - Q_AT))
                            while done < upto:
                                scores(n + 1, 1 - k, done)
                                done += 1
                if more:
                    q_and_max(n + 1)
                else:
                    pe.wait_ge(ao_done, n + 1)
                pe.wait_ge(ot_done, n + 3)
                for i in range(TB):
                    mm = nc.tensor.transpose(ps[i // 4][:, P * (i % 4):P * (i % 4) + P], ot[:, P * i:P * i + P], ident[:])
                mm.then_inc(ot_ps, 1)

            k_select(0)
            q_select(0)
            for u in range(UNITS):
                scores(0, 0, u)
            q_and_max(0)
            with nc.tensor.Fori(0, GROUPS // 2 - 1) as f:
                for k in range(2):
                    group(f * 2 + k, k, True)
            group(GROUPS - 2, 0, True)
            group(GROUPS - 1, 1, False)
            pe.wait_ge(ao_done, B * NHG + 1)
            for i in range(NT):
                nc.tensor.transpose(ps[i // 4][0:LAT, P * (i % 4):P * (i % 4) + P], ao[:, i, :], ident[:]).then_inc(aoT_ps, 1)
            for c in range(NC):
                pe.wait_ge(aoT_done, c + 1)
                nc.tensor.matmul(ps[4 + c][:], wo[:], aoT[:, CH * c:CH * c + CH], start=True, stop=True).then_inc(mla_ps, 1)

        @block.vector
        def _(ve):
            link = Chain(ve, dve)
            nc.vector.memset(rs[:], 0.0).then_inc(pv, 2)
            nc.vector.memset(ot[:, 0:2], 0.0).then_inc(ot_done, 2)
            nc.vector.memset(ao[:, 0, 0:2], 0.0).then_inc(ao_done, 1)
            layer_norm(nc, link, xn, x, stats, small, xn_done)
            ve.wait_ge(qk_done, NC)
            for k in range(PARTS):
                link(nc.vector.tensor_copy(part[:, k, :], qk[:]))
                if k < PARTS - 1:
                    link(nc.vector.tensor_tensor(qk[:], qk[:], part[:, k, :], ALU.subtract))
            nc.vector.memset(mx[:], 0.0).then_inc(split, 1)
            ve.wait_ge(ld_c, LOADS)
            for c in range(NT // 4):
                ve.wait_ge(v_ps, NT)
                nc.vector.tensor_tensor(vall[:, 4 * c:4 * c + 4].rearrange("p i h k -> p i (h k)"),
                                        ps[c // 2][:, LAT * 4 * (c % 2):LAT * 4 * (c % 2) + LAT * 4].rearrange("p (i e) -> p i e", i=4),
                                        vb[:].rearrange("p (o e) -> p o e", o=1).broadcast_to([P, 4, LAT]),
                                        ALU.add).then_inc(v_done, 1)
            NM = 6

            def maxima(n, k):
                ve.wait_ge(k_out, n * 2 + 2)
                for hh in range(HG):
                    nc.vector.tensor_scalar(km[:, k, hh, :], kall[:], col[:, 3 + hh:4 + hh], None, ALU.mult).then_inc(km_done, 1)
                for u in range(UNITS):
                    for h in range(2):
                        ve.wait_ge(s_ps, n * (2 * UNITS) + (2 * u + h + 1))
                        nc.vector.tensor_reduce(mx[:, h, u // HG, u % HG:u % HG + 1], ps[h][:], AX, ALU.max).then_inc(s_max, 1)
                ve.wait_ge(s_max, (n + 1) * (2 * UNITS))
                mlink = Chain(ve, mdve, n * NM)
                mlink(nc.vector.tensor_tensor(mtop[:, 0], mx[:, 0], mx[:, 1], ALU.max))
                mlink(nc.vector.tensor_scalar(mtop[:, 0], mtop[:, 0], -1.0, None, ALU.mult))
                for p in range(PARTS):
                    at = mrow[:, :, :, MAX_ROW + p]
                    if p < PARTS - 1:
                        mlink(nc.vector.tensor_copy(at, mtop[:, 0]))
                        mlink(nc.vector.tensor_tensor(mtop[:, 0], mtop[:, 0], at, ALU.subtract))
                    else:
                        nc.vector.tensor_copy(at, mtop[:, 0]).then_inc(m_done, 1)
                assert mlink.n == NM

            def outputs(n):
                ve.wait_ge(ot_ps, n + 1)
                for h in range(2):
                    o = ps[h][:].rearrange("p (s q c) -> p s q c", s=4, q=HG)
                    ins = nc.vector.reciprocal(rs[:, 4 * h:4 * h + 4, :], o[:, :, :, KPH])
                ins.then_inc(rs_done, 1)
                ve.wait_ge(rs_done, n + 1)
                for h in range(2):
                    o = ps[h][:].rearrange("p (s q c) -> p s q c", s=4, q=HG)
                    for q in range(HG):
                        dst = aov[:, bass.ds(n // NHG, 1), bass.ds(n % NHG, 1), 4 * h:4 * h + 4, KPH * q:KPH * q + KPH]
                        ins = nc.vector.tensor_tensor(dst.rearrange("p a c s k -> p (a c s) k"), o[:, :, q, 0:KPH],
                                                      rs[:, 4 * h:4 * h + 4, q:q + 1].broadcast_to([P, 4, KPH]), ALU.mult)
                ins.then_inc(ao_done, 1)

            maxima(0, 0)
            with nc.vector.Fori(0, GROUPS // 2 - 1) as f:
                for k in range(2):
                    maxima(f * 2 + (k + 1), 1 - k)
                    outputs(f * 2 + k)
            maxima(GROUPS - 1, 1)
            outputs(GROUPS - 2)
            outputs(GROUPS - 1)


def gelu_experts(nc, own, a, m, g, ps, mla):
    sb, sem = scoped(nc, own)
    x, ident = m["x"], m["ident"]
    wt = sb("e_wt", [P, 2, 4, D])
    b1 = sb("e_b1", [P, 2 * E1])
    b1e = sb("e_b1e", [P, 2, 2])
    b2 = sb("e_b2", [E1, D])
    rw = sb("e_rw", [P, E1])
    rb = sb("e_rb", [P, E1])
    low = sb("e_low", [P, E1, E1])
    rank = sb("e_rank", [P, 2, NT, E1 * E1])
    rk = sb("e_rk", [P, NT, E1])
    pr = sb("e_pr", [P, NT, E1])
    tot = sb("e_tot", [P, NT])
    combT = sb("e_combT", [E1, B * T])
    act_ = sb("e_act", [P, 2, 2, CH])
    ld_c, ld_w = sem("e_ld_c"), [sem("e_ld_w0"), sem("e_ld_w1")]
    b_cur = sem("e_b_cur")
    dve, logit, arg, ex_done, comb_done = (sem("e_" + n) for n in ("dve", "logit", "arg", "ex", "comb"))
    cT_ps, cT_done, b_ps, h_ps, act_done, y_ps, acc_done = (sem("e_" + n) for n in
                                                           ("cT_ps", "cT", "b_ps", "h", "act", "y", "acc"))

    with nc.Block() as block:
        @block.sync
        def _(sp):
            w = a["moe1"].rearrange("(f k) r c -> k f r c", k=2)
            for k in range(2):
                sp.dma_start(wt[:, k].rearrange("p m c -> p (m c)"), w[k, 0]).then_inc(ld_w[k], 16)
            for dst, src in ((rw[:], a["router1"]), (b1[:], a["b1T"]), (b2[:], a["b2"]),
                             (rb[:], a["rb1"].rearrange("(o e) -> o e", o=1).broadcast_to([P, E1])),
                             (low[:].rearrange("p i j -> p (i j)"),
                              a["low_1"].rearrange("(o e) -> o e", o=1).broadcast_to([P, E1 * E1]))):
                sp.dma_start(dst, src).then_inc(ld_c, 16)
            with nc.sync.Fori(1, E1 // 2) as f:
                for k in range(2):
                    sp.wait_ge(y_ps, f * (2 * NC) + ((k - 1) * NC + 2))
                    sp.dma_start(wt[:, k].rearrange("p m c -> p (m c)"),
                                 w[k, bass.ds(f, 1)].rearrange("o r c -> r (o c)")).then_inc(ld_w[k], 16)

        @block.scalar
        def _(act):
            act.wait_ge(arg, 1)
            nc.scalar.activation(pr[:].rearrange("p i e -> p (i e)"), pr[:].rearrange("p i e -> p (i e)"),
                                 ACT.Exp).then_inc(ex_done, 1)
            for c in range(NC):
                act.wait_ge(cT_ps, 4 * c + 4)
                nc.scalar.copy(combT[:, CH * c:CH * c + CH], ps[4 + c % 2][0:E1, :]).then_inc(cT_done, 1)
            nc.scalar.preload_act_table(ACT.Gelu)
            with nc.scalar.Fori(0, E1 // 2) as f:
              for k in range(2):
                e = f * 2 + k
                nc.scalar.copy(b1e[:, k], b1[:, bass.ds(e * 2, 2)]).then_inc(b_cur, 1)
                act.wait_ge(b_cur, e + 1)
                for c in range(NC):
                    act.wait_ge(y_ps, e * NC + (c + 1))
                    for h in range(2):
                        act.wait_ge(h_ps, e * (2 * NC) + (2 * c + h + 1))
                        nc.scalar.activation(act_[:, c % 2, h, :], ps[2 * (c % 2) + h][:], ACT.Gelu,
                                             bias=b1e[:, k, h:h + 1]).then_inc(act_done, 1)

        @block.tensor
        def _(pe):
            pe.wait_ge(ld_c, 80)
            for i in range(NT):
                mm = nc.tensor.matmul(ps[6][:, E1 * i:E1 * i + E1], mla[:, P * i:P * i + P], rw[:], start=True, stop=True)
            mm.then_inc(logit, 1)
            pe.wait_ge(comb_done, 1)
            for i in range(NT):
                c = i // 4
                if i % 4 == 0 and c >= 2:
                    pe.wait_ge(cT_done, c - 1)
                nc.tensor.transpose(ps[4 + c % 2][0:E1, P * (i % 4):P * (i % 4) + P], pr[:, i, :], ident[:]).then_inc(cT_ps, 1)
            pe.wait_ge(cT_done, NC)
            for i in range(NT):
                c = i // 4
                mm = nc.tensor.matmul(ps[c][:, P * (i % 4):P * (i % 4) + P], combT[:, P * i:P * i + P], b2[:],
                                      start=True, stop=True)
            mm.then_inc(b_ps, 1)
            pe.wait_ge(acc_done, 2)

            def up(k, e, c):
                if k or c >= 2:
                    pe.wait_ge(act_done, e * (2 * NC) + 2 * (c - 1))
                for h in range(2):
                    nc.tensor.matmul(ps[2 * (c % 2) + h][:], wt[:, k, h, :], mla[:, CH * c:CH * c + CH],
                                     start=True, stop=True).then_inc(h_ps, 1)

            def down(k, e, c):
                pe.wait_ge(act_done, e * (2 * NC) + (2 * c + 2))
                pe.wait_ge(acc_done, e * NC + (c + 1))
                for i in range(4):
                    for h in range(2):
                        mm = nc.tensor.matmul(ps[4 + c % 2][:, P * i:P * i + P], act_[:, c % 2, h, P * i:P * i + P],
                                              wt[:, k, 2 + h, :], start=(h == 0), stop=(h == 1))
                mm.then_inc(y_ps, 1)

            with nc.tensor.Fori(0, E1 // 2) as f:
                for k in range(2):
                    e = f * 2 + k
                    pe.wait_ge(ld_w[k], f * 16 + 16)
                    up(k, e, 0)
                    up(k, e, 1)
                    down(k, e, 0)
                    up(k, e, 2)
                    down(k, e, 1)
                    up(k, e, 3)
                    down(k, e, 2)
                    down(k, e, 3)

        @block.vector
        def _(ve):
            link = Chain(ve, dve)
            flat = lambda t: t.rearrange("p i e -> p (i e)")
            nc.vector.memset(rk[:], 0.0).then_inc(y_ps, 2)
            wide = lambda t, n: t.rearrange("p (i o) -> p i o", o=1).broadcast_to([P, NT, n])
            ve.wait_ge(ld_c, 80)
            ve.wait_ge(logit, 1)
            link(nc.vector.tensor_tensor(pr[:], ps[6][:, 0:NT * E1].rearrange("p (i e) -> p i e", e=E1),
                                         rb[:].rearrange("p (o e) -> p o e", o=1).broadcast_to([P, NT, E1]), ALU.add))
            link(nc.vector.tensor_reduce(tot[:], pr[:], AX, ALU.max))
            nc.vector.tensor_tensor(pr[:], pr[:], wide(tot[:], E1), ALU.subtract).then_inc(arg, 1)
            ve.wait_ge(ex_done, 1)
            link(nc.vector.tensor_reduce(tot[:], pr[:], AX, ALU.add))
            link(nc.vector.reciprocal(tot[:], tot[:]))
            link(nc.vector.tensor_tensor(pr[:], pr[:], wide(tot[:], E1), ALU.mult))
            ranks(nc, link, rk[:], pr[:], rank, low, E1)
            link(nc.vector.tensor_scalar(flat(rk[:]), flat(rk[:]), float(TOPK), None, ALU.is_lt))
            link(nc.vector.tensor_tensor(pr[:], pr[:], rk[:], ALU.mult))
            link(nc.vector.tensor_reduce(tot[:], pr[:], AX, ALU.add))
            link(nc.vector.tensor_scalar(tot[:], tot[:], 1e-8, None, ALU.add))
            link(nc.vector.reciprocal(tot[:], tot[:]))
            link(nc.vector.tensor_scalar(tot[:], tot[:], 0.3, None, ALU.mult))
            nc.vector.tensor_tensor(pr[:], pr[:], wide(tot[:], E1), ALU.mult).then_inc(comb_done, 1)
            ve.wait_ge(b_ps, 1)
            for c in range(NC):
                xs = x[:, 4 * c:4 * c + 4, :].rearrange("p i d -> p (i d)")
                ins = nc.vector.tensor_tensor(xs, xs, ps[c][:], ALU.add)
            ins.then_inc(acc_done, 2)
            ve.wait_ge(acc_done, 2)
            with nc.vector.Fori(0, E1) as e:
                for c in range(NC):
                    ve.wait_ge(y_ps, e * NC + (c + 3))
                    for i in range(4 * c, 4 * c + 4):
                        ins = nc.vector.scalar_tensor_tensor(out=x[:, i, :], in0=ps[4 + c % 2][:, P * (i % 4):P * (i % 4) + P],
                                                             scalar=pr[:, i, bass.ds(e, 1)], in1=x[:, i, :],
                                                             op0=ALU.mult, op1=ALU.add)
                    ins.then_inc(acc_done, 1)


_STAGE = 4


def kernel(**inputs):
    import numpy as np
    import concourse.bacc as bacc
    from concourse import mybir as mb
    from concourse.bass_utils import run_bass_kernel_spmd

    i = {k: np.asarray(v) for k, v in inputs.items()}
    arrays = {
        "x": i["L0_attn_x"],
        "WqT": i["L0_attn_Wq"].T, "WkT": i["L0_attn_Wk"].T, "WvT": i["L0_attn_Wv"].T, "WoT": i["L0_attn_Wo"].T,
        "W_gamma": i["L0_attn_W_gamma"], "b_gamma": i["L0_attn_b_gamma"],
        "W_lambda": i["L0_attn_W_lambda"], "b_lambda": i["L0_attn_b_lambda"],
        "ident": np.eye(128, dtype=np.float32),
        "AT": i["L1_attn_A"].T, "BT": i["L1_attn_B"].T, "CT": i["L1_attn_C"].T,
        "gamma": i["L1_attn_gamma"], "beta": i["L1_attn_beta"],
        "wqk": np.concatenate([i["L1_ffn_q_w"].reshape(128, 16, 8)[:, :, :4].reshape(128, 64), i["L1_ffn_k_w"]], axis=1),
        "bqk": np.concatenate([i["L1_ffn_q_b"].reshape(16, 8)[:, :4].reshape(64), i["L1_ffn_k_b"]]),
        "wv1": i["L1_ffn_v_w"], "vb1": i["L1_ffn_v_b"], "wo1": i["L1_ffn_o_w"][:LAT], "ob1": i["L1_ffn_o_b"],
        "sel": selections().astype(mb.dt.np(mb.dt.bfloat16)), "identb": np.eye(128).astype(mb.dt.np(mb.dt.bfloat16)),
        "rows": np.stack([np.tile(np.isin(np.arange(32), MAX_ROW + np.arange(PARTS)), HG)]
                         + [np.arange(P) // 32 == h for h in range(HG)], axis=1).astype(np.float32),
        "moe1": np.concatenate([i["L1_ffn_w1"], i["L1_ffn_w2"].reshape(8, 2, 128, 128).transpose(0, 2, 1, 3).reshape(8, 128, 256)], axis=2),
        "b1T": i["L1_ffn_b1"].reshape(16, 128).T, "b2": i["L1_ffn_b2"],
        "router1": i["L1_ffn_router_w"], "rb1": i["L1_ffn_router_b"],
        "low_1": np.tri(8, k=-1, dtype=np.float32).reshape(-1),
        "router0": i["L0_ffn_router_w"].T, "bias0": i["L0_ffn_bias"],
        "low_e": np.tri(16, k=-1, dtype=np.float32).reshape(-1), "low_g": np.tri(4, k=-1, dtype=np.float32).reshape(-1),
        "moe0": np.concatenate([
            np.concatenate([i["L0_ffn_gate_w"], i["L0_ffn_sh_gate_w"].reshape(128, 2, 128).transpose(1, 0, 2)]),
            np.concatenate([i["L0_ffn_up_w"], i["L0_ffn_sh_up_w"].reshape(128, 2, 128).transpose(1, 0, 2)]),
            np.concatenate([i["L0_ffn_down_w"], i["L0_ffn_sh_down_w"].reshape(2, 128, 128)])], axis=2),
    }
    arrays = {k: np.ascontiguousarray(v) for k, v in arrays.items()}
    nc = bacc.Bacc("TRN2", target_bir_lowering=False, num_devices=1)
    a = {k: nc.dram_tensor(f"in_{k}", v.shape, mb.dt.from_np(v.dtype), kind="ExternalInput").ap()
         for k, v in arrays.items()}
    out = nc.dram_tensor("out_0_dram", (2, 1024, 128), mb.dt.float32, kind="ExternalOutput").ap()
    build(nc, a, out, _STAGE)
    r = run_bass_kernel_spmd(nc, [{f"in_{k}": v for k, v in arrays.items()}], core_ids=[0])
    return r.results[0]["out_0_dram"]
```

```python
from contextlib import ExitStack

import concourse.bass as bass
from concourse import mybir

F32 = mybir.dt.float32
I32 = mybir.dt.int32
F16 = mybir.dt.float16
BF16 = mybir.dt.bfloat16
ALU = mybir.AluOpType
ACT = mybir.ActivationFunctionType
AX = mybir.AxisListType.X

B, T, D = 2, 1024, 128
P = 128
NT = B * T // P
TB = T // P
CH = 512
NC = B * T // CH
H1, DK = 16, 8
E0, NG, TKG, K0, NSH = 16, 4, 2, 4, 2
W0 = E0 + NSH
H3, KPH = 16, 4
LAT = H3 * KPH
E1, TOPK = 8, 2
HG = 4
NHG = H3 // HG
LN_EPS = 1e-5
ZSCALE = 64.0
RSQRT_SEED = float(0x5F3759DF)


class Chain:

    def __init__(self, eng, sem, base=0):
        self.eng, self.sem, self.base, self.n = eng, sem, base, 0

    def __call__(self, ins):
        self.n += 1
        ins.then_inc(self.sem, 1)
        self.eng.wait_ge(self.sem, self.base + self.n)
        return ins


def rsqrt(nc, link, y, x, t):
    link(nc.vector.tensor_scalar(y.bitcast(I32), x.bitcast(I32), 1, None, ALU.logical_shift_right))
    link(nc.vector.tensor_scalar(y.bitcast(I32), y.bitcast(I32), -1.0, RSQRT_SEED, ALU.mult, ALU.add))
    for _ in range(3):
        link(nc.vector.tensor_tensor(t, y, y, ALU.mult))
        link(nc.vector.scalar_tensor_tensor(out=t, in0=x, scalar=-0.5, in1=t, op0=ALU.mult, op1=ALU.mult))
        link(nc.vector.scalar_tensor_tensor(out=y, in0=t, scalar=1.5, in1=y, op0=ALU.add, op1=ALU.mult))


def ln_moments(nc, link, stats, small):
    mean, rstd, dif, cv = (small[:, k, :] for k in range(4))
    nc.vector.tensor_tensor(dif, stats[:, :, 1], stats[:, :, 4], ALU.subtract)
    nc.vector.tensor_tensor(mean, stats[:, :, 1], stats[:, :, 4], ALU.add)
    link(nc.vector.tensor_tensor(cv, stats[:, :, 2], stats[:, :, 5], ALU.add))
    nc.vector.tensor_scalar(mean, mean, 0.5, None, ALU.mult)
    nc.vector.tensor_scalar(cv, cv, 1.0 / D, LN_EPS, ALU.mult, ALU.add)
    link(nc.vector.tensor_tensor(dif, dif, dif, ALU.mult))
    link(nc.vector.scalar_tensor_tensor(out=cv, in0=dif, scalar=0.25, in1=cv, op0=ALU.mult, op1=ALU.add))
    rsqrt(nc, link, rstd, cv, dif)


def layer_norm(nc, link, dst, src, stats, small, done, n=NT):
    for i in range(n):
        ins = nc.vector.bn_stats(stats[:, i, :], src[:, i, :])
    link(ins)
    ln_moments(nc, link, stats, small)
    for i in range(n):
        nc.vector.tensor_scalar(dst[:, i, :], src[:, i, :], small[:, 0, i:i + 1], small[:, 1, i:i + 1],
                                ALU.subtract, ALU.mult).then_inc(done, 1)


def build(nc, a, out, stage):
    ctx = ExitStack()
    with ctx:
        def sb(name, shape, dt=F32):
            return ctx.enter_context(nc.sbuf_tensor(name, shape, dt))

        def sem(name):
            return ctx.enter_context(nc.semaphore(name))

        banks = ctx.enter_context(nc.psum_tensor("banks", [P, 8, 512], F32))
        ps = [banks[:, i, :] for i in range(8)]
        m = {
            "x": sb("x", [P, NT, D]), "xn": sb("xn", [P, NT, D]), "xT": sb("xT", [P, B * T]),
            "stats": sb("stats", [P, NT, 6]), "small": sb("small", [P, 4, NT]),
            "ident": sb("ident", [P, P]), "banks": banks,
        }
        g = {"ld_x": [sem(f"ld_x{i}") for i in range(NC)], "ld_id": sem("ld_id")}
        with ExitStack() as own:
            gated_recurrence(nc, own, a, m, g, ps)
        if stage >= 2:
            with ExitStack() as own:
                grouped_experts(nc, own, a, m, g, ps)
        if stage >= 3:
            with ExitStack() as own:
                gelu_recurrence(nc, own, a, m, g, ps)
        if stage >= 4:
            with ExitStack() as own:
                attention_experts(nc, own, a, m, g, ps)
        stored = sem("stored")
        with nc.Block() as block:
            @block.sync
            def _(sp):
                o = out.rearrange("b (i p) d -> p (b i) d", p=P)
                for c in range(NC):
                    sp.dma_start(o[:, 4 * c:4 * c + 4, :], m["x"][:, 4 * c:4 * c + 4, :]).then_inc(stored, 16)
                sp.wait_ge(stored, 16 * NC)


def scoped(nc, own):
    def sb(name, shape, dt=F32):
        return own.enter_context(nc.sbuf_tensor(name, shape, dt))

    def sem(name):
        return own.enter_context(nc.semaphore(name))

    return sb, sem


def gated_recurrence(nc, own, a, m, g, ps):
    sb, sem = scoped(nc, own)
    x, xn, xT, stats, small, ident = (m[k] for k in ("x", "xn", "xT", "stats", "small", "ident"))
    wT = sb("wT", [P, 3, D])
    wk_rep = sb("wk_rep", [P, DK, P])
    wo_rep = sb("wo_rep", [P, DK, D])
    par = sb("par", [P, 4, H1])
    qT = sb("qT", [P, B * T])
    vT = sb("vT", [P, B * T])
    rhoE = sb("rhoE", [P, B * T])
    uT = sb("uT", [P, B * T])
    ksq = sb("ksq", [P, NT, D])
    s1 = sb("s1", [P, NT, H1])
    s2 = sb("s2", [P, NT, H1])
    gat = sb("gat", [P, 4, NT, H1])
    rho_x, g_x = ksq, xn
    w = sb("w", [P, 2, T])
    S = sb("S", [P, 2, T])
    qS = sb("qS", [P, 2, T])
    ld_w, ld_p, ld_o = sem("a_ld_w"), sem("a_ld_p"), sem("a_ld_o")
    dve, xn_done, xT_ps, xT_done = sem("a_dve"), sem("a_xn"), sem("a_xT_ps"), sem("a_xT")
    rep, proj, proj_out, kt_ps, ksq_done, s_done = (sem("a_" + n) for n in
                                                     ("rep", "proj", "proj_out", "kt", "ksq", "s"))
    z_done, th_done, gate_done, exp_ps, rho_out, u_done = (sem("a_" + n) for n in
                                                          ("z", "th", "gate", "exp", "rho", "u"))
    rho_spread, g_spread = sem("a_rho_spread"), sem("a_g_spread")
    k_ps, w_done, S_done, qS_done, o_ps = (sem("a_" + n) for n in ("kps", "w", "S", "qS", "o"))

    def spread(gate):
        return gate.rearrange("p i (h o) -> p (i h) o", o=1).broadcast_to([P, NT * H1, DK])

    with nc.Block() as block:
        @block.sync
        def _(sp):
            xin = a["x"].rearrange("b (i p) d -> p (b i) d", p=P)
            for c in range(NC):
                sp.dma_start(x[:, 4 * c:4 * c + 4, :], xin[:, 4 * c:4 * c + 4, :]).then_inc(g["ld_x"][c], 16)
            for k, name in enumerate(("W_gamma", "b_gamma", "W_lambda", "b_lambda")):
                src = a[name].rearrange("(o h) -> o h", o=1)
                sp.dma_start(par[:, k, :], src.broadcast_to([P, H1])).then_inc(ld_p, 16)

        @block.scalar
        def _(act):
            act.dma_start(ident[:], a["ident"]).then_inc(g["ld_id"], 16)
            for k, name in enumerate(("WkT", "WqT", "WvT")):
                act.dma_start(wT[:, (1, 0, 2)[k], :], a[name]).then_inc(ld_w, 16)
            wo = a["WoT"].rearrange("(h j) e -> h j e", j=DK)
            for v in range(DK):
                act.dma_start(wo_rep[v:P:DK, :, :], wo).then_inc(ld_o, 16)
            for c in range(NC):
                act.wait_ge(xT_ps, 4 * c + 4)
                nc.scalar.copy(xT[:, CH * c:CH * c + CH], ps[c][:]).then_inc(xT_done, 1)
            for c in range(NC):
                act.wait_ge(kt_ps, 4 * c + 4)
                nc.scalar.activation(ksq[:, 4 * c:4 * c + 4, :].rearrange("p i d -> p (i d)"), ps[c][:],
                                     ACT.Square).then_inc(ksq_done, 1)
            for c in range(NC):
                for k, dst in enumerate((qT, vT)):
                    act.wait_ge(proj, 2 * c + k + 1)
                    nc.scalar.copy(dst[:, CH * c:CH * c + CH], ps[4 + (2 * c + k) % 4][:]).then_inc(proj_out, 1)
            act.wait_ge(z_done, 1)
            nc.scalar.activation(gat[:, 0:2].rearrange("p k i h -> p (k i h)"),
                                 gat[:, 0:2].rearrange("p k i h -> p (k i h)"), ACT.Tanh, scale=0.5).then_inc(th_done, 1)
            act.wait_ge(gate_done, 1)
            nc.scalar.copy(rho_x[:].rearrange("p i (h v) -> p (i h) v", v=DK), spread(gat[:, 2])).then_inc(rho_spread, 1)
            for c in range(NC):
                act.wait_ge(exp_ps, 2 * c + 1)
                nc.scalar.copy(rhoE[:, CH * c:CH * c + CH], ps[2 * (c % 2)][:]).then_inc(rho_out, 1)

        @block.gpsimd
        def _(pool):
            pool.wait_ge(ld_w, 48)
            for j in range(DK):
                src = wT[:, 1, j::DK].rearrange("p (h o) -> p h o", o=1).broadcast_to([P, H1, DK])
                nc.gpsimd.tensor_copy(wk_rep[:, j, :].rearrange("p (h v) -> p h v", v=DK), src).then_inc(rep, 1)
            for b in range(B):
                for j in range(DK):
                    n = DK * b + j
                    pool.wait_ge(S_done, n + 1)
                    if n >= 2:
                        pool.wait_ge(o_ps, n - 1)
                    if n == 0:
                        pool.wait_ge(proj_out, 2 * NC)
                    nc.gpsimd.tensor_tensor(qS[:, n % 2, :], S[:, n % 2, :], qT[:, T * b:T * b + T],
                                            ALU.mult).then_inc(qS_done, 1)

        @block.tensor
        def _(pe):
            pe.wait_ge(g["ld_id"], 16)
            for i in range(NT):
                pe.wait_ge(xn_done, i + 1)
                nc.tensor.transpose(ps[i // 4][:, P * (i % 4):P * (i % 4) + P], xn[:, i, :], ident[:]).then_inc(xT_ps, 1)
            pe.wait_ge(ld_w, 48)
            pe.wait_ge(xT_done, NC)
            for i in range(NT):
                nc.tensor.matmul(ps[i // 4][:, P * (i % 4):P * (i % 4) + P], xT[:, P * i:P * i + P], wT[:, 1, :],
                                 start=True, stop=True).then_inc(kt_ps, 1)
            for c in range(NC):
                for k in range(2):
                    n = 2 * c + k
                    if n >= 4:
                        pe.wait_ge(proj_out, n - 3)
                    nc.tensor.matmul(ps[4 + n % 4][:], wT[:, 2 * k, :], xT[:, CH * c:CH * c + CH],
                                     start=True, stop=True).then_inc(proj, 1)
            pe.wait_ge(s_done, NC)
            for c in range(NC):
                if c >= 2:
                    pe.wait_ge(rho_out, c - 1)
                    pe.wait_ge(u_done, c - 1)
                if c == 0:
                    pe.wait_ge(rho_spread, 1)
                    pe.wait_ge(g_spread, 1)
                for k in range(2):
                    for i in range(4):
                        mm = nc.tensor.transpose(ps[2 * (c % 2) + k][:, P * i:P * i + P],
                                                 (rho_x, g_x)[k][:, 4 * c + i, :], ident[:])
                    mm.then_inc(exp_ps, 1)
            pe.wait_ge(rep, DK)
            pe.wait_ge(ld_o, 16 * DK)
            pe.wait_ge(proj_out, 2 * NC)
            pe.wait_ge(u_done, NC)
            pe.wait_ge(rho_out, NC)

            def key_column(n):
                if n >= 2:
                    pe.wait_ge(w_done, n - 1)
                for h in range(2):
                    c = T * (n // DK) + CH * h
                    mm = nc.tensor.matmul(ps[2 * (n % 2) + h][:], wk_rep[:, n % DK, :], xT[:, c:c + CH],
                                          start=True, stop=True)
                mm.then_inc(k_ps, 1)

            key_column(0)
            for n in range(B * DK):
                if n + 1 < B * DK:
                    key_column(n + 1)
                pe.wait_ge(qS_done, n + 1)
                b, j = n // DK, n % DK
                for i in range(TB):
                    mm = nc.tensor.matmul(ps[4 + 2 * b + i // 4][:, P * (i % 4):P * (i % 4) + P],
                                          qS[:, n % 2, P * i:P * i + P], wo_rep[:, j, :],
                                          start=(j == 0 and i % 4 == 0), stop=(j == DK - 1), skip_group_check=True)
                mm.then_inc(o_ps, 1)

        @block.vector
        def _(ve):
            link = Chain(ve, dve)
            for c in range(NC):
                ve.wait_ge(g["ld_x"][c], 16)
            layer_norm(nc, link, xn, x, stats, small, xn_done)
            for c in range(NC):
                ve.wait_ge(ksq_done, c + 1)
                nc.vector.tensor_reduce(s1[:, 4 * c:4 * c + 4, :], ps[c][:].rearrange("p (i h j) -> p i h j", i=4, j=DK),
                                        AX, ALU.add)
                nc.vector.tensor_reduce(s2[:, 4 * c:4 * c + 4, :],
                                        ksq[:, 4 * c:4 * c + 4, :].rearrange("p i (h j) -> p i h j", j=DK),
                                        AX, ALU.add).then_inc(s_done, 1)
            ve.wait_ge(s_done, NC)
            flat = lambda t: t.rearrange("p i h -> p (i h)")
            g0, g1, g2, g3 = (flat(gat[:, k]) for k in range(4))
            link(nc.vector.tensor_scalar(flat(s2[:]), flat(s2[:]), 1e-24, None, ALU.max))
            rsqrt(nc, link, g2, flat(s2[:]), g3)
            link(nc.vector.scalar_tensor_tensor(out=flat(s1[:]), in0=flat(s1[:]), scalar=1.0 / DK, in1=g2,
                                                op0=ALU.mult, op1=ALU.mult))
            ve.wait_ge(ld_p, 64)
            bc = lambda k: par[:, k, :].rearrange("p (o h) -> p o h", o=1).broadcast_to([P, NT, H1])
            for k in range(2):
                link(nc.vector.tensor_tensor(gat[:, k], s1[:], bc(2 * k), ALU.mult))
                ins = nc.vector.tensor_tensor(gat[:, k], gat[:, k], bc(2 * k + 1), ALU.add)
                if k == 0:
                    link(ins)
            ins.then_inc(z_done, 1)
            ve.wait_ge(th_done, 1)
            link(nc.vector.tensor_scalar(g1, g1, -0.25, 0.25, ALU.mult, ALU.add))
            link(nc.vector.scalar_tensor_tensor(out=g0, in0=g0, scalar=1.0, in1=g1, op0=ALU.add, op1=ALU.mult))
            link(nc.vector.tensor_scalar(g3, g0, -1.0, 1.0, ALU.mult, ALU.add))
            link(nc.vector.tensor_tensor(g3, g3, g2, ALU.mult))
            nc.vector.tensor_copy(g2, g0).then_inc(gate_done, 1)
            nc.vector.tensor_copy(g_x[:].rearrange("p i (h v) -> p (i h) v", v=DK), spread(gat[:, 3])).then_inc(g_spread, 1)
            ve.wait_ge(proj_out, 2 * NC)
            for c in range(NC):
                ve.wait_ge(exp_ps, 2 * c + 2)
                cols = slice(CH * c, CH * c + CH)
                nc.vector.tensor_tensor(uT[:, cols], vT[:, cols], ps[2 * (c % 2) + 1][:], ALU.mult).then_inc(u_done, 1)
            ve.wait_ge(u_done, NC)
            ve.wait_ge(rho_out, NC)
            for n in range(B * DK):
                b = n // DK
                ve.wait_ge(k_ps, n + 1)
                for h in range(2):
                    ins = nc.vector.tensor_tensor(w[:, n % 2, CH * h:CH * h + CH],
                                                  uT[:, T * b + CH * h:T * b + CH * h + CH],
                                                  ps[2 * (n % 2) + h][:], ALU.mult)
                ins.then_inc(w_done, 1)
                ve.wait_ge(w_done, n + 1)
                if n >= 2:
                    ve.wait_ge(qS_done, n - 1)
                nc.vector.tensor_tensor_scan(S[:, n % 2, :], rhoE[:, T * b:T * b + T], w[:, n % 2, :], 0.0,
                                             ALU.mult, ALU.add).then_inc(S_done, 1)
            for b in range(B):
                ve.wait_ge(o_ps, DK * (b + 1))
                for h in range(2):
                    i = TB * b + 4 * h
                    xs = x[:, i:i + 4, :].rearrange("p i d -> p (i d)")
                    nc.vector.tensor_tensor(xs, xs, ps[4 + 2 * b + h][:], ALU.add)


def turn_tiles(nc, eng, ps, src, ident, ready, turned, first=0):
    for i in range(first, first + NT):
        eng.wait_ge(ready, i + 1)
        nc.tensor.transpose(ps[i // 4][:, P * (i % 4):P * (i % 4) + P], src[:, i, :], ident[:]).then_inc(turned, 1)


def grouped_experts(nc, own, a, m, g, ps):
    sb, sem = scoped(nc, own)
    x, xn, xT, stats, small, ident = (m[k] for k in ("x", "xn", "xT", "stats", "small", "ident"))
    wt = sb("b_wt", [P, 2, 3, D])
    rw = sb("b_rw", [P, E0])
    bias = sb("b_bias", [P, E0])
    low_e = sb("b_low_e", [P, E0, E0])
    low_g = sb("b_low_g", [P, NG, NG])
    sc = sb("b_sc", [P, NT, E0])
    s = sb("b_s", [P, NT, E0])
    gs = sb("b_gs", [P, 6, NT, NG])
    rank = sb("b_rank", [P, 2, NT, E0 * E0])
    rk = sb("b_rk", [P, NT, E0])
    tot = sb("b_tot", [P, NT])
    comb = sb("b_comb", [P, NT, W0])
    th = sb("b_th", [P, 2, CH])
    act_ = sb("b_act", [P, 4, CH])
    ld_c, ld_w = sem("b_ld_c"), [sem("b_ld_w0"), sem("b_ld_w1")]
    dve, xn_done, xT_ps, xT_done = sem("b_dve"), sem("b_xn"), sem("b_xT_ps"), sem("b_xT")
    logit, esig = sem("b_logit"), sem("b_esig")
    h_ps, u_ps, th_done, hu_done, h_free, y_ps, acc_done = (sem("b_" + n) for n in
                                                          ("h", "u", "th", "hu", "hfree", "y", "acc"))
    gtmp = sem("b_gtmp")

    with nc.Block() as block:
        @block.sync
        def _(sp):
            sp.dma_start(rw[:], a["router0"]).then_inc(ld_c, 16)
            sp.dma_start(bias[:], a["bias0"].rearrange("(o e) -> o e", o=1).broadcast_to([P, E0])).then_inc(ld_c, 16)
            sp.dma_start(low_e[:].rearrange("p i j -> p (i j)"),
                         a["low_e"].rearrange("(o e) -> o e", o=1).broadcast_to([P, E0 * E0])).then_inc(ld_c, 16)
            sp.dma_start(low_g[:].rearrange("p i j -> p (i j)"),
                         a["low_g"].rearrange("(o e) -> o e", o=1).broadcast_to([P, NG * NG])).then_inc(ld_c, 16)
            w = a["moe0"].rearrange("(f k) r c -> k f r c", k=2)
            for k in range(2):
                sp.dma_start(wt[:, k].rearrange("p m c -> p (m c)"), w[k, 0]).then_inc(ld_w[k], 16)
            with nc.sync.Fori(1, W0 // 2) as f:
                for k in range(2):
                    sp.wait_ge(y_ps, f * (2 * NC) + (k - 1) * NC)
                    sp.dma_start(wt[:, k].rearrange("p m c -> p (m c)"),
                                 w[k, bass.ds(f, 1)].rearrange("o r c -> r (o c)")).then_inc(ld_w[k], 16)

        @block.scalar
        def _(act):
            for c in range(NC):
                act.wait_ge(xT_ps, 4 * c + 4)
                nc.scalar.copy(xT[:, CH * c:CH * c + CH], ps[c][:]).then_inc(xT_done, 1)
            act.wait_ge(logit, 1)
            nc.scalar.activation(sc[:].rearrange("p i e -> p (i e)"), ps[4][:, 0:NT * E0], ACT.Exp,
                                 scale=-1.0).then_inc(esig, 1)
            nc.scalar.preload_act_table(ACT.Tanh)
            with nc.scalar.Fori(0, W0) as e:
                for c in range(NC):
                    act.wait_ge(h_ps, e * NC + (c + 1))
                    act.wait_ge(hu_done, e * NC + (c + 1))
                    nc.scalar.activation(th[:, c % 2, :], ps[c % 2][:], ACT.Tanh, scale=0.5).then_inc(th_done, 1)

        @block.tensor
        def _(pe):
            turn_tiles(nc, pe, ps, xn, ident, xn_done, xT_ps)
            pe.wait_ge(ld_c, 64)
            pe.wait_ge(xT_done, NC)
            for i in range(NT):
                mm = nc.tensor.matmul(ps[4][:, E0 * i:E0 * i + E0], xT[:, P * i:P * i + P], rw[:], start=True, stop=True)
            mm.then_inc(logit, 1)
            pe.wait_ge(esig, 1)

            def up(k, e, c):
                pe.wait_ge(hu_done, e * NC + (c + 1))
                nc.tensor.matmul(ps[c % 2][:], wt[:, k, 0, :], xT[:, CH * c:CH * c + CH], start=True,
                                 stop=True).then_inc(h_ps, 1)
                nc.tensor.matmul(ps[2 + c % 2][:], wt[:, k, 1, :], xT[:, CH * c:CH * c + CH], start=True,
                                 stop=True).then_inc(u_ps, 1)

            def down(k, e, c):
                pe.wait_ge(hu_done, e * NC + (c + 3))
                pe.wait_ge(acc_done, e * NC + (c + 1))
                for i in range(4):
                    mm = nc.tensor.matmul(ps[4 + c % 2][:, P * i:P * i + P], act_[:, c, P * i:P * i + P],
                                          wt[:, k, 2, :], start=True, stop=True)
                mm.then_inc(y_ps, 1)
                return mm

            with nc.tensor.Fori(0, W0 // 2) as f:
                for k in range(2):
                    e = f * 2 + k
                    pe.wait_ge(ld_w[k], f * 16 + 16)
                    up(k, e, 0)
                    up(k, e, 1)
                    down(k, e, 0)
                    up(k, e, 2)
                    down(k, e, 1)
                    up(k, e, 3)
                    down(k, e, 2)
                    down(k, e, 3)

        @block.vector
        def _(ve):
            link = Chain(ve, dve)
            nc.vector.memset(tot[:], 0.0).then_inc(hu_done, 2)
            nc.vector.memset(rk[:], 0.0).then_inc(acc_done, 2)
            layer_norm(nc, link, xn, x, stats, small, xn_done)
            ve.wait_ge(esig, 1)
            flat = lambda t: t.rearrange("p i e -> p (i e)")
            link(nc.vector.tensor_scalar(flat(sc[:]), flat(sc[:]), 1.0, None, ALU.add))
            link(nc.vector.reciprocal(flat(sc[:]), flat(sc[:])))
            link(nc.vector.tensor_tensor(s[:], sc[:], bias[:].rearrange("p (o e) -> p o e", o=1).broadcast_to([P, NT, E0]),
                                         ALU.add))
            mem = [flat(s[:]).rearrange("p (i g q) -> p i g q", i=NT, g=NG)[:, :, :, q] for q in range(4)]
            nc.vector.tensor_tensor(gs[:, 0], mem[0], mem[1], ALU.add)
            nc.vector.tensor_tensor(gs[:, 1], mem[2], mem[3], ALU.add)
            nc.vector.tensor_tensor(gs[:, 2], mem[0], mem[1], ALU.max)
            link(nc.vector.tensor_tensor(gs[:, 3], mem[2], mem[3], ALU.max))
            nc.vector.tensor_tensor(gs[:, 0], gs[:, 0], gs[:, 1], ALU.max)
            link(nc.vector.tensor_tensor(gs[:, 4], gs[:, 2], gs[:, 3], ALU.add))
            link(nc.vector.tensor_tensor(gs[:, 0], gs[:, 0], gs[:, 4], ALU.max))
            ranks(nc, link, gs[:, 5], gs[:, 0], rank, low_g, NG)
            keep = gs[:, 4]
            link(nc.vector.tensor_scalar(flat(keep), flat(gs[:, 5]), float(TKG), None, ALU.is_lt))
            keep_e = keep.rearrange("p i (g o) -> p (i g) o", o=1).broadcast_to([P, NT * NG, E0 // NG])
            s_g = flat(s[:]).rearrange("p (ig q) -> p ig q", q=E0 // NG)
            link(nc.vector.tensor_tensor(s_g, s_g, keep_e, ALU.mult))
            link(nc.vector.tensor_scalar(flat(keep), flat(keep), 1.0, None, ALU.subtract))
            link(nc.vector.tensor_tensor(s_g, s_g, keep_e, ALU.add))
            ranks(nc, link, rk[:], s[:], rank, low_e, E0)
            link(nc.vector.tensor_scalar(flat(rk[:]), flat(rk[:]), float(K0), None, ALU.is_lt))
            link(nc.vector.tensor_tensor(sc[:], sc[:], rk[:], ALU.mult))
            link(nc.vector.tensor_reduce(tot[:], sc[:], AX, ALU.add))
            link(nc.vector.tensor_scalar(tot[:], tot[:], 1e-20, None, ALU.add))
            link(nc.vector.reciprocal(tot[:], tot[:]))
            link(nc.vector.tensor_scalar(tot[:], tot[:], 1.25, None, ALU.mult))
            nc.vector.tensor_tensor(comb[:, :, 0:E0], sc[:],
                                    tot[:].rearrange("p (i o) -> p i o", o=1).broadcast_to([P, NT, E0]), ALU.mult)
            link(nc.vector.memset(comb[:, :, E0:W0], 0.5))

            def silu(e, c):
                ve.wait_ge(th_done, e * NC + (c + 1))
                nc.vector.scalar_tensor_tensor(out=act_[:, c, :], in0=th[:, c % 2, :], scalar=1.0, in1=ps[c % 2][:],
                                               op0=ALU.add, op1=ALU.mult).then_inc(gtmp, 1)
                ve.wait_ge(u_ps, e * NC + (c + 1))
                ve.wait_ge(gtmp, e * NC + (c + 1))
                nc.vector.tensor_tensor(act_[:, c, :], act_[:, c, :], ps[2 + c % 2][:], ALU.mult).then_inc(hu_done, 1)

            def accumulate(e, c):
                ve.wait_ge(y_ps, e * NC + (c + 1))
                for i in range(4 * c, 4 * c + 4):
                    ins = nc.vector.scalar_tensor_tensor(out=x[:, i, :], in0=ps[4 + c % 2][:, P * (i % 4):P * (i % 4) + P],
                                                         scalar=comb[:, i, bass.ds(e, 1)], in1=x[:, i, :],
                                                         op0=ALU.mult, op1=ALU.add)
                ins.then_inc(acc_done, 1)

            with nc.vector.Fori(0, W0) as e:
                silu(e, 0)
                silu(e, 1)
                accumulate(e, 0)
                silu(e, 2)
                accumulate(e, 1)
                silu(e, 3)
                accumulate(e, 2)
                accumulate(e, 3)


def ranks(nc, link, out, val, scratch, low, n):
    gt = scratch[:, 0, :, 0:n * n].rearrange("p t (i j) -> p t i j", j=n)
    eq = scratch[:, 1, :, 0:n * n].rearrange("p t (i j) -> p t i j", j=n)
    other = val.rearrange("p t (o j) -> p t o j", o=1).broadcast_to([P, NT, n, n])
    own = val.rearrange("p t (i o) -> p t i o", o=1).broadcast_to([P, NT, n, n])
    lower = low[:].rearrange("p (o i) j -> p o (i j)", o=1).broadcast_to([P, NT, n * n])
    nc.vector.tensor_tensor(gt, other, own, ALU.is_gt)
    link(nc.vector.tensor_tensor(eq, other, own, ALU.is_equal))
    link(nc.vector.tensor_tensor(scratch[:, 1, :, 0:n * n], scratch[:, 1, :, 0:n * n], lower, ALU.mult))
    link(nc.vector.tensor_tensor(gt, gt, eq, ALU.add))
    link(nc.vector.tensor_reduce(out, gt, AX, ALU.add))


def gelu_recurrence(nc, own, a, m, g, ps):
    sb, sem = scoped(nc, own)
    x, xn, xT, stats, small, ident = (m[k] for k in ("x", "xn", "xT", "stats", "small", "ident"))
    HALF = 32
    RING = 2 * HALF
    wABC = sb("c_w", [P, 3, D])
    A12 = sb("c_A12", [P, 2, D], F16)
    A1f = sb("c_A1f", [P, D])
    gb = sb("c_gb", [P, 2, D])
    h1 = sb("c_h1", [P, RING, B], F16)
    h2 = sb("c_h2", [P, RING, B], F16)
    hf = sb("c_hf", [P, RING, B])
    hall = sb("c_hall", [P, B, T])
    ld_w, dve, xn_done, xT_ps, xT_done = (sem("c_" + n) for n in ("ldw", "dve", "xn", "xT_ps", "xT"))
    zero, split, h1_done, hf_done, h2_done, z_ps, kept = (sem("c_" + n) for n in
                                                         ("zero", "split", "h1", "hf", "h2", "z", "kept"))
    y_ps, nrm, out_done = sem("c_y"), sem("c_nrm"), sem("c_out")
    xs = xT[:].rearrange("p (b t) -> p t b", b=B)

    with nc.Block() as block:
        @block.sync
        def _(sp):
            for k, name in enumerate(("AT", "BT", "CT")):
                sp.dma_start(wABC[:, k, :], a[name]).then_inc(ld_w, 16)
            for k, name in enumerate(("gamma", "beta")):
                sp.dma_start(gb[:, k, :], a[name].rearrange("(o e) -> o e", o=1).broadcast_to([P, D])).then_inc(ld_w, 16)

        @block.scalar
        def _(act):
            for c in range(NC):
                act.wait_ge(xT_ps, 4 * c + 4)
                nc.scalar.copy(xT[:, CH * c:CH * c + CH], ps[c][:]).then_inc(xT_done, 1)
            nc.scalar.preload_act_table(ACT.Gelu)
            with nc.scalar.Fori(0, T // RING) as r:
                for s in range(RING):
                    if s % HALF == 0:
                        act.wait_ge(kept, r * 2 + (s // HALF + 1))
                    z = ps[4 + 2 * (s // HALF) + s % 2][:, B * (s % HALF // 2):B * (s % HALF // 2) + B]
                    act.wait_ge(z_ps, r * RING + (s + 1))
                    nc.scalar.activation(h1[:, s, :], z, ACT.Gelu, scale=1.0 / ZSCALE).then_inc(h1_done, 1)
                    nc.scalar.activation(hf[:, s, :], z, ACT.Gelu, scale=1.0 / ZSCALE).then_inc(hf_done, 1)

        @block.gpsimd
        def _(pool):
            nc.gpsimd.memset(hall[:, 0, 0:2], 0.0).then_inc(kept, 2)
            with nc.gpsimd.Fori(0, T // RING) as r:
                for k in range(2):
                    pool.wait_ge(hf_done, r * RING + HALF * (k + 1))
                    nc.gpsimd.tensor_copy(hall[:, :, bass.ds(r * RING + k * HALF, HALF)],
                                          hf[:, HALF * k:HALF * k + HALF, :].rearrange("p t b -> p b t")).then_inc(kept, 1)

        @block.tensor
        def _(pe):
            turn_tiles(nc, pe, ps, xn, ident, xn_done, xT_ps)
            pe.wait_ge(xT_done, NC)
            pe.wait_ge(zero, 2)
            pe.wait_ge(split, 1)

            def inputs(k, par, t0):
                nc.tensor.matmul(ps[4 + 2 * k + par][:, 0:HALF], wABC[:, 1, :], xs[:, bass.ds(t0, HALF // 2, step=2), :],
                                 start=True, stop=True, skip_group_check=True)

            with nc.tensor.Fori(0, T // RING) as r:
                inputs(0, 0, r * RING)
                inputs(0, 1, r * RING + 1)
                for s in range(RING):
                    prev = (s - 1) % RING
                    z = ps[4 + 2 * (s // HALF) + s % 2][:, B * (s % HALF // 2):B * (s % HALF // 2) + B]
                    pe.wait_ge(h1_done, r * RING + (s + 1))
                    nc.tensor.matmul(z, A12[:, 1, :], h1[:, prev, :], start=False, stop=True, skip_group_check=True)
                    nc.tensor.matmul(z, A12[:, 0, :], h1[:, prev, :], start=False, stop=True, skip_group_check=True)
                    pe.wait_ge(h2_done, r * RING + (s + 1))
                    nc.tensor.matmul(z, A12[:, 0, :], h2[:, prev, :], start=False, stop=True,
                                     skip_group_check=True).then_inc(z_ps, 1)
                    if s in (4, 5):
                        inputs(1, s % 2, r * RING + (HALF + s % 2))
            for i in range(NT):
                if i == 0:
                    pe.wait_ge(kept, T // HALF + 2)
                hp = hall[:].rearrange("p b t -> p (b t)")[:, P * i:P * i + P]
                nc.tensor.matmul(ps[i // 4][:, P * (i % 4):P * (i % 4) + P], hp, wABC[:, 2, :],
                                 start=True, stop=True).then_inc(y_ps, 1)

        @block.vector
        def _(ve):
            link = Chain(ve, dve)
            nc.vector.memset(h1[:, RING - 1, :], 0.0).then_inc(h1_done, 1)
            nc.vector.memset(h2[:, RING - 1, :], 0.0).then_inc(h2_done, 1)
            nc.vector.memset(hf[:, RING - 1, :], 0.0).then_inc(zero, 2)
            layer_norm(nc, link, xn, x, stats, small, xn_done)
            ve.wait_ge(ld_w, 80)
            link(nc.vector.tensor_scalar(wABC[:, 0:2], wABC[:, 0:2], ZSCALE, None, ALU.mult))
            link(nc.vector.tensor_copy(A12[:, 0, :], wABC[:, 0, :]))
            link(nc.vector.tensor_copy(A1f[:], A12[:, 0, :]))
            nc.vector.tensor_tensor(A12[:, 1, :], wABC[:, 0, :], A1f[:], ALU.subtract).then_inc(split, 1)
            with nc.vector.Fori(0, T // RING) as r:
                for s in range(RING):
                    ve.wait_ge(hf_done, r * RING + (s + 1))
                    nc.vector.tensor_tensor(h2[:, s, :], hf[:, s, :], h1[:, s, :], ALU.subtract).then_inc(h2_done, 1)
            for i in range(NT):
                ve.wait_ge(y_ps, i + 1 if i % 4 else i + 4)
                ins = nc.vector.bn_stats(stats[:, i, :], ps[i // 4][:, P * (i % 4):P * (i % 4) + P])
            link(ins)
            ln_moments(nc, link, stats, small)
            for i in range(NT):
                ins = nc.vector.tensor_scalar(xn[:, i, :], ps[i // 4][:, P * (i % 4):P * (i % 4) + P],
                                              small[:, 0, i:i + 1], small[:, 1, i:i + 1], ALU.subtract, ALU.mult)
            link(ins)
            whole = lambda k: gb[:, k, :].rearrange("p (o e) -> p o e", o=1).broadcast_to([P, NT, D])
            link(nc.vector.tensor_tensor(xn[:], xn[:], whole(0), ALU.mult))
            link(nc.vector.tensor_tensor(xn[:], xn[:], whole(1), ALU.add))
            link(nc.vector.tensor_tensor(x[:], x[:], xn[:], ALU.add))


def attention_experts(nc, own, a, m, g, ps):
    sb, sem = scoped(nc, own)
    mla = sb("d_mla", [P, B * T])
    with ExitStack() as inner:
        attention(nc, inner, a, m, g, ps, mla)
    gelu_experts(nc, own, a, m, g, ps, mla)


PARTS = 3
TERMS = ((0, 0), (0, 1), (1, 0), (1, 1), (0, 2), (2, 0))
MAX_ROW = len(TERMS) * KPH
GROUPS = B * NHG
UNITS = HG * TB
AHEAD = 4
PIECES = 4
PIECE = T // PIECES
TURN_AT = 6
MAX_AT = UNITS - 2
READ = 2 * PIECES


def selections():
    import numpy as np
    sel = np.zeros((2, H3, KPH, NHG, 2, PARTS, HG, 32), np.float32)
    for h in range(H3):
        for t, parts in enumerate(TERMS):
            for side in range(2):
                for k in range(KPH):
                    sel[side, h, k, h // HG, side, parts[side], h % HG, t * KPH + k] = 1
    return sel.reshape(P, NHG * 2 * PARTS * P)


def attention(nc, own, a, m, g, ps, mla):
    sb, sem = scoped(nc, own)
    x, xn, xT, stats, small, ident = (m[k] for k in ("x", "xn", "xT", "stats", "small", "ident"))
    banks = m["banks"]
    wqk = sb("d_wqk", [P, P])
    wv = sb("d_wv", [P, LAT])
    wo = sb("d_wo", [LAT, D])
    col = sb("d_col", [P, 3 + HG])
    vb = sb("d_vb", [P, LAT])
    sel = sb("d_sel", [P, NHG, 2, PARTS, P], BF16)
    idb = sb("d_idb", [P, P], BF16)
    qk = sb("d_qk", [P, B * T])
    part = sb("d_part", [P, PARTS, B * T], BF16)
    vall = sb("d_vall", [P, GROUPS, TB, HG, KPH])
    vs = sb("d_vs", [P, 2, TB, HG, 32])
    rows = sb("d_rows", [P, 2, GROUPS, T], BF16)
    km = sb("d_km", [P, 2, HG, T], BF16)
    qh = sb("d_qh", [P, 2, HG, T], BF16)
    qm = sb("d_qm", [P, 2, T], BF16)
    mx = sb("d_mx", [P, 2, TB, HG])
    mtop = sb("d_mtop", [P, TB, HG])
    mrow = sb("d_mrow", [P, TB, HG, 32], BF16)
    NE = 2 * HG
    ex = sb("d_ex", [P, NE, T])
    ot = sb("d_ot", [P, T])
    rs = sb("d_rs", [P, TB, HG])
    ao = sb("d_ao", [P, NT, LAT])
    aoT = xT[0:LAT]
    ld_c, dve, xn_done, xT_ps, xT_done = (sem("d_" + n) for n in ("ldc", "dve", "xn", "xT_ps", "xT"))
    qk_ps, qk_done, split, v_ps, v_done, hs_in = (sem("d_" + n) for n in ("qk_ps", "qk", "split", "v_ps", "v", "hs"))
    r_ps, r_out, km_done, qh_done, vs_done = (sem("d_" + n) for n in ("r_ps", "r_out", "km", "qh", "vs"))
    s_ps, s_max, m_done, qm_ps, qm_out = (sem("d_" + n) for n in ("s_ps", "smax", "m", "qm_ps", "qm_out"))
    e_ps, e_done, pv, ot_done, ot_ps, ao_done = (sem("d_" + n) for n in ("e_ps", "e", "pv", "ot", "ot_ps", "ao"))
    aoT_ps, aoT_done, mla_ps, fin = (sem("d_" + n) for n in ("aoT_ps", "aoT", "mla_ps", "fin"))
    ready, mdve, rs_done = sem("d_ready"), sem("d_mdve"), sem("d_rs")
    aov = ao[:].rearrange("p (b s) (g c) -> p b g s c", b=B, g=NHG)

    SPREADS = [(n, side, h) for n in range(GROUPS) for side in (1, 0) for h in range(2)]

    def bank_of(i):
        return ps[2 + i % 6]

    def groups(engine, body):
        body(0, 0, False, 2)
        body(1, 1, True, 2)
        with engine.Fori(1, GROUPS // 2 - 1) as f:
            for k in range(2):
                body(f * 2 + k, k, True, 2)
        body(GROUPS - 2, 0, True, 1)
        body(GROUPS - 1, 1, True, 0)

    with nc.Block() as block:
        @block.sync
        def _(sp):
            sp.dma_start(wqk[:], a["wqk"]).then_inc(ld_c, 16)
            sp.dma_start(wv[:], a["wv1"]).then_inc(ld_c, 16)
            sp.dma_start(wo[:], a["wo1"]).then_inc(ld_c, 16)
            sp.dma_start(col[:, 0:1], a["bqk"].rearrange("(p o) -> p o", o=1)).then_inc(ld_c, 16)
            sp.dma_start(col[:, 1:2], a["ob1"].rearrange("(p o) -> p o", o=1)).then_inc(ld_c, 16)
            sp.dma_start(col[:, 2:3 + HG], a["rows"]).then_inc(ld_c, 16)
            sp.dma_start(vb[:], a["vb1"].rearrange("(o e) -> o e", o=1).broadcast_to([P, LAT])).then_inc(ld_c, 16)
            sp.dma_start(sel[:].rearrange("p g s k c -> p (g s k c)"), a["sel"]).then_inc(ld_c, 16)
            sp.dma_start(idb[:], a["identb"]).then_inc(ld_c, 16)

        LOADS = 16 * 9

        @block.scalar
        def _(act):
            for c in range(NC):
                act.wait_ge(xT_ps, 4 * c + 4)
                nc.scalar.copy(xT[:, CH * c:CH * c + CH], ps[c][:]).then_inc(xT_done, 1)
            act.wait_ge(ld_c, LOADS)
            for c in range(NC):
                act.wait_ge(qk_ps, c + 1)
                nc.scalar.activation(qk[:, CH * c:CH * c + CH], ps[4 + c][:], ACT.Identity, bias=col[:, 0:1]).then_inc(qk_done, 1)
            nc.scalar.preload_act_table(ACT.Exp)
            for i, (n, side, h) in enumerate(SPREADS):
                act.wait_ge(r_ps, i + 1)
                dst = rows[:, side, n, CH * h:CH * h + CH]
                if side:
                    nc.scalar.activation(dst, bank_of(i)[:], ACT.Identity, bias=col[:, 2:3]).then_inc(r_out, 1)
                else:
                    nc.scalar.copy(dst, bank_of(i)[:]).then_inc(r_out, 1)

            def q_rows(n, k):
                for h in range(2):
                    act.wait_ge(qm_ps, n * 2 + (h + 1))
                    nc.scalar.copy(qm[:, k, CH * h:CH * h + CH], ps[h][:]).then_inc(qm_out, 1)

            def take_outputs(n, h):
                act.wait_ge(pv, n * (TB * PIECES) + (READ + (TB - 1) * PIECES + 2 * (h + 1)))
                nc.scalar.copy(ot[:, CH * h:CH * h + CH], ps[6 + h][:]).then_inc(ot_done, 1)

            def group(n, k, before, after):
                for u in range(UNITS):
                    act.wait_ge(e_ps, n * UNITS + (u + 1))
                    if u % HG == 0:
                        act.wait_ge(pv, n * (TB * PIECES) + ((u // HG - 2) * PIECES + PIECES + READ))
                    nc.scalar.activation(ex[:, u % NE, :], banks[:, 2 + 2 * (u % 2):4 + 2 * (u % 2), :].rearrange("p k c -> p (k c)"),
                                         ACT.Exp, scale=0.5).then_inc(e_done, 1)
                    if before and u in (2, 3):
                        if u == 2 and (not isinstance(n, int) or n > 1):
                            act.wait_ge(ot_ps, n - 1)
                        take_outputs(n - 1, u - 2)
                    if after and u == MAX_AT:
                        q_rows(n + 1, 1 - k)

            q_rows(0, 0)
            groups(nc.scalar, group)
            for h in range(2):
                take_outputs(GROUPS - 1, h)
            for c in range(NC):
                act.wait_ge(aoT_ps, 4 * c + 4)
                nc.scalar.copy(aoT[:, CH * c:CH * c + CH], ps[c][0:LAT, :]).then_inc(aoT_done, 1)
            for c in range(NC):
                act.wait_ge(mla_ps, c + 1)
                nc.scalar.activation(mla[:, CH * c:CH * c + CH], ps[4 + c][:], ACT.Identity, bias=col[:, 1:2]).then_inc(fin, 1)

        @block.gpsimd
        def _(pool):
            nc.gpsimd.memset(vs[:], 1.0).then_inc(vs_done, 1)
            nc.gpsimd.memset(mrow[:].rearrange("p s h c -> p (s h c)"), 0.0).then_inc(ready, 1)
            pool.wait_ge(xn_done, NT)
            nc.gpsimd.tensor_tensor(x[:], x[:], xn[:], ALU.add).then_inc(hs_in, 1)

            def one_head_rows(dst, side, n, done):
                for hh in range(HG):
                    src = rows[:, side, bass.ds(n, 1), :].rearrange("p o t -> p (o t)")
                    nc.gpsimd.tensor_tensor(dst[:, hh, :], src, col[:, 3 + hh:4 + hh].broadcast_to([P, T]), ALU.mult).then_inc(done, 1)

            def values_of(n, k):
                src = vall[:, bass.ds(n, 1)].rearrange("p o s h k -> p (o s) h k")
                nc.gpsimd.tensor_copy(vs[:, k, :, :, 0:KPH], src).then_inc(vs_done, 1)

            pool.wait_ge(ld_c, LOADS)
            pool.wait_ge(r_out, 4)
            one_head_rows(km[:, 0], 1, 0, km_done)
            pool.wait_ge(r_out, 8)
            one_head_rows(qh[:, 1], 0, 1, qh_done)
            pool.wait_ge(v_done, B)
            pool.wait_ge(vs_done, 1)
            values_of(0, 0)

            def group(n, k, more):
                if more:
                    pool.wait_ge(s_ps, n * (2 * UNITS) + 2 * UNITS)
                    one_head_rows(qh[:, k], 0, n + 2, qh_done)
                pool.wait_ge(e_ps, n * UNITS + 1)
                one_head_rows(km[:, 1 - k], 1, n + 1, km_done)
                pool.wait_ge(pv, n * (TB * PIECES) + (READ + 1))
                values_of(n + 1, 1 - k)

            pool.wait_ge(r_out, len(SPREADS))
            with nc.gpsimd.Fori(0, GROUPS // 2 - 1) as f:
                for k in range(2):
                    group(f * 2 + k, k, True)
            group(GROUPS - 2, 0, False)

        @block.tensor
        def _(pe):
            turn_tiles(nc, pe, ps, xn, ident, xn_done, xT_ps)
            pe.wait_ge(ld_c, LOADS)
            for c in range(NC):
                pe.wait_ge(xT_done, c + 1)
                nc.tensor.matmul(ps[4 + c][:], wqk[:], xT[:, CH * c:CH * c + CH], start=True, stop=True).then_inc(qk_ps, 1)
            for i in range(NT):
                nc.tensor.matmul(ps[i // 8][:, LAT * (i % 8):LAT * (i % 8) + LAT], xT[:, P * i:P * i + P], wv[:],
                                 start=True, stop=True).then_inc(v_ps, 1)
            pe.wait_ge(qk_done, NC)

            def spread(i):
                n, side, h = SPREADS[i]
                c = (n // NHG) * T + CH * h
                if i >= 6:
                    pe.wait_ge(r_out, i - 5)
                for k in range(PARTS):
                    if i < 4:
                        pe.wait_ge(split, PARTS * (c // CH) + k + 1)
                    mm = nc.tensor.matmul(bank_of(i)[:], sel[:, n % NHG, side, k, :], part[:, k, c:c + CH],
                                          start=(k == 0), stop=(k == PARTS - 1))
                mm.then_inc(r_ps, 1)

            def scores(n, k, u):
                for h in range(2):
                    if not isinstance(n, int) or n or u:
                        pe.wait_ge(s_max, n * (2 * UNITS) + (2 * u + h - 1))
                    nc.tensor.matmul(ps[h][:], qh[:, k, u % HG, P * (u // HG):P * (u // HG) + P],
                                     rows[:, 1, bass.ds(n, 1), CH * h:CH * h + CH].rearrange("p o t -> p (o t)"),
                                     start=True, stop=True).then_inc(s_ps, 1)

            def scores_after(n, k, u, after):
                if u + AHEAD < UNITS:
                    if after >= 1:
                        scores(n + 1, 1 - k, u + AHEAD)
                elif after >= 2:
                    if u + AHEAD == UNITS:
                        pe.wait_ge(qh_done, n * HG + 3 * HG)
                    scores(n + 2, k, u + AHEAD - UNITS)

            def q_and_max(n, seen):
                pe.wait_ge(m_done, n + 1)
                pe.wait_ge(s_max, seen)
                for h in range(2):
                    nc.tensor.matmul(ps[h][:], idb[:], rows[:, 0, bass.ds(n, 1), CH * h:CH * h + CH].rearrange("p o t -> p (o t)"),
                                     start=True, stop=False, skip_group_check=True)
                    for i in range(4):
                        st = 4 * h + i
                        mm = nc.tensor.matmul(ps[h][:, P * i:P * i + P], mrow[:, st].rearrange("p h c -> p (h c)"), idb[:],
                                              start=False, stop=True, skip_group_check=True)
                    mm.then_inc(qm_ps, 1)

            def weights(n, k, u):
                tt, hh = u // HG, u % HG
                if not isinstance(n, int) or n or u >= 2:
                    pe.wait_ge(e_done, n * UNITS + (u - 1))
                for h in range(2):
                    mm = nc.tensor.matmul(ps[2 + 2 * (u % 2) + h][:], km[:, k, hh, P * tt:P * tt + P],
                                          qm[:, k, CH * h:CH * h + CH], start=True, stop=True)
                mm.then_inc(e_ps, 1)

            def values(n, k, v):
                tt, piece = v // PIECES, v % PIECES
                if piece == 0:
                    pe.wait_ge(e_done, n * UNITS + HG * (tt + 1))
                c = PIECE * piece
                for hh in range(HG):
                    mm = nc.tensor.matmul(ps[6 + c // CH][32 * hh:32 * hh + 32, c % CH:c % CH + PIECE], vs[:, k, tt, hh, :],
                                          ex[:, (HG * tt + hh) % NE, c:c + PIECE],
                                          start=(tt == 0 and c % CH == 0), stop=(tt == TB - 1),
                                          tile_position=(0, 32 * hh), skip_group_check=True)
                mm.then_inc(pv, 1)

            def turn_outputs(n, seen):
                pe.wait_ge(ot_done, n * 2 + 2)
                pe.wait_ge(s_max, seen)
                for i in range(TB):
                    mm = nc.tensor.transpose(ps[i // 4][:, P * (i % 4):P * (i % 4) + P], ot[:, P * i:P * i + P], ident[:])
                mm.then_inc(ot_ps, 1)

            def group(n, k, before, after):
                seen = lambda u: n * (2 * UNITS) + (2 * UNITS + 2 * (u + AHEAD))
                for u in range(UNITS):
                    if u == 0:
                        pe.wait_ge(qm_out, n * 2 + 2)
                        pe.wait_ge(km_done, n * HG + HG)
                    weights(n, k, u)
                    if before and u < PIECES:
                        values(n - 1, 1 - k, UNITS - PIECES + u)
                    if u == PIECES:
                        pe.wait_ge(vs_done, n + 2)
                    if u >= PIECES:
                        if before and u in (PIECES, PIECES + 2):
                            pe.wait_ge(ot_done, n * 2 - 1 + (u - PIECES) // 2)
                        values(n, k, u - PIECES)
                    if before and u == TURN_AT:
                        turn_outputs(n - 1, seen(u) if after else GROUPS * 2 * UNITS)
                    if before and u == TURN_AT and after:
                        pe.wait_ge(ao_done, n)
                    if u == MAX_AT + 1 and after:
                        pe.wait_ge(qm_out, n * 2 + 4)
                    scores_after(n, k, u, after)
                    if u == MAX_AT and after:
                        q_and_max(n + 1, seen(u + 1) if after == 2 else GROUPS * 2 * UNITS)

            for i in range(4):
                spread(i)
            pe.wait_ge(qh_done, HG)
            pe.wait_ge(v_done, B)
            done = 4
            for u in range(UNITS):
                scores(0, 0, u)
                while done < len(SPREADS) and done < 4 + (u + 1):
                    spread(done)
                    done += 1
            pe.wait_ge(qh_done, 2 * HG)
            pe.wait_ge(ready, 1)
            for u in range(AHEAD):
                scores(1, 1, u)
            q_and_max(0, 2 * (UNITS + AHEAD))
            pe.wait_ge(r_out, len(SPREADS))
            groups(nc.tensor, group)
            for v in range(UNITS - PIECES, UNITS):
                values(GROUPS - 1, 1, v)
            pe.wait_ge(ao_done, GROUPS - 1)
            turn_outputs(GROUPS - 1, GROUPS * 2 * UNITS)
            pe.wait_ge(ao_done, GROUPS)
            for i in range(NT):
                nc.tensor.transpose(ps[i // 4][0:LAT, P * (i % 4):P * (i % 4) + P], ao[:, i, :], ident[:]).then_inc(aoT_ps, 1)
            for c in range(NC):
                pe.wait_ge(aoT_done, c + 1)
                nc.tensor.matmul(ps[4 + c][:], wo[:], aoT[:, CH * c:CH * c + CH], start=True, stop=True).then_inc(mla_ps, 1)

        @block.vector
        def _(ve):
            link = Chain(ve, dve)
            nc.vector.memset(rs[:], 0.0).then_inc(pv, READ)
            layer_norm(nc, link, xn, x, stats, small, xn_done)
            for c in range(NC):
                ve.wait_ge(qk_done, c + 1)
                at = slice(CH * c, CH * c + CH)
                for k in range(PARTS):
                    nc.vector.tensor_copy(part[:, k, at], qk[:, at]).then_inc(split, 1)
                    if k < PARTS - 1:
                        ve.wait_ge(split, PARTS * c + k + 1)
                        link(nc.vector.tensor_tensor(qk[:, at], qk[:, at], part[:, k, at], ALU.subtract))
                if c == 0:
                    ve.wait_ge(ld_c, LOADS)
                    for b in range(B):
                        ve.wait_ge(v_ps, NT)
                        nc.vector.tensor_tensor(vall[:, NHG * b:NHG * b + NHG].rearrange("p g s h k -> p s g (h k)"),
                                                ps[b][:].rearrange("p (s g e) -> p s g e", s=TB, g=NHG),
                                                vb[:].rearrange("p (o g e) -> p o g e", o=1, g=NHG).broadcast_to([P, TB, NHG, HG * KPH]),
                                                ALU.add).then_inc(v_done, 1)
                if c == 1:
                    ve.wait_ge(r_out, 4)
                    for hh in range(HG):
                        nc.vector.tensor_scalar(qh[:, 0, hh, :], rows[:, 0, 0, :], col[:, 3 + hh:4 + hh], None,
                                                ALU.mult).then_inc(qh_done, 1)
            NM = 6

            def maximum(n, u):
                for h in range(2):
                    ve.wait_ge(s_ps, n * (2 * UNITS) + (2 * u + h + 1))
                    nc.vector.tensor_reduce(mx[:, h, u // HG, u % HG:u % HG + 1], ps[h][:], AX, ALU.max).then_inc(s_max, 1)

            def maxima_to_rows(n, after):
                ve.wait_ge(s_max, n * (2 * UNITS) + 2 * UNITS)
                mlink = Chain(ve, mdve, n * NM)
                mlink(nc.vector.tensor_tensor(mtop[:], mx[:, 0], mx[:, 1], ALU.max))
                mlink(nc.vector.tensor_scalar(mtop[:], mtop[:], -1.0, None, ALU.mult))
                for p in range(PARTS):
                    at = mrow[:, :, :, MAX_ROW + p]
                    if p < PARTS - 1:
                        mlink(nc.vector.tensor_copy(at, mtop[:]))
                        mlink(nc.vector.tensor_tensor(mtop[:], mtop[:], at, ALU.subtract))
                    else:
                        nc.vector.tensor_copy(at, mtop[:]).then_inc(m_done, 1)
                assert mlink.n == NM

            def outputs(n):
                ve.wait_ge(ot_ps, n + 1)
                o = banks[:, 0:2, :].rearrange("p b (s q c) -> p (b s) q c", s=4, q=HG)
                nc.vector.reciprocal(rs[:], o[:, :, :, KPH]).then_inc(rs_done, 1)
                ve.wait_ge(rs_done, n + 1)
                dst = aov[:, bass.ds(n // NHG, 1), bass.ds(n % NHG, 1), :, :]
                nc.vector.tensor_tensor(dst.rearrange("p a c s (q k) -> p (a c s) q k", q=HG), o[:, :, :, 0:KPH],
                                        rs[:].rearrange("p s (q o) -> p s q o", o=1).broadcast_to([P, TB, HG, KPH]),
                                        ALU.mult).then_inc(ao_done, 1)

            def group(n, k, before, after):
                for u in range(UNITS):
                    if before and u == TURN_AT:
                        outputs(n - 1)
                    if u + AHEAD < UNITS:
                        if after >= 1:
                            maximum(n + 1, u + AHEAD)
                    elif after >= 2:
                        maximum(n + 2, u + AHEAD - UNITS)
                    if u + AHEAD == UNITS - 1 and after:
                        maxima_to_rows(n + 1, after)

            ve.wait_ge(ready, 1)
            for u in range(UNITS):
                maximum(0, u)
            maxima_to_rows(0, 1)
            for u in range(AHEAD):
                maximum(1, u)
            groups(nc.vector, group)
            outputs(GROUPS - 1)


def gelu_experts(nc, own, a, m, g, ps, mla):
    sb, sem = scoped(nc, own)
    x, ident = m["x"], m["ident"]
    wt = sb("e_wt", [P, 2, 4, D])
    b1 = sb("e_b1", [P, 2 * E1])
    b1e = sb("e_b1e", [P, 2, 2])
    b2 = sb("e_b2", [E1, D])
    rw = sb("e_rw", [P, E1])
    rb = sb("e_rb", [P, E1])
    low = sb("e_low", [P, E1, E1])
    rank = sb("e_rank", [P, 2, NT, E1 * E1])
    rk = sb("e_rk", [P, NT, E1])
    pr = sb("e_pr", [P, NT, E1])
    tot = sb("e_tot", [P, NT])
    combT = sb("e_combT", [E1, B * T])
    act_ = sb("e_act", [P, 2, 2, CH])
    ld_c, ld_w = sem("e_ld_c"), [sem("e_ld_w0"), sem("e_ld_w1")]
    b_cur = sem("e_b_cur")
    dve, logit, arg, ex_done, comb_done = (sem("e_" + n) for n in ("dve", "logit", "arg", "ex", "comb"))
    cT_ps, cT_done, b_ps, h_ps, act_done, y_ps, acc_done = (sem("e_" + n) for n in
                                                           ("cT_ps", "cT", "b_ps", "h", "act", "y", "acc"))

    with nc.Block() as block:
        @block.sync
        def _(sp):
            w = a["moe1"].rearrange("(f k) r c -> k f r c", k=2)
            for k in range(2):
                sp.dma_start(wt[:, k].rearrange("p m c -> p (m c)"), w[k, 0]).then_inc(ld_w[k], 16)
            for dst, src in ((rw[:], a["router1"]), (b1[:], a["b1T"]), (b2[:], a["b2"]),
                             (rb[:], a["rb1"].rearrange("(o e) -> o e", o=1).broadcast_to([P, E1])),
                             (low[:].rearrange("p i j -> p (i j)"),
                              a["low_1"].rearrange("(o e) -> o e", o=1).broadcast_to([P, E1 * E1]))):
                sp.dma_start(dst, src).then_inc(ld_c, 16)
            with nc.sync.Fori(1, E1 // 2) as f:
                for k in range(2):
                    sp.wait_ge(y_ps, f * (2 * NC) + ((k - 1) * NC + 2))
                    sp.dma_start(wt[:, k].rearrange("p m c -> p (m c)"),
                                 w[k, bass.ds(f, 1)].rearrange("o r c -> r (o c)")).then_inc(ld_w[k], 16)

        @block.scalar
        def _(act):
            act.wait_ge(arg, 1)
            nc.scalar.activation(pr[:].rearrange("p i e -> p (i e)"), pr[:].rearrange("p i e -> p (i e)"),
                                 ACT.Exp).then_inc(ex_done, 1)
            for c in range(NC):
                act.wait_ge(cT_ps, 4 * c + 4)
                nc.scalar.copy(combT[:, CH * c:CH * c + CH], ps[4 + c % 2][0:E1, :]).then_inc(cT_done, 1)
            nc.scalar.preload_act_table(ACT.Gelu)
            with nc.scalar.Fori(0, E1 // 2) as f:
              for k in range(2):
                e = f * 2 + k
                nc.scalar.copy(b1e[:, k], b1[:, bass.ds(e * 2, 2)]).then_inc(b_cur, 1)
                act.wait_ge(b_cur, e + 1)
                for c in range(NC):
                    act.wait_ge(y_ps, e * NC + (c + 1))
                    for h in range(2):
                        act.wait_ge(h_ps, e * (2 * NC) + (2 * c + h + 1))
                        nc.scalar.activation(act_[:, c % 2, h, :], ps[2 * (c % 2) + h][:], ACT.Gelu,
                                             bias=b1e[:, k, h:h + 1]).then_inc(act_done, 1)

        @block.tensor
        def _(pe):
            pe.wait_ge(ld_c, 80)
            for i in range(NT):
                mm = nc.tensor.matmul(ps[6][:, E1 * i:E1 * i + E1], mla[:, P * i:P * i + P], rw[:], start=True, stop=True)
            mm.then_inc(logit, 1)
            pe.wait_ge(comb_done, 1)
            for i in range(NT):
                c = i // 4
                if i % 4 == 0 and c >= 2:
                    pe.wait_ge(cT_done, c - 1)
                nc.tensor.transpose(ps[4 + c % 2][0:E1, P * (i % 4):P * (i % 4) + P], pr[:, i, :], ident[:]).then_inc(cT_ps, 1)
            pe.wait_ge(cT_done, NC)
            for i in range(NT):
                c = i // 4
                mm = nc.tensor.matmul(ps[c][:, P * (i % 4):P * (i % 4) + P], combT[:, P * i:P * i + P], b2[:],
                                      start=True, stop=True)
            mm.then_inc(b_ps, 1)
            pe.wait_ge(acc_done, 2)

            def up(k, e, c):
                if k or c >= 2:
                    pe.wait_ge(act_done, e * (2 * NC) + 2 * (c - 1))
                for h in range(2):
                    nc.tensor.matmul(ps[2 * (c % 2) + h][:], wt[:, k, h, :], mla[:, CH * c:CH * c + CH],
                                     start=True, stop=True).then_inc(h_ps, 1)

            def down(k, e, c):
                pe.wait_ge(act_done, e * (2 * NC) + (2 * c + 2))
                pe.wait_ge(acc_done, e * NC + (c + 1))
                for i in range(4):
                    for h in range(2):
                        mm = nc.tensor.matmul(ps[4 + c % 2][:, P * i:P * i + P], act_[:, c % 2, h, P * i:P * i + P],
                                              wt[:, k, 2 + h, :], start=(h == 0), stop=(h == 1))
                mm.then_inc(y_ps, 1)

            with nc.tensor.Fori(0, E1 // 2) as f:
                for k in range(2):
                    e = f * 2 + k
                    pe.wait_ge(ld_w[k], f * 16 + 16)
                    up(k, e, 0)
                    up(k, e, 1)
                    down(k, e, 0)
                    up(k, e, 2)
                    down(k, e, 1)
                    up(k, e, 3)
                    down(k, e, 2)
                    down(k, e, 3)

        @block.vector
        def _(ve):
            link = Chain(ve, dve)
            flat = lambda t: t.rearrange("p i e -> p (i e)")
            nc.vector.memset(rk[:], 0.0).then_inc(y_ps, 2)
            wide = lambda t, n: t.rearrange("p (i o) -> p i o", o=1).broadcast_to([P, NT, n])
            ve.wait_ge(ld_c, 80)
            ve.wait_ge(logit, 1)
            link(nc.vector.tensor_tensor(pr[:], ps[6][:, 0:NT * E1].rearrange("p (i e) -> p i e", e=E1),
                                         rb[:].rearrange("p (o e) -> p o e", o=1).broadcast_to([P, NT, E1]), ALU.add))
            link(nc.vector.tensor_reduce(tot[:], pr[:], AX, ALU.max))
            nc.vector.tensor_tensor(pr[:], pr[:], wide(tot[:], E1), ALU.subtract).then_inc(arg, 1)
            ve.wait_ge(ex_done, 1)
            link(nc.vector.tensor_reduce(tot[:], pr[:], AX, ALU.add))
            link(nc.vector.reciprocal(tot[:], tot[:]))
            link(nc.vector.tensor_tensor(pr[:], pr[:], wide(tot[:], E1), ALU.mult))
            ranks(nc, link, rk[:], pr[:], rank, low, E1)
            link(nc.vector.tensor_scalar(flat(rk[:]), flat(rk[:]), float(TOPK), None, ALU.is_lt))
            link(nc.vector.tensor_tensor(pr[:], pr[:], rk[:], ALU.mult))
            link(nc.vector.tensor_reduce(tot[:], pr[:], AX, ALU.add))
            link(nc.vector.tensor_scalar(tot[:], tot[:], 1e-8, None, ALU.add))
            link(nc.vector.reciprocal(tot[:], tot[:]))
            link(nc.vector.tensor_scalar(tot[:], tot[:], 0.3, None, ALU.mult))
            nc.vector.tensor_tensor(pr[:], pr[:], wide(tot[:], E1), ALU.mult).then_inc(comb_done, 1)
            ve.wait_ge(b_ps, 1)
            for c in range(NC):
                xs = x[:, 4 * c:4 * c + 4, :].rearrange("p i d -> p (i d)")
                ins = nc.vector.tensor_tensor(xs, xs, ps[c][:], ALU.add)
            ins.then_inc(acc_done, 2)
            ve.wait_ge(acc_done, 2)
            with nc.vector.Fori(0, E1) as e:
                for c in range(NC):
                    ve.wait_ge(y_ps, e * NC + (c + 3))
                    for i in range(4 * c, 4 * c + 4):
                        ins = nc.vector.scalar_tensor_tensor(out=x[:, i, :], in0=ps[4 + c % 2][:, P * (i % 4):P * (i % 4) + P],
                                                             scalar=pr[:, i, bass.ds(e, 1)], in1=x[:, i, :],
                                                             op0=ALU.mult, op1=ALU.add)
                    ins.then_inc(acc_done, 1)


_STAGE = 4


def kernel(**inputs):
    import numpy as np
    import concourse.bacc as bacc
    from concourse import mybir as mb
    from concourse.bass_utils import run_bass_kernel_spmd

    i = {k: np.asarray(v) for k, v in inputs.items()}
    arrays = {
        "x": i["L0_attn_x"],
        "WqT": i["L0_attn_Wq"].T, "WkT": i["L0_attn_Wk"].T, "WvT": i["L0_attn_Wv"].T, "WoT": i["L0_attn_Wo"].T,
        "W_gamma": i["L0_attn_W_gamma"], "b_gamma": i["L0_attn_b_gamma"],
        "W_lambda": i["L0_attn_W_lambda"], "b_lambda": i["L0_attn_b_lambda"],
        "ident": np.eye(128, dtype=np.float32),
        "AT": i["L1_attn_A"].T, "BT": i["L1_attn_B"].T, "CT": i["L1_attn_C"].T,
        "gamma": i["L1_attn_gamma"], "beta": i["L1_attn_beta"],
        "wqk": np.concatenate([i["L1_ffn_q_w"].reshape(128, 16, 8)[:, :, :4].reshape(128, 64), i["L1_ffn_k_w"]], axis=1),
        "bqk": np.concatenate([i["L1_ffn_q_b"].reshape(16, 8)[:, :4].reshape(64), i["L1_ffn_k_b"]]),
        "wv1": i["L1_ffn_v_w"], "vb1": i["L1_ffn_v_b"], "wo1": i["L1_ffn_o_w"][:LAT], "ob1": i["L1_ffn_o_b"],
        "sel": selections().astype(mb.dt.np(mb.dt.bfloat16)), "identb": np.eye(128).astype(mb.dt.np(mb.dt.bfloat16)),
        "rows": np.stack([np.tile(np.isin(np.arange(32), MAX_ROW + np.arange(PARTS)), HG)]
                         + [np.arange(P) // 32 == h for h in range(HG)], axis=1).astype(np.float32),
        "moe1": np.concatenate([i["L1_ffn_w1"], i["L1_ffn_w2"].reshape(8, 2, 128, 128).transpose(0, 2, 1, 3).reshape(8, 128, 256)], axis=2),
        "b1T": i["L1_ffn_b1"].reshape(16, 128).T, "b2": i["L1_ffn_b2"],
        "router1": i["L1_ffn_router_w"], "rb1": i["L1_ffn_router_b"],
        "low_1": np.tri(8, k=-1, dtype=np.float32).reshape(-1),
        "router0": i["L0_ffn_router_w"].T, "bias0": i["L0_ffn_bias"],
        "low_e": np.tri(16, k=-1, dtype=np.float32).reshape(-1), "low_g": np.tri(4, k=-1, dtype=np.float32).reshape(-1),
        "moe0": np.concatenate([
            np.concatenate([i["L0_ffn_gate_w"], i["L0_ffn_sh_gate_w"].reshape(128, 2, 128).transpose(1, 0, 2)]),
            np.concatenate([i["L0_ffn_up_w"], i["L0_ffn_sh_up_w"].reshape(128, 2, 128).transpose(1, 0, 2)]),
            np.concatenate([i["L0_ffn_down_w"], i["L0_ffn_sh_down_w"].reshape(2, 128, 128)])], axis=2),
    }
    arrays = {k: np.ascontiguousarray(v) for k, v in arrays.items()}
    nc = bacc.Bacc("TRN2", target_bir_lowering=False, num_devices=1)
    a = {k: nc.dram_tensor(f"in_{k}", v.shape, mb.dt.from_np(v.dtype), kind="ExternalInput").ap()
         for k, v in arrays.items()}
    out = nc.dram_tensor("out_0_dram", (2, 1024, 128), mb.dt.float32, kind="ExternalOutput").ap()
    build(nc, a, out, _STAGE)
    r = run_bass_kernel_spmd(nc, [{f"in_{k}": v for k, v in arrays.items()}], core_ids=[0])
    return r.results[0]["out_0_dram"]
```

```python
from contextlib import ExitStack

import concourse.bass as bass
from concourse import mybir

F32 = mybir.dt.float32
I32 = mybir.dt.int32
F16 = mybir.dt.float16
BF16 = mybir.dt.bfloat16
ALU = mybir.AluOpType
ACT = mybir.ActivationFunctionType
AX = mybir.AxisListType.X

B, T, D = 2, 1024, 128
P = 128
NT = B * T // P
TB = T // P
CH = 512
NC = B * T // CH
H1, DK = 16, 8
E0, NG, TKG, K0, NSH = 16, 4, 2, 4, 2
WR = 4
SEG = 256
SEGS = T // SEG
H3, KPH = 16, 4
LAT = H3 * KPH
E1, TOPK = 8, 2
HG = 4
NHG = H3 // HG
LN_EPS = 1e-5
ZSCALE = 64.0
RSQRT_SEED = float(0x5F3759DF)


FIRST = "first"


class Chain:

    def __init__(self, eng, sem, base=0):
        self.eng, self.sem, self.base, self.n = eng, sem, base, 0

    def __call__(self, ins):
        self.n += 1
        ins.then_inc(self.sem, 1)
        self.eng.wait_ge(self.sem, self.base + self.n)
        return ins


def rsqrt_step(nc, k, y, x, t):
    if k == 0:
        return nc.vector.tensor_scalar(y.bitcast(I32), x.bitcast(I32), 1, None, ALU.logical_shift_right)
    if k == 1:
        return nc.vector.tensor_scalar(y.bitcast(I32), y.bitcast(I32), -1.0, RSQRT_SEED, ALU.mult, ALU.add)
    if k % 3 == 2:
        return nc.vector.tensor_tensor(t, y, y, ALU.mult)
    if k % 3 == 0:
        return nc.vector.scalar_tensor_tensor(out=t, in0=x, scalar=-0.5, in1=t, op0=ALU.mult, op1=ALU.mult)
    return nc.vector.scalar_tensor_tensor(out=y, in0=t, scalar=1.5, in1=y, op0=ALU.add, op1=ALU.mult)


RSQRT = 11


def rsqrt(nc, link, y, x, t):
    for k in range(RSQRT):
        link(rsqrt_step(nc, k, y, x, t))


def moments_step(nc, k, stats, small):
    mean, rstd, dif, cv = (small[:, q, :] for q in range(4))
    if k == 0:
        nc.vector.tensor_tensor(dif, stats[:, :, 1], stats[:, :, 4], ALU.subtract)
        nc.vector.tensor_tensor(mean, stats[:, :, 1], stats[:, :, 4], ALU.add)
        return nc.vector.tensor_tensor(cv, stats[:, :, 2], stats[:, :, 5], ALU.add)
    if k == 1:
        nc.vector.tensor_scalar(mean, mean, 0.5, None, ALU.mult)
        nc.vector.tensor_scalar(cv, cv, 1.0 / D, LN_EPS, ALU.mult, ALU.add)
        return nc.vector.tensor_tensor(dif, dif, dif, ALU.mult)
    if k == 2:
        return nc.vector.scalar_tensor_tensor(out=cv, in0=dif, scalar=0.25, in1=cv, op0=ALU.mult, op1=ALU.add)
    return rsqrt_step(nc, k - 3, rstd, cv, dif)


MOMENTS = 3 + RSQRT


def ln_moments(nc, link, stats, small):
    for k in range(MOMENTS):
        link(moments_step(nc, k, stats, small))


def layer_norm(nc, link, dst, src, stats, small, done, n=NT):
    for i in range(n):
        ins = nc.vector.bn_stats(stats[:, i, :], src[:, i, :])
    link(ins)
    ln_moments(nc, link, stats, small)
    for i in range(n):
        nc.vector.tensor_scalar(dst[:, i, :], src[:, i, :], small[:, 0, i:i + 1], small[:, 1, i:i + 1],
                                ALU.subtract, ALU.mult).then_inc(done, 1)


def seg_tiles(c):
    n = SEG // P
    return [b * TB + c * n + q for b in range(B) for q in range(n)]


def build(nc, a, out):
    ctx = ExitStack()
    with ctx:
        def sb(name, shape, dt=F32):
            return ctx.enter_context(nc.sbuf_tensor(name, shape, dt))

        def sem(name):
            return ctx.enter_context(nc.semaphore(name))

        banks = ctx.enter_context(nc.psum_tensor("banks", [P, 8, 512], F32))
        ps = [banks[:, i, :] for i in range(8)]
        m = {
            "x": sb("x", [P, NT, D]), "xn": sb("xn", [P, NT, D]), "xT": sb("xT", [P, B * T]),
            "stats": sb("stats", [P, NT, 6]), "small": sb("small", [P, 4, NT]),
            "ident": sb("ident", [P, P]), "banks": banks,
        }
        g = {"ld_x": [sem(f"ld_x{i}") for i in range(NC)], "ld_id": sem("ld_id")}
        with ExitStack() as own:
            gated_recurrence(nc, own, a, m, g, ps)
        with ExitStack() as both:
            m["wt"] = both.enter_context(nc.sbuf_tensor("wt", [P, WR, 3, D], F32))
            m["comb"] = both.enter_context(nc.sbuf_tensor("comb", [P, NT, E0], F32))
            with ExitStack() as own:
                grouped_experts(nc, own, a, m, ps)
            with ExitStack() as own:
                gelu_recurrence(nc, own, a, m, ps)
        with ExitStack() as own:
            attention_experts(nc, own, a, m, ps, out)


def scoped(nc, own):
    def sb(name, shape, dt=F32):
        return own.enter_context(nc.sbuf_tensor(name, shape, dt))

    def sem(name):
        return own.enter_context(nc.semaphore(name))

    return sb, sem


def gated_recurrence(nc, own, a, m, g, ps):
    sb, sem = scoped(nc, own)
    x, xn, xT, stats, small, ident = (m[k] for k in ("x", "xn", "xT", "stats", "small", "ident"))
    wT = sb("wT", [P, 3, D])
    wk_rep = sb("wk_rep", [P, DK, P])
    wo_rep = sb("wo_rep", [P, DK, D])
    par = sb("par", [P, 4, H1])
    qT = sb("qT", [P, B * T])
    vT = sb("vT", [P, B * T])
    rhoE = sb("rhoE", [P, B * T])
    uT = sb("uT", [P, B * T])
    ksq = sb("ksq", [P, NT, D])
    s1 = sb("s1", [P, NT, H1])
    s2 = sb("s2", [P, NT, H1])
    gat = sb("gat", [P, 4, NT, H1])
    rho_x, g_x = ksq, xn
    w = sb("w", [P, 2, T])
    S = sb("S", [P, 2, T])
    qS = sb("qS", [P, 2, T])
    ld_w, ld_p, ld_o = sem("a_ld_w"), sem("a_ld_p"), sem("a_ld_o")
    dve, xn_done, xT_ps, xT_done = sem("a_dve"), sem("a_xn"), sem("a_xT_ps"), sem("a_xT")
    rep, proj, proj_out, kt_ps, ksq_done, s_done = (sem("a_" + n) for n in
                                                     ("rep", "proj", "proj_out", "kt", "ksq", "s"))
    z_done, th_done, gate_done, exp_ps, rho_out, u_done = (sem("a_" + n) for n in
                                                          ("z", "th", "gate", "exp", "rho", "u"))
    rho_spread, g_spread = sem("a_rho_spread"), sem("a_g_spread")
    k_ps, w_done, S_done, qS_done, o_ps = (sem("a_" + n) for n in ("kps", "w", "S", "qS", "o"))

    def spread(gate):
        return gate.rearrange("p i (h o) -> p (i h) o", o=1).broadcast_to([P, NT * H1, DK])

    with nc.Block() as block:
        @block.sync
        def _(sp):
            xin = a["x"].rearrange("b (i p) d -> p (b i) d", p=P)
            for c in range(NC):
                sp.dma_start(x[:, 4 * c:4 * c + 4, :], xin[:, 4 * c:4 * c + 4, :]).then_inc(g["ld_x"][c], 16)
            for k, name in enumerate(("W_gamma", "b_gamma", "W_lambda", "b_lambda")):
                src = a[name].rearrange("(o h) -> o h", o=1)
                sp.dma_start(par[:, k, :], src.broadcast_to([P, H1])).then_inc(ld_p, 16)

        @block.scalar
        def _(act):
            act.dma_start(ident[:], a["ident"]).then_inc(g["ld_id"], 16)
            for k, name in enumerate(("WkT", "WqT", "WvT")):
                act.dma_start(wT[:, (1, 0, 2)[k], :], a[name]).then_inc(ld_w, 16)
            wo = a["WoT"].rearrange("(h j) e -> h j e", j=DK)
            for v in range(DK):
                act.dma_start(wo_rep[v:P:DK, :, :], wo).then_inc(ld_o, 16)
            for c in range(NC):
                act.wait_ge(xT_ps, 4 * c + 4)
                nc.scalar.copy(xT[:, CH * c:CH * c + CH], ps[c][:]).then_inc(xT_done, 1)
            for c in range(NC):
                act.wait_ge(kt_ps, 4 * c + 4)
                nc.scalar.activation(ksq[:, 4 * c:4 * c + 4, :].rearrange("p i d -> p (i d)"), ps[c][:],
                                     ACT.Square).then_inc(ksq_done, 1)
            for c in range(NC):
                for k, dst in enumerate((qT, vT)):
                    act.wait_ge(proj, 2 * c + k + 1)
                    nc.scalar.copy(dst[:, CH * c:CH * c + CH], ps[4 + (2 * c + k) % 4][:]).then_inc(proj_out, 1)
            act.wait_ge(z_done, 1)
            nc.scalar.activation(gat[:, 0:2].rearrange("p k i h -> p (k i h)"),
                                 gat[:, 0:2].rearrange("p k i h -> p (k i h)"), ACT.Tanh, scale=0.5).then_inc(th_done, 1)
            act.wait_ge(gate_done, 1)
            nc.scalar.copy(rho_x[:].rearrange("p i (h v) -> p (i h) v", v=DK), spread(gat[:, 2])).then_inc(rho_spread, 1)
            for c in range(NC):
                act.wait_ge(exp_ps, 2 * c + 1)
                nc.scalar.copy(rhoE[:, CH * c:CH * c + CH], ps[4 + 2 * (c % 2)][:]).then_inc(rho_out, 1)

        @block.gpsimd
        def _(pool):
            pool.wait_ge(ld_w, 48)
            for j in range(DK):
                src = wT[:, 1, j::DK].rearrange("p (h o) -> p h o", o=1).broadcast_to([P, H1, DK])
                nc.gpsimd.tensor_copy(wk_rep[:, j, :].rearrange("p (h v) -> p h v", v=DK), src).then_inc(rep, 1)
            for b in range(B):
                for j in range(DK):
                    n = DK * b + j
                    pool.wait_ge(S_done, n + 1)
                    if n >= 2:
                        pool.wait_ge(o_ps, n - 1)
                    if n == 0:
                        pool.wait_ge(proj_out, 2 * NC)
                    nc.gpsimd.tensor_tensor(qS[:, n % 2, :], S[:, n % 2, :], qT[:, T * b:T * b + T],
                                            ALU.mult).then_inc(qS_done, 1)

        @block.tensor
        def _(pe):
            pe.wait_ge(g["ld_id"], 16)
            for i in range(NT):
                pe.wait_ge(xn_done, i + 1)
                nc.tensor.transpose(ps[i // 4][:, P * (i % 4):P * (i % 4) + P], xn[:, i, :], ident[:]).then_inc(xT_ps, 1)
            pe.wait_ge(ld_w, 48)
            pe.wait_ge(xT_done, NC)
            for i in range(NT):
                nc.tensor.matmul(ps[i // 4][:, P * (i % 4):P * (i % 4) + P], xT[:, P * i:P * i + P], wT[:, 1, :],
                                 start=True, stop=True).then_inc(kt_ps, 1)
            for c in range(NC):
                for k in range(2):
                    n = 2 * c + k
                    if n >= 4:
                        pe.wait_ge(proj_out, n - 3)
                    nc.tensor.matmul(ps[4 + n % 4][:], wT[:, 2 * k, :], xT[:, CH * c:CH * c + CH],
                                     start=True, stop=True).then_inc(proj, 1)
            pe.wait_ge(s_done, NC)
            pe.wait_ge(rep, DK)

            def key_column(n):
                if n >= 2:
                    pe.wait_ge(w_done, n - 1)
                for h in range(2):
                    c = T * (n // DK) + CH * h
                    mm = nc.tensor.matmul(ps[2 * (n % 2) + h][:], wk_rep[:, n % DK, :], xT[:, c:c + CH],
                                          start=True, stop=True)
                mm.then_inc(k_ps, 1)

            key_column(0)
            key_column(1)
            pe.wait_ge(proj_out, 2 * NC)
            for c in range(NC):
                if c >= 2:
                    pe.wait_ge(rho_out, c - 1)
                    pe.wait_ge(u_done, c - 1)
                if c == 0:
                    pe.wait_ge(rho_spread, 1)
                    pe.wait_ge(g_spread, 1)
                for k in range(2):
                    for i in range(4):
                        mm = nc.tensor.transpose(ps[4 + 2 * (c % 2) + k][:, P * i:P * i + P],
                                                 (rho_x, g_x)[k][:, 4 * c + i, :], ident[:])
                    mm.then_inc(exp_ps, 1)
            pe.wait_ge(ld_o, 16 * DK)
            pe.wait_ge(u_done, NC)
            pe.wait_ge(rho_out, NC)
            for n in range(B * DK):
                if n + 2 < B * DK:
                    key_column(n + 2)
                pe.wait_ge(qS_done, n + 1)
                b, j = n // DK, n % DK
                for i in range(TB):
                    mm = nc.tensor.matmul(ps[4 + 2 * b + i // 4][:, P * (i % 4):P * (i % 4) + P],
                                          qS[:, n % 2, P * i:P * i + P], wo_rep[:, j, :],
                                          start=(j == 0 and i % 4 == 0), stop=(j == DK - 1), skip_group_check=True)
                mm.then_inc(o_ps, 1)

        @block.vector
        def _(ve):
            link = Chain(ve, dve)
            for c in range(NC):
                ve.wait_ge(g["ld_x"][c], 16)
            layer_norm(nc, link, xn, x, stats, small, xn_done)
            for c in range(NC):
                ve.wait_ge(ksq_done, c + 1)
                nc.vector.tensor_reduce(s1[:, 4 * c:4 * c + 4, :], ps[c][:].rearrange("p (i h j) -> p i h j", i=4, j=DK),
                                        AX, ALU.add)
                nc.vector.tensor_reduce(s2[:, 4 * c:4 * c + 4, :],
                                        ksq[:, 4 * c:4 * c + 4, :].rearrange("p i (h j) -> p i h j", j=DK),
                                        AX, ALU.add).then_inc(s_done, 1)
            ve.wait_ge(s_done, NC)
            flat = lambda t: t.rearrange("p i h -> p (i h)")
            g0, g1, g2, g3 = (flat(gat[:, k]) for k in range(4))
            link(nc.vector.tensor_scalar(flat(s2[:]), flat(s2[:]), 1e-24, None, ALU.max))
            rsqrt(nc, link, g2, flat(s2[:]), g3)
            link(nc.vector.scalar_tensor_tensor(out=flat(s1[:]), in0=flat(s1[:]), scalar=1.0 / DK, in1=g2,
                                                op0=ALU.mult, op1=ALU.mult))
            ve.wait_ge(ld_p, 64)
            bc = lambda k: par[:, k, :].rearrange("p (o h) -> p o h", o=1).broadcast_to([P, NT, H1])
            for k in range(2):
                link(nc.vector.tensor_tensor(gat[:, k], s1[:], bc(2 * k), ALU.mult))
                ins = nc.vector.tensor_tensor(gat[:, k], gat[:, k], bc(2 * k + 1), ALU.add)
                if k == 0:
                    link(ins)
            ins.then_inc(z_done, 1)
            ve.wait_ge(th_done, 1)
            link(nc.vector.tensor_scalar(g1, g1, -0.25, 0.25, ALU.mult, ALU.add))
            link(nc.vector.scalar_tensor_tensor(out=g0, in0=g0, scalar=1.0, in1=g1, op0=ALU.add, op1=ALU.mult))
            link(nc.vector.tensor_scalar(g3, g0, -1.0, 1.0, ALU.mult, ALU.add))
            link(nc.vector.tensor_tensor(g3, g3, g2, ALU.mult))
            nc.vector.tensor_copy(g2, g0).then_inc(gate_done, 1)
            nc.vector.tensor_copy(g_x[:].rearrange("p i (h v) -> p (i h) v", v=DK), spread(gat[:, 3])).then_inc(g_spread, 1)
            ve.wait_ge(proj_out, 2 * NC)
            for c in range(NC):
                ve.wait_ge(exp_ps, 2 * c + 2)
                cols = slice(CH * c, CH * c + CH)
                nc.vector.tensor_tensor(uT[:, cols], vT[:, cols], ps[5 + 2 * (c % 2)][:], ALU.mult).then_inc(u_done, 1)
            ve.wait_ge(u_done, NC)
            ve.wait_ge(rho_out, NC)

            def add_products(b):
                ve.wait_ge(o_ps, DK * (b + 1))
                for h in range(2):
                    i = TB * b + 4 * h
                    xs = x[:, i:i + 4, :].rearrange("p i d -> p (i d)")
                    nc.vector.tensor_tensor(xs, xs, ps[4 + 2 * b + h][:], ALU.add)

            for n in range(B * DK):
                b = n // DK
                ve.wait_ge(k_ps, n + 1)
                for h in range(2):
                    ins = nc.vector.tensor_tensor(w[:, n % 2, CH * h:CH * h + CH],
                                                  uT[:, T * b + CH * h:T * b + CH * h + CH],
                                                  ps[2 * (n % 2) + h][:], ALU.mult)
                ins.then_inc(w_done, 1)
                ve.wait_ge(w_done, n + 1)
                if n >= 2:
                    ve.wait_ge(qS_done, n - 1)
                nc.vector.tensor_tensor_scan(S[:, n % 2, :], rhoE[:, T * b:T * b + T], w[:, n % 2, :], 0.0,
                                             ALU.mult, ALU.add).then_inc(S_done, 1)
                if n == DK + 3:
                    add_products(0)
            add_products(1)


def turn_tiles(nc, eng, ps, src, ident, ready, turned, first=0):
    for i in range(first, first + NT):
        eng.wait_ge(ready, i + 1)
        nc.tensor.transpose(ps[i // 4][:, P * (i % 4):P * (i % 4) + P], src[:, i, :], ident[:]).then_inc(turned, 1)


def grouped_experts(nc, own, a, m, ps):
    sb, sem = scoped(nc, own)
    x, xn, xT, stats, small, ident = (m[k] for k in ("x", "xn", "xT", "stats", "small", "ident"))
    wt, comb = m["wt"], m["comb"]
    wsh = sb("b_wsh", [P, NSH, 3, D])
    rw = sb("b_rw", [P, E0])
    bias = sb("b_bias", [P, E0])
    sc = sb("b_sc", [P, NT, E0])
    s = sb("b_s", [P, NT, E0])
    gs = sb("b_gs", [P, 6, NT, NG])
    rank = sb("b_rank", [P, NT, E0 * E0])
    rk = sb("b_rk", [P, NT, E0])
    tot = sb("b_tot", [P, NT])
    th = sb("b_th", [P, 2, CH])
    act_ = sb("b_act", [P, 2, CH])
    ld_c, ld_s, ld_w = sem("b_ld_c"), sem("b_ld_s"), [sem(f"b_ld_w{j}") for j in range(WR)]
    dve, xn_done, xT_ps, xT_done = sem("b_dve"), sem("b_xn"), sem("b_xT_ps"), sem("b_xT")
    logit, esig = sem("b_logit"), sem("b_esig")
    h_ps, u_ps, th_done, hu_done, y_ps, acc_done = (sem("b_" + n) for n in ("h", "u", "th", "hu", "y", "acc"))
    gtmp = sem("b_gtmp")
    SHARED = NSH * NC
    first = xT[:].rearrange("p (b t) -> p b t", b=B)[:, :, 0:SEG]

    with nc.Block() as block:
        @block.sync
        def _(sp):
            sp.dma_start(rw[:], a["router0"]).then_inc(ld_c, 16)
            sp.dma_start(bias[:], a["bias0"].rearrange("(o e) -> o e", o=1).broadcast_to([P, E0])).then_inc(ld_c, 16)
            for k in range(NSH):
                sp.dma_start(wsh[:, k].rearrange("p m c -> p (m c)"), a["moe0"][E0 + k]).then_inc(ld_s, 16)
            w = a["moe0"][0:E0].rearrange("(f k) r c -> k f r c", k=WR)
            for j in range(WR):
                sp.dma_start(wt[:, j].rearrange("p m c -> p (m c)"), w[j, 0]).then_inc(ld_w[j], 16)
            with nc.sync.Fori(1, E0 // WR) as f:
                for j in range(WR):
                    sp.wait_ge(y_ps, f * WR + (SHARED - WR + j + 1))
                    sp.dma_start(wt[:, j].rearrange("p m c -> p (m c)"),
                                 w[j, bass.ds(f, 1)].rearrange("o r c -> r (o c)")).then_inc(ld_w[j], 16)

        @block.scalar
        def _(act):
            for c in range(NC):
                act.wait_ge(xT_ps, 4 * c + 4)
                nc.scalar.copy(xT[:, CH * c:CH * c + CH], ps[c][:]).then_inc(xT_done, 1)
            act.wait_ge(logit, 1)
            nc.scalar.activation(sc[:].rearrange("p i e -> p (i e)"), ps[4][:, 0:NT * E0], ACT.Exp,
                                 scale=-1.0).then_inc(esig, 1)
            nc.scalar.preload_act_table(ACT.Tanh)

            def half_tanh(n, k):
                act.wait_ge(h_ps, n + 1)
                act.wait_ge(hu_done, n + 1)
                nc.scalar.activation(th[:, k, :], ps[k][:], ACT.Tanh, scale=0.5).then_inc(th_done, 1)

            with nc.scalar.Fori(0, (SHARED + E0) // 2) as f:
                for k in range(2):
                    half_tanh(f * 2 + k, k)

        @block.tensor
        def _(pe):
            turn_tiles(nc, pe, ps, xn, ident, xn_done, xT_ps)
            pe.wait_ge(ld_c, 32)
            pe.wait_ge(xT_done, NC)
            for i in range(NT):
                mm = nc.tensor.matmul(ps[4][:, E0 * i:E0 * i + E0], xT[:, P * i:P * i + P], rw[:], start=True, stop=True)
            mm.then_inc(logit, 1)
            pe.wait_ge(esig, 1)

            def up(n, k, w, cols):
                pe.wait_ge(hu_done, n + 1)
                nc.tensor.matmul(ps[k][:], w[:, 0, :], cols, start=True, stop=True).then_inc(h_ps, 1)
                nc.tensor.matmul(ps[2 + k][:], w[:, 1, :], cols, start=True, stop=True).then_inc(u_ps, 1)

            def down(n, k, w):
                pe.wait_ge(hu_done, n + 3)
                pe.wait_ge(acc_done, n + 1)
                for i in range(4):
                    mm = nc.tensor.matmul(ps[4 + k][:, P * i:P * i + P], act_[:, k, P * i:P * i + P],
                                          w[:, 2, :], start=True, stop=True)
                mm.then_inc(y_ps, 1)

            pe.wait_ge(ld_s, 16 * NSH)
            for n in range(SHARED):
                c = n % NC
                up(n, n % 2, wsh[:, n // NC], xT[:, CH * c:CH * c + CH])
                if n:
                    down(n - 1, 1 - n % 2, wsh[:, (n - 1) // NC])
            pe.wait_ge(ld_w[0], 16)
            up(SHARED, 0, wt[:, 0], first)
            down(SHARED - 1, 1, wsh[:, NSH - 1])
            with nc.tensor.Fori(0, E0 // WR - 1) as f:
                for j in range(WR):
                    nxt = (j + 1) % WR
                    pe.wait_ge(ld_w[nxt], f * 16 + (16 if j + 1 < WR else 32))
                    up(f * WR + (SHARED + j + 1), (j + 1) % 2, wt[:, nxt], first)
                    down(f * WR + (SHARED + j), j % 2, wt[:, j])
            for j in range(WR):
                n = SHARED + E0 - WR + j
                if j + 1 < WR:
                    pe.wait_ge(ld_w[j + 1], 16 * (E0 // WR))
                    up(n + 1, (j + 1) % 2, wt[:, j + 1], first)
                down(n, j % 2, wt[:, j])

        @block.vector
        def _(ve):
            link = Chain(ve, dve)
            nc.vector.memset(tot[:], 0.0).then_inc(hu_done, 2)
            nc.vector.memset(rk[:], 0.0).then_inc(acc_done, 2)
            layer_norm(nc, link, xn, x, stats, small, xn_done)
            ve.wait_ge(esig, 1)
            flat = lambda t: t.rearrange("p i e -> p (i e)")
            link(nc.vector.tensor_scalar(flat(sc[:]), flat(sc[:]), 1.0, None, ALU.add))
            link(nc.vector.reciprocal(flat(sc[:]), flat(sc[:])))
            link(nc.vector.tensor_tensor(s[:], sc[:], bias[:].rearrange("p (o e) -> p o e", o=1).broadcast_to([P, NT, E0]),
                                         ALU.add))
            mem = [flat(s[:]).rearrange("p (i g q) -> p i g q", i=NT, g=NG)[:, :, :, q] for q in range(4)]
            nc.vector.tensor_tensor(gs[:, 0], mem[0], mem[1], ALU.add)
            nc.vector.tensor_tensor(gs[:, 1], mem[2], mem[3], ALU.add)
            nc.vector.tensor_tensor(gs[:, 2], mem[0], mem[1], ALU.max)
            link(nc.vector.tensor_tensor(gs[:, 3], mem[2], mem[3], ALU.max))
            nc.vector.tensor_tensor(gs[:, 0], gs[:, 0], gs[:, 1], ALU.max)
            link(nc.vector.tensor_tensor(gs[:, 4], gs[:, 2], gs[:, 3], ALU.add))
            link(nc.vector.tensor_tensor(gs[:, 0], gs[:, 0], gs[:, 4], ALU.max))
            ranks(nc, link, gs[:, 5], gs[:, 0], rank, NG)
            keep = gs[:, 4]
            link(nc.vector.tensor_scalar(flat(keep), flat(gs[:, 5]), float(TKG), None, ALU.is_lt))
            keep_e = keep.rearrange("p i (g o) -> p (i g) o", o=1).broadcast_to([P, NT * NG, E0 // NG])
            s_g = flat(s[:]).rearrange("p (ig q) -> p ig q", q=E0 // NG)
            link(nc.vector.tensor_tensor(s_g, s_g, keep_e, ALU.mult))
            link(nc.vector.tensor_scalar(flat(keep), flat(keep), 1.0, None, ALU.subtract))
            link(nc.vector.tensor_tensor(s_g, s_g, keep_e, ALU.add))
            ranks(nc, link, rk[:], s[:], rank, E0)
            link(nc.vector.tensor_scalar(flat(rk[:]), flat(rk[:]), float(K0), None, ALU.is_lt))
            link(nc.vector.tensor_tensor(sc[:], sc[:], rk[:], ALU.mult))
            link(nc.vector.tensor_reduce(tot[:], sc[:], AX, ALU.add))
            link(nc.vector.tensor_scalar(tot[:], tot[:], 1e-20, None, ALU.add))
            link(nc.vector.reciprocal(tot[:], tot[:]))
            link(nc.vector.tensor_scalar(tot[:], tot[:], 1.25, None, ALU.mult))
            link(nc.vector.tensor_tensor(comb[:], sc[:], tot[:].rearrange("p (i o) -> p i o", o=1).broadcast_to([P, NT, E0]),
                                         ALU.mult))

            def silu(n, k):
                ve.wait_ge(th_done, n + 1)
                nc.vector.scalar_tensor_tensor(out=act_[:, k, :], in0=th[:, k, :], scalar=1.0, in1=ps[k][:],
                                               op0=ALU.add, op1=ALU.mult).then_inc(gtmp, 1)
                ve.wait_ge(u_ps, n + 1)
                ve.wait_ge(gtmp, n + 1)
                nc.vector.tensor_tensor(act_[:, k, :], act_[:, k, :], ps[2 + k][:], ALU.mult).then_inc(hu_done, 1)

            def accumulate(n, k, tiles, weight):
                ve.wait_ge(y_ps, n + 1)
                ve.wait_ge(acc_done, n + 2)
                for q, i in enumerate(tiles):
                    ins = nc.vector.scalar_tensor_tensor(out=x[:, i, :], in0=ps[4 + k][:, P * q:P * q + P],
                                                         scalar=weight(i), in1=x[:, i, :], op0=ALU.mult, op1=ALU.add)
                ins.then_inc(acc_done, 1)

            def shared(n):
                accumulate(n, n % 2, range(4 * (n % NC), 4 * (n % NC) + 4), lambda i: 0.5)

            def expert(n, k, e):
                accumulate(n, k, seg_tiles(0), lambda i: comb[:, i, bass.ds(e, 1)])

            silu(0, 0)
            for n in range(1, SHARED):
                silu(n, n % 2)
                shared(n - 1)
            silu(SHARED, 0)
            shared(SHARED - 1)
            with nc.vector.Fori(0, E0 // 2 - 1) as f:
                for k in range(2):
                    silu(f * 2 + (SHARED + 1 + k), 1 - k)
                    expert(f * 2 + (SHARED + k), k, f * 2 + k)
            silu(SHARED + E0 - 1, 1)
            expert(SHARED + E0 - 2, 0, E0 - 2)
            expert(SHARED + E0 - 1, 1, E0 - 1)


def ranks(nc, link, out, val, beats, n):
    beats = beats[:, :, 0:n * n].rearrange("p t (i j) -> p t i j", j=n)
    for j in range(n):
        for lo, hi, op in ((0, j + 1, ALU.is_gt), (j + 1, n, ALU.is_ge)):
            if lo == n:
                continue
            ins = nc.vector.tensor_tensor(beats[:, :, lo:hi, j], val[:, :, j:j + 1].broadcast_to([P, NT, hi - lo]),
                                          val[:, :, lo:hi], op)
    link(ins)
    link(nc.vector.tensor_reduce(out, beats, AX, ALU.add))


def gelu_recurrence(nc, own, a, m, ps):
    sb, sem = scoped(nc, own)
    x, xn, xT, stats, small, ident = (m[k] for k in ("x", "xn", "xT", "stats", "small", "ident"))
    wt, comb = m["wt"], m["comb"]
    HALF = 32
    RING = 2 * HALF
    SLOT = RING // WR
    ROUNDS = SEG // RING
    GATE, TANH, UP, GATED, HIDDEN, DOWN, ADD = 0, 2, 4, 3, 7, 10, 12
    wABC = sb("c_w", [P, 3, D])
    A12 = sb("c_A12", [P, 2, D], F16)
    A1f = sb("c_A1f", [P, D])
    gb = sb("c_gb", [P, 2, D])
    h1 = sb("c_h1", [P, RING, B], F16)
    h2 = sb("c_h2", [P, RING, B], F16)
    hf = sb("c_hf", [P, RING, B])
    hall = sb("c_hall", [P, B, T])
    xc = sb("c_xc", [P, 4, D])
    cc = sb("c_cc", [P, 4, E0])
    nx = sb("c_nx", [P, 4, D])
    nxT = sb("c_nxT", [P, B, SEG + RING])
    stats4 = sb("c_stats4", [P, 4, 6])
    small4 = sb("c_small4", [P, 4, 4])
    th = sb("c_th", [P, 4, P])
    hid = sb("c_hid", [P, 4, P])
    hT = sb("c_hT", [P, 4, P])
    yn = sb("c_yn", [P, 4, D])
    xs = sb("c_xs", [P, 4, D])
    hT_in, fy_ps, fm, yn_done, fp, xs_in, fn_done = (sem("c_f_" + n) for n in ("hT", "y", "m", "yn", "p", "xs", "n"))
    ld_a, ld_w = sem("c_lda"), [sem(f"c_ld_w{j}") for j in range(WR)]
    dve, nx_done, nxT_ps, nxT_done, xc_in = (sem("c_" + n) for n in ("dve", "nx", "nxT_ps", "nxT", "xc"))
    zero, split, h1_done, hf_done, h2_done, z_ps, kept = (sem("c_" + n) for n in
                                                         ("zero", "split", "h1", "hf", "h2", "z", "kept"))
    gate_ps, up_ps, down_ps, th_done, gated, hid_done, added = (sem("c_" + n) for n in
                                                               ("gate", "up", "down", "th", "gated", "hid", "added"))
    y_ps = sem("c_y")
    xv = x[:].rearrange("p (b c q) d -> p c b q d", b=B, q=SEG // P)
    xnv = xn[:].rearrange("p (b c q) d -> p c b q d", b=B, q=SEG // P)
    cv = comb[:].rearrange("p (b c q) e -> p c b q e", b=B, q=SEG // P)
    pairs = lambda t: t[:].rearrange("p (b q) d -> p b q d", b=B)

    F_PRODUCT, F_STATS, F_NORM, F_STATS2, F_NORM2 = 2, 7, 25, 37, 55
    assert F_STATS + 4 + MOMENTS == F_NORM and F_STATS2 + 4 + MOMENTS == F_NORM2 and F_NORM2 + 4 <= RING

    def chunks(engine, begin, turn, end):
        with engine.Fori(0, SEGS - 1) as c:
            begin(c)
            with engine.Fori(0, ROUNDS) as r:
                turn(c, r, "experts")
            end(c)
        begin(SEGS - 1)
        with engine.Fori(0, ROUNDS - 1) as r:
            turn(SEGS - 1, r, "finished")
        turn(SEGS - 1, ROUNDS - 1, None)

    with nc.Block() as block:
        @block.sync
        def _(sp):
            for k, name in enumerate(("AT", "BT", "CT")):
                sp.dma_start(wABC[:, k, :], a[name]).then_inc(ld_a, 16)
            for k, name in enumerate(("gamma", "beta")):
                sp.dma_start(gb[:, k, :], a[name].rearrange("(o e) -> o e", o=1).broadcast_to([P, D])).then_inc(ld_a, 16)
            w = a["moe0"][0:E0].rearrange("(f k) r c -> k f r c", k=WR)
            with nc.sync.Fori(0, SEGS - 1) as c:
                with nc.sync.Fori(0, E0 // WR) as f:
                    for j in range(WR):
                        sp.wait_ge(down_ps, c * (4 * E0) + f * (4 * WR) + 4 * (j + 1))
                        sp.dma_start(wt[:, j].rearrange("p m c -> p (m c)"),
                                     w[j, bass.ds(f, 1)].rearrange("o r c -> r (o c)")).then_inc(ld_w[j], 16)

        @block.scalar
        def _(act):
            nc.scalar.preload_act_table(ACT.Gelu)

            def begin(c):
                act.wait_ge(nxT_ps, c + 1)
                nc.scalar.copy(nxT[:, :, 0:SEG], ps[0][:].rearrange("p (b t) -> p b t", b=B)).then_inc(nxT_done, 1)

            def turn(c, r, beside):
                steps = c * SEG + r * RING
                tiles = c * (4 * E0) + r * (4 * WR)
                for s in range(RING):
                    if s % HALF == 0:
                        act.wait_ge(kept, c * (2 * ROUNDS) + r * 2 + (s // HALF + 1))
                    z = ps[4 + 2 * (s // HALF) + s % 2][:, B * (s % HALF // 2):B * (s % HALF // 2) + B]
                    act.wait_ge(z_ps, steps + (s + 1))
                    nc.scalar.activation(h1[:, s, :], z, ACT.Gelu, scale=1.0 / ZSCALE).then_inc(h1_done, 1)
                    nc.scalar.activation(hf[:, s, :], z, ACT.Gelu, scale=1.0 / ZSCALE).then_inc(hf_done, 1)
                    if beside == "experts" and s % SLOT in (TANH, TANH + 2):
                        q = (s % SLOT - TANH) // 2
                        act.wait_ge(gate_ps, tiles + (4 * (s // SLOT) + 2 * q + 2))
                        nc.scalar.activation(th[:, 2 * q:2 * q + 2, :].rearrange("p i c -> p (i c)"), ps[q][:, 0:2 * P],
                                             ACT.Tanh, scale=0.5).then_inc(th_done, 2)

            chunks(nc.scalar, begin, turn, lambda c: None)

        @block.gpsimd
        def _(pool):
            nc.gpsimd.memset(hall[:, 0, 0:2], 0.0).then_inc(kept, 2)

            link = Chain(pool, fp)
            whole = lambda k: gb[:, k, :].rearrange("p (o e) -> p o e", o=1).broadcast_to([P, 4, D])

            def keep_half(c, r, k):
                pool.wait_ge(hf_done, c * SEG + r * RING + HALF * (k + 1))
                nc.gpsimd.tensor_copy(hall[:, :, bass.ds(c * SEG + r * RING + k * HALF, HALF)],
                                      hf[:, HALF * k:HALF * k + HALF, :].rearrange("p t b -> p b t")).then_inc(kept, 1)

            for c in range(SEGS - 1):
                pool.wait_ge(nx_done, c * 4 + 4)
                if c:
                    pool.wait_ge(xc_in, 3 * c)
                nc.gpsimd.tensor_copy(pairs(xc), xv[:, c + 1]).then_inc(xc_in, 1)
                nc.gpsimd.tensor_copy(pairs(cc), cv[:, c + 1]).then_inc(xc_in, 1)
                with nc.gpsimd.Fori(0, ROUNDS) as r:
                    for k in range(2):
                        keep_half(c, r, k)
                pool.wait_ge(added, c * (4 * E0) + (4 * E0 + 4))
                nc.gpsimd.tensor_copy(xv[:, c + 1], pairs(xc)).then_inc(xc_in, 1)
            pool.wait_ge(xc_in, 3 * (SEGS - 1))
            pool.wait_ge(ld_a, 80)
            for r in range(ROUNDS - 1):
                pool.wait_ge(kept, 2 + 2 * ROUNDS * (r + 1))
                nc.gpsimd.tensor_copy(hT[:].rearrange("p (b q) c -> p b (q c)", b=B), hall[:, :, SEG * r:SEG * r + SEG]).then_inc(hT_in, 1)
                pool.wait_ge(yn_done, 4 * r + 4)
                link(nc.gpsimd.tensor_tensor(yn[:], yn[:], whole(0), ALU.mult))
                link(nc.gpsimd.tensor_tensor(yn[:], yn[:], whole(1), ALU.add))
                nc.gpsimd.tensor_tensor(pairs(xs), pairs(yn), xv[:, r], ALU.add).then_inc(xs_in, 1)
                keep_half(SEGS - 1, r, 0)
                pool.wait_ge(fn_done, 4 * r + 4)
                nc.gpsimd.tensor_copy(xnv[:, r], pairs(nx))
                pool.wait_ge(xs_in, r + 1)
                link(nc.gpsimd.tensor_tensor(xv[:, r], pairs(xs), pairs(nx), ALU.add))
                keep_half(SEGS - 1, r, 1)
            for k in range(2):
                keep_half(SEGS - 1, ROUNDS - 1, k)

        @block.tensor
        def _(pe):
            pe.wait_ge(zero, 2)
            pe.wait_ge(split, 1)

            def inputs(k, par, t0):
                nc.tensor.matmul(ps[4 + 2 * k + par][:, 0:HALF], wABC[:, 1, :],
                                 nxT[:].rearrange("p b t -> p t b")[:, bass.ds(t0, HALF // 2, step=2), :],
                                 start=True, stop=True, skip_group_check=True)

            def beside_step(s, c, r, tiles):
                j, w = s // SLOT, s % SLOT
                before = tiles + 4 * j
                if GATE <= w < GATE + 4 or UP <= w < UP + 4:
                    up = w >= UP
                    i = w % 4
                    if w == GATE:
                        pe.wait_ge(ld_w[j], c * (16 * (E0 // WR)) + r * 16 + 16)
                    if w in (GATE, GATE + 2):
                        pe.wait_ge(added, before + (2 + i))
                    t = c * SEG + ((i // 2) * T + SEG + P * (i % 2))
                    nc.tensor.matmul(ps[2 * up + i // 2][:, P * (i % 2):P * (i % 2) + P], wt[:, j, int(up), :],
                                     xT[:, bass.ds(t, P)], start=True, stop=True).then_inc(up_ps if up else gate_ps, 1)
                elif DOWN <= w < DOWN + 4:
                    i = w - DOWN
                    pe.wait_ge(hid_done, before + (2 * (i // 2) + 2))
                    nc.tensor.matmul(ps[i // 2][:, P * (i % 2):P * (i % 2) + P], hid[:, i, :], wt[:, j, 2, :],
                                     start=True, stop=True).then_inc(down_ps, 1)

            def begin(c):
                for i in range(4):
                    pe.wait_ge(nx_done, c * 4 + (i + 1))
                    mm = nc.tensor.transpose(ps[0][:, P * i:P * i + P], nx[:, i, :], ident[:])
                mm.then_inc(nxT_ps, 1)
                pe.wait_ge(nxT_done, c + 1)
                for par in range(2):
                    inputs(0, par, par)

            def turn(c, r, beside):
                steps = c * SEG + r * RING
                tiles = c * (4 * E0) + r * (4 * WR)
                for s in range(RING):
                    prev = (s - 1) % RING
                    z = ps[4 + 2 * (s // HALF) + s % 2][:, B * (s % HALF // 2):B * (s % HALF // 2) + B]
                    pe.wait_ge(h1_done, steps + (s + 1))
                    nc.tensor.matmul(z, A12[:, 1, :], h1[:, prev, :], start=False, stop=True, skip_group_check=True)
                    nc.tensor.matmul(z, A12[:, 0, :], h1[:, prev, :], start=False, stop=True, skip_group_check=True)
                    pe.wait_ge(h2_done, steps + (s + 1))
                    nc.tensor.matmul(z, A12[:, 0, :], h2[:, prev, :], start=False, stop=True,
                                     skip_group_check=True).then_inc(z_ps, 1)
                    if beside == "experts":
                        beside_step(s, c, r, tiles)
                    if beside == "finished" and F_PRODUCT <= s < F_PRODUCT + 4:
                        i = s - F_PRODUCT
                        pe.wait_ge(hT_in, r + 1)
                        nc.tensor.matmul(ps[0][:, P * i:P * i + P], hT[:, i, :], wABC[:, 2, :],
                                         start=True, stop=True).then_inc(fy_ps, 1)
                    if s in (SLOT - 2, SLOT - 1):
                        inputs(1, s % 2, r * RING + (HALF + s % 2))
                    if beside and s in (3 * SLOT - 2, 3 * SLOT - 1):
                        inputs(0, s % 2, r * RING + (RING + s % 2))

            chunks(nc.tensor, begin, turn, lambda c: None)
            pe.wait_ge(kept, T // HALF + 2)
            for q, i in enumerate(seg_tiles(SEGS - 1)):
                hp = hall[:].rearrange("p b t -> p (b t)")[:, P * i:P * i + P]
                mm = nc.tensor.matmul(ps[1][:, P * q:P * q + P], hp, wABC[:, 2, :], start=True, stop=True)
            mm.then_inc(y_ps, 1)

        @block.vector
        def _(ve):
            NORM = 15
            nc.vector.memset(h1[:, RING - 1, :], 0.0).then_inc(h1_done, 1)
            nc.vector.memset(h2[:, RING - 1, :], 0.0).then_inc(h2_done, 1)
            nc.vector.memset(nxT[:, :, SEG:SEG + RING], 0.0)
            nc.vector.memset(hf[:, RING - 1, :], 0.0).then_inc(zero, 2)
            nc.vector.memset(th[:], 0.0).then_inc(down_ps, 4 * WR)
            nc.vector.memset(hid[:], 0.0).then_inc(added, 4)

            def norm(n, link, tiles):
                for i in range(4):
                    ins = nc.vector.bn_stats(stats4[:, i, :], tiles[i])
                link(ins)
                ln_moments(nc, link, stats4, small4)
                for i in range(4):
                    nc.vector.tensor_scalar(nx[:, i, :], tiles[i], small4[:, 0, i:i + 1], small4[:, 1, i:i + 1],
                                            ALU.subtract, ALU.mult).then_inc(nx_done, 1)
                assert link.n == NORM

            norm(0, Chain(ve, dve), [x[:, i, :] for i in seg_tiles(0)])
            link = Chain(ve, dve, NORM)
            ve.wait_ge(ld_a, 80)
            link(nc.vector.tensor_scalar(wABC[:, 0:2], wABC[:, 0:2], ZSCALE, None, ALU.mult))
            link(nc.vector.tensor_copy(A12[:, 0, :], wABC[:, 0, :]))
            link(nc.vector.tensor_copy(A1f[:], A12[:, 0, :]))
            nc.vector.tensor_tensor(A12[:, 1, :], wABC[:, 0, :], A1f[:], ALU.subtract).then_inc(split, 1)
            LINKS = NORM + link.n

            def beside_step(s, c, r, tiles):
                j, w = s // SLOT, s % SLOT
                before = tiles + 4 * j
                if GATED <= w < GATED + 4:
                    i = w - GATED
                    ve.wait_ge(th_done, before + (2 * (i // 2) + 2))
                    nc.vector.scalar_tensor_tensor(out=hid[:, i, :], in0=th[:, i, :], scalar=1.0,
                                                   in1=ps[i // 2][:, P * (i % 2):P * (i % 2) + P],
                                                   op0=ALU.add, op1=ALU.mult).then_inc(gated, 1)
                elif HIDDEN <= w < HIDDEN + 4:
                    i = w - HIDDEN
                    ve.wait_ge(up_ps, before + (2 * (i // 2) + 2))
                    ve.wait_ge(gated, before + (i + 1))
                    nc.vector.tensor_tensor(hid[:, i, :], hid[:, i, :], ps[2 + i // 2][:, P * (i % 2):P * (i % 2) + P],
                                            ALU.mult).then_inc(hid_done, 1)
                elif ADD <= w < ADD + 4:
                    i = w - ADD
                    if s == ADD:
                        ve.wait_ge(xc_in, c * 3 + 2)
                    ve.wait_ge(down_ps, before + (2 * (i // 2) + 2 + 4 * WR))
                    nc.vector.scalar_tensor_tensor(out=xc[:, i, :], in0=ps[i // 2][:, P * (i % 2):P * (i % 2) + P],
                                                   scalar=cc[:, i, bass.ds(r * WR + j, 1)], in1=xc[:, i, :],
                                                   op0=ALU.mult, op1=ALU.add).then_inc(added, 1)

            def finished_step(s, r):
                before = r * (2 * (MOMENTS + 1))
                for k, (stats_at, norm_at) in enumerate(((F_STATS, F_NORM), (F_STATS2, F_NORM2))):
                    src = lambda i: xs[:, i, :] if k else ps[0][:, P * i:P * i + P]
                    done = before + k * (MOMENTS + 1)
                    if s == stats_at:
                        if k:
                            ve.wait_ge(xs_in, r + 1)
                        else:
                            ve.wait_ge(fy_ps, r * 4 + 4)
                    if stats_at <= s < stats_at + 4:
                        ins = nc.vector.bn_stats(stats4[:, s - stats_at, :], src(s - stats_at))
                        if s == stats_at + 3:
                            ins.then_inc(fm, 1)
                    elif stats_at + 4 <= s < norm_at:
                        step = s - stats_at - 4
                        ve.wait_ge(fm, done + (step + 1))
                        moments_step(nc, step, stats4, small4).then_inc(fm, 1)
                    elif norm_at <= s < norm_at + 4:
                        i = s - norm_at
                        if i == 0:
                            ve.wait_ge(fm, done + (MOMENTS + 1))
                        nc.vector.tensor_scalar((nx if k else yn)[:, i, :], src(i), small4[:, 0, i:i + 1], small4[:, 1, i:i + 1],
                                                ALU.subtract, ALU.mult).then_inc(fn_done if k else yn_done, 1)

            def turn(c, r, beside):
                steps = c * SEG + r * RING
                tiles = c * (4 * E0) + r * (4 * WR)
                for s in range(RING):
                    ve.wait_ge(hf_done, steps + (s + 1))
                    nc.vector.tensor_tensor(h2[:, s, :], hf[:, s, :], h1[:, s, :], ALU.subtract).then_inc(h2_done, 1)
                    if beside == "experts":
                        beside_step(s, c, r, tiles)
                    elif beside == "finished":
                        finished_step(s, r)

            def end(c):
                ve.wait_ge(added, c * (4 * E0) + (4 * E0 + 4))
                norm(c + 1, Chain(ve, dve, c * NORM + LINKS), [xc[:, i, :] for i in range(4)])

            chunks(nc.vector, lambda c: None, turn, end)
            link = Chain(ve, dve, LINKS + (SEGS - 1) * NORM)
            tiles = [ps[1][:, P * i:P * i + P] for i in range(4)]
            ve.wait_ge(y_ps, 1)
            for i in range(4):
                ins = nc.vector.bn_stats(stats4[:, i, :], tiles[i])
            link(ins)
            ln_moments(nc, link, stats4, small4)
            ve.wait_ge(xs_in, ROUNDS - 1)
            for i in range(4):
                ins = nc.vector.tensor_scalar(yn[:, i, :], tiles[i], small4[:, 0, i:i + 1], small4[:, 1, i:i + 1],
                                              ALU.subtract, ALU.mult)
            link(ins)
            whole = lambda k: gb[:, k, :].rearrange("p (o e) -> p o e", o=1).broadcast_to([P, 4, D])
            link(nc.vector.tensor_tensor(yn[:], yn[:], whole(0), ALU.mult))
            link(nc.vector.tensor_tensor(yn[:], yn[:], whole(1), ALU.add))
            last = xv[:, SEGS - 1]
            link(nc.vector.tensor_tensor(last, last, pairs(yn), ALU.add))


def attention_experts(nc, own, a, m, ps, out):
    sb, sem = scoped(nc, own)
    e = {
        "mla": sb("d_mla", [P, B * T]),
        "wt": sb("e_wt", [P, 2, 4, D]),
        "b1": sb("e_b1", [P, 2 * E1]),
        "b2": sb("e_b2", [E1, D]),
        "rw": sb("e_rw", [P, E1]),
        "rb": sb("e_rb", [P, E1]),
        "ld_c": sem("e_ld_c"), "ld_w": [sem("e_ld_w0"), sem("e_ld_w1")],
    }
    with ExitStack() as inner:
        attention(nc, inner, a, m, ps, e)
    gelu_experts(nc, own, a, m, ps, e, out)


PARTS = 3
TERMS = ((0, 0), (0, 1), (1, 0), (1, 1), (0, 2), (2, 0))
MAX_ROW = len(TERMS) * KPH
GROUPS = B * NHG
UNITS = HG * TB
AHEAD = 8
PIECES = 4
PIECE = T // PIECES
NM = 1 + 2 * PARTS
TURN_AT = 6
MAX_AT = UNITS - 2
READ = 2 * PIECES


def selections():
    import numpy as np
    sel = np.zeros((2, H3, KPH, NHG, 2, PARTS, HG, 32), np.float32)
    for h in range(H3):
        for t, parts in enumerate(TERMS):
            for side in range(2):
                for k in range(KPH):
                    sel[side, h, k, h // HG, side, parts[side], h % HG, t * KPH + k] = 1
    return sel.reshape(P, NHG * 2 * PARTS * P)


def attention(nc, own, a, m, ps, e):
    sb, sem = scoped(nc, own)
    x, xn, xT, stats, small, ident = (m[k] for k in ("x", "xn", "xT", "stats", "small", "ident"))
    banks, mla = m["banks"], e["mla"]
    NORMED = seg_tiles(SEGS - 1)
    CHUNKS = (0, 2, 1, 3)
    assert not [i for i in NORMED if i // 4 in CHUNKS[:2]]
    wqk = sb("d_wqk", [P, P])
    wv = sb("d_wv", [P, LAT])
    wo = sb("d_wo", [LAT, D])
    col = sb("d_col", [P, 3 + HG])
    vb = sb("d_vb", [P, LAT])
    sel = sb("d_sel", [P, NHG, 2, PARTS, P], BF16)
    idb = sb("d_idb", [P, P], BF16)
    qk = sb("d_qk", [P, B * T])
    part = sb("d_part", [P, PARTS, B * T], BF16)
    vall = sb("d_vall", [P, GROUPS, TB, HG, KPH])
    vs = sb("d_vs", [P, 2, TB, HG, 32])
    rows = sb("d_rows", [P, 2, GROUPS, T], BF16)
    km = sb("d_km", [P, 2, HG, T], BF16)
    qh = sb("d_qh", [P, 2, HG, T], BF16)
    qm = sb("d_qm", [P, 2, T], BF16)
    mx = sb("d_mx", [P, 2, TB, HG])
    mtop = sb("d_mtop", [P, TB, HG])
    mrow = sb("d_mrow", [P, TB, HG, 32], BF16)
    NE = 2 * HG
    ex = sb("d_ex", [P, NE, T])
    ot = sb("d_ot", [P, T])
    rs = sb("d_rs", [P, TB, HG])
    ao = sb("d_ao", [P, NT, LAT])
    aoT = xT[0:LAT]
    ld_c, dve, xn_done, xT_ps, xT_done = (sem("d_" + n) for n in ("ldc", "dve", "xn", "xT_ps", "xT"))
    qk_ps, qk_done, split, v_ps, v_done, hs_in = (sem("d_" + n) for n in ("qk_ps", "qk", "split", "v_ps", "v", "hs"))
    split_b, rest_b = sem("d_split_b"), sem("d_rest_b")
    r_ps, r_out, km_done, qh_done, vs_done = (sem("d_" + n) for n in ("r_ps", "r_out", "km", "qh", "vs"))
    s_ps, s_max, qm_ps, qm_out = (sem("d_" + n) for n in ("s_ps", "smax", "qm_ps", "qm_out"))
    e_ps, e_done, pv, ot_done, ot_ps, ao_done = (sem("d_" + n) for n in ("e_ps", "e", "pv", "ot", "ot_ps", "ao"))
    aoT_ps, aoT_done, mla_ps, fin = (sem("d_" + n) for n in ("aoT_ps", "aoT", "mla_ps", "fin"))
    ready, mdve, rs_done = sem("d_ready"), sem("d_mdve"), sem("d_rs")
    aov = ao[:].rearrange("p (b s) (g c) -> p b g s c", b=B, g=NHG)

    SPREADS = [(n, side, h) for n in range(GROUPS) for side in (1, 0) for h in range(2)]

    def bank_of(i):
        return ps[2 + i % 6]

    def groups(engine, body):
        body(0, 0, False, 2)
        body(1, 1, FIRST, 2)
        with engine.Fori(1, GROUPS // 2 - 1) as f:
            for k in range(2):
                body(f * 2 + k, k, True, 2)
        body(GROUPS - 2, 0, True, 1)
        body(GROUPS - 1, 1, True, 0)

    with nc.Block() as block:
        @block.sync
        def _(sp):
            sp.dma_start(wqk[:], a["wqk"]).then_inc(ld_c, 16)
            sp.dma_start(wv[:], a["wv1"]).then_inc(ld_c, 16)
            sp.dma_start(wo[:], a["wo1"]).then_inc(ld_c, 16)
            sp.dma_start(col[:, 0:1], a["bqk"].rearrange("(p o) -> p o", o=1)).then_inc(ld_c, 16)
            sp.dma_start(col[:, 1:2], a["ob1"].rearrange("(p o) -> p o", o=1)).then_inc(ld_c, 16)
            sp.dma_start(col[:, 2:3 + HG], a["rows"]).then_inc(ld_c, 16)
            sp.dma_start(vb[:], a["vb1"].rearrange("(o e) -> o e", o=1).broadcast_to([P, LAT])).then_inc(ld_c, 16)
            sp.dma_start(sel[:].rearrange("p g s k c -> p (g s k c)"), a["sel"]).then_inc(ld_c, 16)
            sp.dma_start(idb[:], a["identb"]).then_inc(ld_c, 16)
            w = a["moe1"].rearrange("(f k) r c -> k f r c", k=2)
            for k in range(2):
                sp.dma_start(e["wt"][:, k].rearrange("p m c -> p (m c)"), w[k, 0]).then_inc(e["ld_w"][k], 16)
            for dst, src in ((e["rw"][:], a["router1"]), (e["b1"][:], a["b1T"]), (e["b2"][:], a["b2"]),
                             (e["rb"][:], a["rb1"].rearrange("(o e) -> o e", o=1).broadcast_to([P, E1]))):
                sp.dma_start(dst, src).then_inc(e["ld_c"], 16)

        LOADS = 16 * 9

        @block.scalar
        def _(act):
            def turned(q):
                c = CHUNKS[q]
                act.wait_ge(xT_ps, 4 * q + 4)
                nc.scalar.copy(xT[:, CH * c:CH * c + CH], ps[c][:]).then_inc(xT_done, 1)

            def q_and_k(q):
                c = CHUNKS[q]
                act.wait_ge(qk_ps, q + 1)
                nc.scalar.activation(qk[:, CH * c:CH * c + CH], ps[4 + c][:], ACT.Identity, bias=col[:, 0:1]).then_inc(qk_done, 1)

            turned(0)
            turned(1)
            act.wait_ge(ld_c, LOADS)
            q_and_k(0)
            q_and_k(1)
            for q in (2, 3):
                turned(q)
                q_and_k(q)
            nc.scalar.preload_act_table(ACT.Exp)
            for i, (n, side, h) in enumerate(SPREADS):
                act.wait_ge(r_ps, i + 1)
                dst = rows[:, side, n, CH * h:CH * h + CH]
                if side:
                    nc.scalar.activation(dst, bank_of(i)[:], ACT.Identity, bias=col[:, 2:3]).then_inc(r_out, 1)
                else:
                    nc.scalar.copy(dst, bank_of(i)[:]).then_inc(r_out, 1)

            def q_rows(n, k, h):
                act.wait_ge(qm_ps, n * 2 + (h + 1))
                nc.scalar.copy(qm[:, k, CH * h:CH * h + CH], ps[h][:]).then_inc(qm_out, 1)

            def take_outputs(n, h):
                act.wait_ge(pv, n * (TB * PIECES) + (READ + (TB - 1) * PIECES + 2 * (h + 1)))
                nc.scalar.copy(ot[:, CH * h:CH * h + CH], ps[6 + h][:]).then_inc(ot_done, 1)

            def group(n, k, before, after):
                for u in range(UNITS):
                    if after and u >= MAX_AT:
                        q_rows(n + 1, 1 - k, u - MAX_AT)
                    act.wait_ge(e_ps, n * UNITS + (u + 1))
                    if u % HG == 0:
                        act.wait_ge(pv, n * (TB * PIECES) + ((u // HG - 2) * PIECES + PIECES + READ))
                    nc.scalar.activation(ex[:, u % NE, :], banks[:, 2 + 2 * (u % 2):4 + 2 * (u % 2), :].rearrange("p k c -> p (k c)"),
                                         ACT.Exp, scale=0.5).then_inc(e_done, 1)
                    if before and u in (2, 3):
                        if before is not FIRST:
                            act.wait_ge(ot_ps, n * 2 + (u - 5))
                        take_outputs(n - 1, u - 2)

            for h in range(2):
                q_rows(0, 0, h)
            groups(nc.scalar, group)
            for h in range(2):
                take_outputs(GROUPS - 1, h)
            for c in range(NC):
                act.wait_ge(aoT_ps, 4 * c + 4)
                nc.scalar.copy(aoT[:, CH * c:CH * c + CH], ps[c][0:LAT, :]).then_inc(aoT_done, 1)
            for c in range(NC):
                act.wait_ge(mla_ps, c + 1)
                nc.scalar.activation(mla[:, CH * c:CH * c + CH], ps[4 + c][:], ACT.Identity, bias=col[:, 1:2]).then_inc(fin, 1)

        @block.gpsimd
        def _(pool):
            nc.gpsimd.memset(vs[:], 1.0).then_inc(vs_done, 1)
            nc.gpsimd.memset(mrow[:].rearrange("p s h c -> p (s h c)"), 0.0).then_inc(ready, 1)
            pool.wait_ge(xn_done, len(NORMED))
            lastv = lambda t: t[:].rearrange("p (b c q) d -> p c b q d", b=B, q=SEG // P)[:, SEGS - 1]
            nc.gpsimd.tensor_tensor(lastv(x), lastv(x), lastv(xn), ALU.add).then_inc(hs_in, 1)

            def one_head_rows(dst, side, n, done):
                for hh in range(HG):
                    src = rows[:, side, bass.ds(n, 1), :].rearrange("p o t -> p (o t)")
                    nc.gpsimd.tensor_tensor(dst[:, hh, :], src, col[:, 3 + hh:4 + hh].broadcast_to([P, T]), ALU.mult).then_inc(done, 1)

            def values_of(n, k):
                src = vall[:, bass.ds(n, 1)].rearrange("p o s h k -> p (o s) h k")
                nc.gpsimd.tensor_copy(vs[:, k, :, :, 0:KPH], src).then_inc(vs_done, 1)

            for c in range(NC // B, NC):
                pool.wait_ge(qk_done, CHUNKS.index(c) + 1)
                at = slice(CH * c, CH * c + CH)
                for k in range(PARTS):
                    nc.gpsimd.tensor_copy(part[:, k, at], qk[:, at]).then_inc(split_b, 1)
                    if k < PARTS - 1:
                        pool.wait_ge(split_b, PARTS * (c - NC // B) + k + 1)
                        nc.gpsimd.tensor_tensor(qk[:, at], qk[:, at], part[:, k, at], ALU.subtract).then_inc(rest_b, 1)
                        pool.wait_ge(rest_b, (PARTS - 1) * (c - NC // B) + k + 1)
            pool.wait_ge(ld_c, LOADS)
            pool.wait_ge(r_out, 4)
            one_head_rows(km[:, 0], 1, 0, km_done)
            pool.wait_ge(r_out, 8)
            one_head_rows(qh[:, 1], 0, 1, qh_done)
            pool.wait_ge(v_done, B)
            pool.wait_ge(vs_done, 1)
            values_of(0, 0)

            def group(n, k, more):
                if more:
                    pool.wait_ge(s_ps, n * (2 * UNITS) + 2 * UNITS)
                    one_head_rows(qh[:, k], 0, n + 2, qh_done)
                pool.wait_ge(e_ps, n * UNITS + 1)
                one_head_rows(km[:, 1 - k], 1, n + 1, km_done)
                pool.wait_ge(pv, n * (TB * PIECES) + (READ + 1))
                values_of(n + 1, 1 - k)

            pool.wait_ge(r_out, len(SPREADS))
            with nc.gpsimd.Fori(0, GROUPS // 2 - 1) as f:
                for k in range(2):
                    group(f * 2 + k, k, True)
            group(GROUPS - 2, 0, False)

        @block.tensor
        def _(pe):
            def turn(q):
                c = CHUNKS[q]
                for i in range(4 * c, 4 * c + 4):
                    if i in NORMED:
                        pe.wait_ge(xn_done, NORMED.index(i) + 1)
                    nc.tensor.transpose(ps[c][:, P * (i % 4):P * (i % 4) + P], xn[:, i, :], ident[:]).then_inc(xT_ps, 1)

            def q_and_k(q):
                c = CHUNKS[q]
                pe.wait_ge(xT_done, q + 1)
                nc.tensor.matmul(ps[4 + c][:], wqk[:], xT[:, CH * c:CH * c + CH], start=True, stop=True).then_inc(qk_ps, 1)

            turn(0)
            turn(1)
            pe.wait_ge(ld_c, LOADS)
            q_and_k(0)
            q_and_k(1)
            for q in (2, 3):
                turn(q)
                q_and_k(q)
            for i in range(NT):
                nc.tensor.matmul(ps[i // 8][:, LAT * (i % 8):LAT * (i % 8) + LAT], xT[:, P * i:P * i + P], wv[:],
                                 start=True, stop=True).then_inc(v_ps, 1)
            pe.wait_ge(qk_done, NC)

            def spread(i):
                n, side, h = SPREADS[i]
                c = (n // NHG) * T + CH * h
                if i >= 6:
                    pe.wait_ge(r_out, i - 5)
                if SPREADS[i - 1][0] == NHG - 1 and n == NHG:
                    pe.wait_ge(split_b, PARTS * NC // B)
                for k in range(PARTS):
                    if i < 4:
                        pe.wait_ge(split, PARTS * (c // CH) + k + 1)
                    mm = nc.tensor.matmul(bank_of(i)[:], sel[:, n % NHG, side, k, :], part[:, k, c:c + CH],
                                          start=(k == 0), stop=(k == PARTS - 1))
                mm.then_inc(r_ps, 1)

            def scores(n, k, u, h, seen=None):
                if seen is None and n is not FIRST:
                    seen = n * (2 * UNITS) + (2 * u + h - 1)
                if seen is not None:
                    pe.wait_ge(s_max, seen)
                nc.tensor.matmul(ps[h][:], qh[:, k, u % HG, P * (u // HG):P * (u // HG) + P],
                                 rows[:, 1, bass.ds(0 if n is FIRST else n, 1), CH * h:CH * h + CH].rearrange("p o t -> p (o t)"),
                                 start=True, stop=True).then_inc(s_ps, 1)

            def scores_beside(n, k, u, after, h, seen=None):
                if u + AHEAD < UNITS:
                    if after >= 1:
                        scores(n + 1, 1 - k, u + AHEAD, h, seen)
                elif after >= 2:
                    if u + AHEAD == UNITS and h == 0:
                        pe.wait_ge(qh_done, n * HG + 3 * HG)
                    scores(n + 2, k, u + AHEAD - UNITS, h, seen)

            def q_and_max(n, h, seen):
                pe.wait_ge(mdve, n * NM + NM)
                pe.wait_ge(s_max, seen)
                nc.tensor.matmul(ps[h][:], idb[:], rows[:, 0, bass.ds(n, 1), CH * h:CH * h + CH].rearrange("p o t -> p (o t)"),
                                 start=True, stop=False, skip_group_check=True)
                for i in range(4):
                    mm = nc.tensor.matmul(ps[h][:, P * i:P * i + P], mrow[:, 4 * h + i].rearrange("p h c -> p (h c)"), idb[:],
                                          start=False, stop=True, skip_group_check=True)
                mm.then_inc(qm_ps, 1)

            def weights(n, k, u, before):
                tt, hh = u // HG, u % HG
                if u >= 2 or before:
                    pe.wait_ge(e_done, n * UNITS + (u - 1))
                for h in range(2):
                    mm = nc.tensor.matmul(ps[2 + 2 * (u % 2) + h][:], km[:, k, hh, P * tt:P * tt + P],
                                          qm[:, k, CH * h:CH * h + CH], start=True, stop=True)
                mm.then_inc(e_ps, 1)

            def values(n, k, v):
                tt, piece = v // PIECES, v % PIECES
                if piece == 0:
                    pe.wait_ge(e_done, n * UNITS + HG * (tt + 1))
                c = PIECE * piece
                for hh in range(HG):
                    mm = nc.tensor.matmul(ps[6 + c // CH][32 * hh:32 * hh + 32, c % CH:c % CH + PIECE], vs[:, k, tt, hh, :],
                                          ex[:, (HG * tt + hh) % NE, c:c + PIECE],
                                          start=(tt == 0 and c % CH == 0), stop=(tt == TB - 1),
                                          tile_position=(0, 32 * hh), skip_group_check=True)
                mm.then_inc(pv, 1)

            def values_beside(n, k, u, before):
                if u < PIECES:
                    if before:
                        values(n - 1, 1 - k, UNITS - PIECES + u)
                    return
                if u == PIECES:
                    pe.wait_ge(vs_done, n + 2)
                if before and u in (PIECES, PIECES + 2):
                    pe.wait_ge(ot_done, n * 2 - 1 + (u - PIECES) // 2)
                values(n, k, u - PIECES)

            def turn_outputs(n, h, seen):
                pe.wait_ge(ot_done, n * 2 + (h + 1))
                pe.wait_ge(s_max, seen)
                for i in range(TB // 2):
                    mm = nc.tensor.transpose(ps[h][:, P * i:P * i + P], ot[:, CH * h + P * i:CH * h + P * i + P], ident[:])
                mm.then_inc(ot_ps, 1)

            def group(n, k, before, after):
                for u in range(UNITS):
                    if u == 0:
                        pe.wait_ge(qm_out, n * 2 + 2)
                        pe.wait_ge(km_done, n * HG + HG)
                    turns = before and TURN_AT <= u < TURN_AT + 2
                    if not turns and not (after and u >= MAX_AT):
                        scores_beside(n, k, u, after, 0)
                        weights(n, k, u, before)
                        scores_beside(n, k, u, after, 1)
                        values_beside(n, k, u, before)
                        continue
                    at = u - (TURN_AT if turns else MAX_AT)
                    if after == 2 or (after and u + AHEAD < UNITS):
                        seen = n * (2 * UNITS) + (2 * UNITS + 2 * (u + AHEAD))
                    else:
                        seen = GROUPS * 2 * UNITS
                    if at == 0:
                        scores_beside(n, k, u, after, 1, seen)
                    if turns:
                        turn_outputs(n - 1, at, seen if at == 0 else seen - 1)
                    else:
                        q_and_max(n + 1, at, seen if at == 0 else seen - 1)
                    weights(n, k, u, before)
                    if at == 1:
                        scores_beside(n, k, u, after, 0, seen)
                    values_beside(n, k, u, before)
                    if turns:
                        pe.wait_ge(ao_done, n * 2 + (at - 1))
                    else:
                        pe.wait_ge(qm_out, n * 2 + (3 + at))
                    scores_beside(n, k, u, after, at, seen)

            for i in range(4):
                spread(i)
            pe.wait_ge(qh_done, HG)
            pe.wait_ge(v_done, B)
            done = 4
            for u in range(UNITS):
                for h in range(2):
                    scores(FIRST if u == 0 else 0, 0, u, h)
                while done < len(SPREADS) and done < 4 + (u + 1):
                    spread(done)
                    done += 1
            pe.wait_ge(qh_done, 2 * HG)
            pe.wait_ge(ready, 1)
            for u in range(AHEAD):
                for h in range(2):
                    scores(1, 1, u, h)
            for h in range(2):
                q_and_max(0, h, 2 * (UNITS + AHEAD))
            pe.wait_ge(r_out, len(SPREADS))
            groups(nc.tensor, group)
            for v in range(UNITS - PIECES, UNITS):
                values(GROUPS - 1, 1, v)
            for h in range(2):
                turn_outputs(GROUPS - 1, h, GROUPS * 2 * UNITS)
            pe.wait_ge(ao_done, GROUPS * 2)
            for i in range(NT):
                nc.tensor.transpose(ps[i // 4][0:LAT, P * (i % 4):P * (i % 4) + P], ao[:, i, :], ident[:]).then_inc(aoT_ps, 1)
            for c in range(NC):
                pe.wait_ge(aoT_done, c + 1)
                nc.tensor.matmul(ps[4 + c][:], wo[:], aoT[:, CH * c:CH * c + CH], start=True, stop=True).then_inc(mla_ps, 1)

        @block.vector
        def _(ve):
            link = Chain(ve, dve)
            nc.vector.memset(rs[:], 0.0).then_inc(pv, READ)
            for q, i in enumerate(NORMED):
                ins = nc.vector.bn_stats(stats[:, q, :], x[:, i, :])
            link(ins)
            ln_moments(nc, link, stats[:, 0:len(NORMED)], small[:, :, 0:len(NORMED)])
            for q, i in enumerate(NORMED):
                nc.vector.tensor_scalar(xn[:, i, :], x[:, i, :], small[:, 0, q:q + 1], small[:, 1, q:q + 1],
                                        ALU.subtract, ALU.mult).then_inc(xn_done, 1)
            for c in range(NC // B):
                ve.wait_ge(qk_done, CHUNKS.index(c) + 1)
                at = slice(CH * c, CH * c + CH)
                for k in range(PARTS):
                    nc.vector.tensor_copy(part[:, k, at], qk[:, at]).then_inc(split, 1)
                    if k < PARTS - 1:
                        ve.wait_ge(split, PARTS * c + k + 1)
                        link(nc.vector.tensor_tensor(qk[:, at], qk[:, at], part[:, k, at], ALU.subtract))
                if c == 1:
                    ve.wait_ge(ld_c, LOADS)
                    for b in range(B):
                        ve.wait_ge(v_ps, NT)
                        nc.vector.tensor_tensor(vall[:, NHG * b:NHG * b + NHG].rearrange("p g s h k -> p s g (h k)"),
                                                ps[b][:].rearrange("p (s g e) -> p s g e", s=TB, g=NHG),
                                                vb[:].rearrange("p (o g e) -> p o g e", o=1, g=NHG).broadcast_to([P, TB, NHG, HG * KPH]),
                                                ALU.add).then_inc(v_done, 1)
                    ve.wait_ge(r_out, 4)
                    for hh in range(HG):
                        nc.vector.tensor_scalar(qh[:, 0, hh, :], rows[:, 0, 0, :], col[:, 3 + hh:4 + hh], None,
                                                ALU.mult).then_inc(qh_done, 1)

            def maximum(n, u, h, place):
                ve.wait_ge(s_ps, n * (2 * UNITS) + (2 * u + place + 1))
                nc.vector.tensor_reduce(mx[:, h, u // HG, u % HG:u % HG + 1], ps[h][:], AX, ALU.max).then_inc(s_max, 1)

            def maximum_beside(n, u, after, h, place):
                if u + AHEAD < UNITS:
                    if after >= 1:
                        maximum(n + 1, u + AHEAD, h, place)
                elif after >= 2:
                    maximum(n + 2, u + AHEAD - UNITS, h, place)

            def maxima_to_rows(n, step):
                part_of = lambda p: mrow[:, :, :, MAX_ROW + p]
                if step == 0:
                    ve.wait_ge(s_max, n * (2 * UNITS) + 2 * UNITS)
                    ins = nc.vector.tensor_tensor(mtop[:], mx[:, 0], mx[:, 1], ALU.max)
                else:
                    ve.wait_ge(mdve, n * NM + step)
                    if step == 1:
                        ins = nc.vector.tensor_scalar(mtop[:], mtop[:], -1.0, None, ALU.mult)
                    elif step % 2 == 0:
                        ins = nc.vector.tensor_copy(part_of(step // 2 - 1), mtop[:])
                    else:
                        ins = nc.vector.tensor_tensor(mtop[:], mtop[:], part_of(step // 2 - 1), ALU.subtract)
                ins.then_inc(mdve, 1)
                if step == 0:
                    ve.wait_ge(mdve, n * NM + 1)

            def outputs(n, h):
                ve.wait_ge(ot_ps, n * 2 + (h + 1))
                o = ps[h][:].rearrange("p (s q c) -> p s q c", s=4, q=HG)
                r = rs[:, 4 * h:4 * h + 4, :]
                nc.vector.reciprocal(r, o[:, :, :, KPH]).then_inc(rs_done, 1)
                ve.wait_ge(rs_done, n * 2 + (h + 1))
                dst = aov[:, bass.ds(n // NHG, 1), bass.ds(n % NHG, 1), 4 * h:4 * h + 4, :]
                nc.vector.tensor_tensor(dst.rearrange("p a c s (q k) -> p (a c s) q k", q=HG), o[:, :, :, 0:KPH],
                                        r.rearrange("p s (q o) -> p s q o", o=1).broadcast_to([P, 4, HG, KPH]),
                                        ALU.mult).then_inc(ao_done, 1)

            def group(n, k, before, after):
                for u in range(UNITS):
                    if after and 0 <= u + AHEAD - UNITS < NM:
                        maxima_to_rows(n + 1, u + AHEAD - UNITS)
                    swapped = (before and u == TURN_AT) or (after and u == MAX_AT)
                    for place, h in enumerate((1, 0) if swapped else (0, 1)):
                        if before and place == 1 and TURN_AT <= u < TURN_AT + 2:
                            outputs(n - 1, u - TURN_AT)
                        maximum_beside(n, u, after, h, place)

            ve.wait_ge(ready, 1)
            for u in range(UNITS):
                for h in range(2):
                    maximum(0, u, h, h)
            for step in range(NM):
                maxima_to_rows(0, step)
            for u in range(AHEAD):
                for h in range(2):
                    maximum(1, u, h, h)
            groups(nc.vector, group)
            for h in range(2):
                outputs(GROUPS - 1, h)


def gelu_experts(nc, own, a, m, ps, e, out):
    sb, sem = scoped(nc, own)
    x, ident = m["x"], m["ident"]
    mla, wt, b1, b2, rw, rb = (e[k] for k in ("mla", "wt", "b1", "b2", "rw", "rb"))
    ld_c, ld_w = e["ld_c"], e["ld_w"]
    b1e = sb("e_b1e", [P, 2, 2])
    rank = sb("e_rank", [P, NT, E1 * E1])
    rk = sb("e_rk", [P, NT, E1])
    pr = sb("e_pr", [P, NT, E1])
    tot = sb("e_tot", [P, NT])
    combT = sb("e_combT", [E1, B * T])
    act_ = sb("e_act", [P, 2, 2, CH])
    b_cur, stored = sem("e_b_cur"), sem("stored")
    dve, logit, arg, ex_done, comb_done = (sem("e_" + n) for n in ("dve", "logit", "arg", "ex", "comb"))
    cT_ps, cT_done, b_ps, b_in, h_ps, act_done, y_ps, acc_done = (
        sem("e_" + n) for n in ("cT_ps", "cT", "b_ps", "b_in", "h", "act", "y", "acc"))

    with nc.Block() as block:
        @block.sync
        def _(sp):
            w = a["moe1"].rearrange("(f k) r c -> k f r c", k=2)
            with nc.sync.Fori(1, E1 // 2) as f:
                for k in range(2):
                    sp.wait_ge(y_ps, f * (2 * NC) + ((k - 1) * NC + 2))
                    sp.dma_start(wt[:, k].rearrange("p m c -> p (m c)"),
                                 w[k, bass.ds(f, 1)].rearrange("o r c -> r (o c)")).then_inc(ld_w[k], 16)
            o = out.rearrange("b (i p) d -> p (b i) d", p=P)
            for c in range(NC):
                sp.wait_ge(b_in, c + 1)
                sp.dma_start(o[:, 4 * c:4 * c + 4, :], x[:, 4 * c:4 * c + 4, :]).then_inc(stored, 16)
            sp.wait_ge(stored, 16 * NC)

        @block.scalar
        def _(act):
            act.wait_ge(arg, 1)
            nc.scalar.activation(pr[:].rearrange("p i e -> p (i e)"), pr[:].rearrange("p i e -> p (i e)"),
                                 ACT.Exp).then_inc(ex_done, 1)
            nc.scalar.preload_act_table(ACT.Gelu)

            def weights_out(c):
                act.wait_ge(cT_ps, c + 1)
                nc.scalar.copy(combT[:, CH * c:CH * c + CH], ps[6 + c % 2][0:E1, :]).then_inc(cT_done, 1)

            def expert(n, k, turned=None):
                nc.scalar.copy(b1e[:, k], b1[:, bass.ds(n * 2, 2)]).then_inc(b_cur, 1)
                act.wait_ge(b_cur, n + 1)
                for c in range(NC):
                    act.wait_ge(y_ps, n * NC + (c + 1))
                    for h in range(2):
                        act.wait_ge(h_ps, n * (2 * NC) + (2 * c + h + 1))
                        nc.scalar.activation(act_[:, c % 2, h, :], ps[2 * (c % 2) + h][:], ACT.Gelu,
                                             bias=b1e[:, k, h:h + 1]).then_inc(act_done, 1)
                    if turned and c in turned:
                        weights_out(turned[c])

            with nc.scalar.Fori(0, E1 // 2 - 1) as f:
                for k in range(2):
                    expert(f * 2 + k, k)
            expert(E1 - 2, 0, {c: c - 1 for c in range(1, NC)})
            expert(E1 - 1, 1, {0: NC - 1})

        @block.tensor
        def _(pe):
            pe.wait_ge(ld_c, 64)
            for i in range(NT):
                mm = nc.tensor.matmul(ps[6][:, E1 * i:E1 * i + E1], mla[:, P * i:P * i + P], rw[:], start=True, stop=True)
            mm.then_inc(logit, 1)

            def up(n, k, c):
                if not (n is FIRST and c < 2):
                    pe.wait_ge(act_done, (0 if n is FIRST else n) * (2 * NC) + 2 * (c - 1))
                for h in range(2):
                    nc.tensor.matmul(ps[2 * (c % 2) + h][:], wt[:, k, h, :], mla[:, CH * c:CH * c + CH],
                                     start=True, stop=True).then_inc(h_ps, 1)

            def down(n, k, c):
                pe.wait_ge(act_done, n * (2 * NC) + (2 * c + 2))
                pe.wait_ge(acc_done, n * NC + (c + 1))
                for i in range(4):
                    for h in range(2):
                        mm = nc.tensor.matmul(ps[4 + c % 2][:, P * i:P * i + P], act_[:, c % 2, h, P * i:P * i + P],
                                              wt[:, k, 2 + h, :], start=(h == 0), stop=(h == 1))
                mm.then_inc(y_ps, 1)

            def turn_weights(c):
                if c >= 2:
                    pe.wait_ge(cT_done, c - 1)
                for i in range(4):
                    mm = nc.tensor.transpose(ps[6 + c % 2][0:E1, P * i:P * i + P], pr[:, 4 * c + i, :], ident[:])
                mm.then_inc(cT_ps, 1)

            def b2_product(c):
                pe.wait_ge(cT_done, min(c + 3, NC))
                if c >= 2:
                    pe.wait_ge(b_in, c - 1)
                for i in range(4):
                    at = CH * c + P * i
                    mm = nc.tensor.matmul(ps[6 + c % 2][:, P * i:P * i + P], combT[:, at:at + P], b2[:], start=True, stop=True)
                mm.then_inc(b_ps, 1)

            def expert(n, k, after, beside=None):
                down(n, k, 0)
                for c in range(1, NC + 1):
                    if c + 1 < NC:
                        up(n, k, c + 1)
                    elif after is not None:
                        if c + 1 == NC:
                            pe.wait_ge(ld_w[1 - k], after)
                        up(n + 1, 1 - k, c + 1 - NC)
                    if beside:
                        beside(c - 1)
                    if c < NC:
                        down(n, k, c)

            pe.wait_ge(ld_w[0], 16)
            up(FIRST, 0, 0)
            up(FIRST, 0, 1)
            with nc.tensor.Fori(0, E1 // 2 - 1) as f:
                expert(f * 2, 0, f * 16 + 16)
                expert(f * 2 + 1, 1, f * 16 + 32)
            pe.wait_ge(comb_done, 1)
            expert(E1 - 2, 0, 16 * (E1 // 2), turn_weights)
            expert(E1 - 1, 1, None, b2_product)

        @block.vector
        def _(ve):
            link = Chain(ve, dve)
            flat = lambda t: t.rearrange("p i e -> p (i e)")
            nc.vector.memset(rk[:], 0.0).then_inc(y_ps, 2)
            nc.vector.memset(tot[:], 0.0).then_inc(acc_done, 2)
            wide = lambda t, n: t.rearrange("p (i o) -> p i o", o=1).broadcast_to([P, NT, n])
            ve.wait_ge(ld_c, 64)
            ve.wait_ge(logit, 1)
            link(nc.vector.tensor_tensor(pr[:], ps[6][:, 0:NT * E1].rearrange("p (i e) -> p i e", e=E1),
                                         rb[:].rearrange("p (o e) -> p o e", o=1).broadcast_to([P, NT, E1]), ALU.add))
            link(nc.vector.tensor_reduce(tot[:], pr[:], AX, ALU.max))
            nc.vector.tensor_tensor(pr[:], pr[:], wide(tot[:], E1), ALU.subtract).then_inc(arg, 1)
            ve.wait_ge(ex_done, 1)
            link(nc.vector.tensor_reduce(tot[:], pr[:], AX, ALU.add))
            link(nc.vector.reciprocal(tot[:], tot[:]))
            link(nc.vector.tensor_tensor(pr[:], pr[:], wide(tot[:], E1), ALU.mult))
            ranks(nc, link, rk[:], pr[:], rank, E1)
            link(nc.vector.tensor_scalar(flat(rk[:]), flat(rk[:]), float(TOPK), None, ALU.is_lt))
            link(nc.vector.tensor_tensor(pr[:], pr[:], rk[:], ALU.mult))
            link(nc.vector.tensor_reduce(tot[:], pr[:], AX, ALU.add))
            link(nc.vector.tensor_scalar(tot[:], tot[:], 1e-8, None, ALU.add))
            link(nc.vector.reciprocal(tot[:], tot[:]))
            link(nc.vector.tensor_scalar(tot[:], tot[:], 0.3, None, ALU.mult))
            nc.vector.tensor_tensor(pr[:], pr[:], wide(tot[:], E1), ALU.mult).then_inc(comb_done, 1)
            ve.wait_ge(comb_done, 1)

            def expert(n, last=False):
                for c in range(NC):
                    ve.wait_ge(y_ps, n * NC + (c + 3))
                    for i in range(4 * c, 4 * c + 4):
                        ins = nc.vector.scalar_tensor_tensor(out=x[:, i, :], in0=ps[4 + c % 2][:, P * (i % 4):P * (i % 4) + P],
                                                             scalar=pr[:, i, bass.ds(n, 1)], in1=x[:, i, :],
                                                             op0=ALU.mult, op1=ALU.add)
                    ins.then_inc(acc_done, 1)
                    if last:
                        ve.wait_ge(b_ps, c + 1)
                        ve.wait_ge(acc_done, NC * E1 - NC + c + 3)
                        xs = x[:, 4 * c:4 * c + 4, :].rearrange("p i d -> p (i d)")
                        nc.vector.tensor_tensor(xs, xs, ps[6 + c % 2][:], ALU.add).then_inc(b_in, 1)

            with nc.vector.Fori(0, E1 - 1) as n:
                expert(n)
            expert(E1 - 1, last=True)


def kernel(**inputs):
    import numpy as np
    import concourse.bacc as bacc
    from concourse import mybir as mb
    from concourse.bass_utils import run_bass_kernel_spmd

    i = {k: np.asarray(v) for k, v in inputs.items()}
    arrays = {
        "x": i["L0_attn_x"],
        "WqT": i["L0_attn_Wq"].T, "WkT": i["L0_attn_Wk"].T, "WvT": i["L0_attn_Wv"].T, "WoT": i["L0_attn_Wo"].T,
        "W_gamma": i["L0_attn_W_gamma"], "b_gamma": i["L0_attn_b_gamma"],
        "W_lambda": i["L0_attn_W_lambda"], "b_lambda": i["L0_attn_b_lambda"],
        "ident": np.eye(128, dtype=np.float32),
        "AT": i["L1_attn_A"].T, "BT": i["L1_attn_B"].T, "CT": i["L1_attn_C"].T,
        "gamma": i["L1_attn_gamma"], "beta": i["L1_attn_beta"],
        "wqk": np.concatenate([i["L1_ffn_q_w"].reshape(128, 16, 8)[:, :, :4].reshape(128, 64), i["L1_ffn_k_w"]], axis=1),
        "bqk": np.concatenate([i["L1_ffn_q_b"].reshape(16, 8)[:, :4].reshape(64), i["L1_ffn_k_b"]]),
        "wv1": i["L1_ffn_v_w"], "vb1": i["L1_ffn_v_b"], "wo1": i["L1_ffn_o_w"][:LAT], "ob1": i["L1_ffn_o_b"],
        "sel": selections().astype(mb.dt.np(mb.dt.bfloat16)), "identb": np.eye(128).astype(mb.dt.np(mb.dt.bfloat16)),
        "rows": np.stack([np.tile(np.isin(np.arange(32), MAX_ROW + np.arange(PARTS)), HG)]
                         + [np.arange(P) // 32 == h for h in range(HG)], axis=1).astype(np.float32),
        "moe1": np.concatenate([i["L1_ffn_w1"], i["L1_ffn_w2"].reshape(8, 2, 128, 128).transpose(0, 2, 1, 3).reshape(8, 128, 256)], axis=2),
        "b1T": i["L1_ffn_b1"].reshape(16, 128).T, "b2": i["L1_ffn_b2"],
        "router1": i["L1_ffn_router_w"], "rb1": i["L1_ffn_router_b"],
        "router0": i["L0_ffn_router_w"].T, "bias0": i["L0_ffn_bias"],
        "moe0": np.concatenate([
            np.concatenate([i["L0_ffn_gate_w"], i["L0_ffn_sh_gate_w"].reshape(128, 2, 128).transpose(1, 0, 2)]),
            np.concatenate([i["L0_ffn_up_w"], i["L0_ffn_sh_up_w"].reshape(128, 2, 128).transpose(1, 0, 2)]),
            np.concatenate([i["L0_ffn_down_w"], i["L0_ffn_sh_down_w"].reshape(2, 128, 128)])], axis=2),
    }
    arrays = {k: np.ascontiguousarray(v) for k, v in arrays.items()}
    nc = bacc.Bacc("TRN2", target_bir_lowering=False, num_devices=1)
    a = {k: nc.dram_tensor(f"in_{k}", v.shape, mb.dt.from_np(v.dtype), kind="ExternalInput").ap()
         for k, v in arrays.items()}
    out = nc.dram_tensor("out_0_dram", (2, 1024, 128), mb.dt.float32, kind="ExternalOutput").ap()
    build(nc, a, out)
    r = run_bass_kernel_spmd(nc, [{f"in_{k}": v for k, v in arrays.items()}], core_ids=[0])
    return r.results[0]["out_0_dram"]
```
